# Optimizing a Trainium2 kernel written in Bass

```python
import numpy as np
import jax
import jax.numpy as jnp

def _softmax(x, axis=-1):
    return jax.nn.softmax(x, axis=axis)

def _gelu(x):
    return jax.nn.gelu(x, approximate=True)

def _silu(x):
    return jax.nn.silu(x)

def _sigmoid(x):
    return jax.nn.sigmoid(x)

def _layernorm(x, axis=-1, eps=1e-05):
    m = jnp.mean(x, axis=axis, keepdims=True)
    v = jnp.var(x, axis=axis, keepdims=True)
    return (x - m) / jnp.sqrt(v + eps)

def _scatter_add(tgt, idx, src, axis=0):
    return tgt.at[idx].add(src)

def _segment_sum(src, seg, n):
    return jax.ops.segment_sum(src, seg, n)
kernel_name = 'mk_vit_tower_d2_tok_img256_r4_7b4a01'

def setup_inputs(seed: int=0):
    np.random.seed(seed)
    _w = jnp.asarray

    def _rec_inputs():
        import jax
        import jax.numpy as jnp
        _rk = jax.random.key(seed)
        x = -0.00016672 + 0.999947 * jax.random.normal(jax.random.fold_in(_rk, 1), (64, 3, 224, 224), jnp.float32)
        return x
    x = _rec_inputs()

    def _L0_tok_setup():
        import jax, jax.numpy as jnp
        import numpy as np
        PATCH = 16
        key = jax.random.key(seed)
        k1, k2, k3 = jax.random.split(key, 3)
        B, C, H, Wd = (64, 3, 96, 96)
        E = 64
        pdim = PATCH * PATCH * C
        x = jax.random.normal(k1, (B, C, H, Wd), dtype=jnp.float32)
        W = jax.random.normal(k2, (E, pdim), dtype=jnp.float32) * pdim ** (-0.5)
        b = jax.random.normal(k3, (E,), dtype=jnp.float32) * 0.01
        return {'x': x, 'W': W, 'b': b}
    _L0_tok_all = _L0_tok_setup()
    _L0_tok_in = {k: v for k, v in _L0_tok_all.items() if k in ('W', 'b')}
    del _L0_tok_all

    def _L0_attn_setup():
        import jax, jax.numpy as jnp
        import numpy as np
        N_EMBD = 64
        N_HEAD = 8
        BATCH = 4
        SEQ = 512
        NEG_BIAS = -1000000000.0
        key = jax.random.key(seed)
        ks = jax.random.split(key, 5)
        scale = 1.0 / np.sqrt(N_EMBD)
        x = jax.random.normal(ks[0], (BATCH, SEQ, N_EMBD), dtype=jnp.float32)
        Wq = jax.random.normal(ks[1], (N_EMBD * N_HEAD, N_EMBD), dtype=jnp.float32) * scale
        Wk = jax.random.normal(ks[2], (N_EMBD * N_HEAD, N_EMBD), dtype=jnp.float32) * scale
        Wv = jax.random.normal(ks[3], (N_EMBD * N_HEAD, N_EMBD), dtype=jnp.float32) * scale
        Wo = jax.random.normal(ks[4], (N_EMBD, N_EMBD * N_HEAD), dtype=jnp.float32) * scale / np.sqrt(N_HEAD)
        return {'x': x, 'Wq': Wq, 'Wk': Wk, 'Wv': Wv, 'Wo': Wo}
    _L0_attn_all = _L0_attn_setup()
    _L0_attn_in = {k: v for k, v in _L0_attn_all.items() if k in ('Wq', 'Wk', 'Wv', 'Wo')}
    del _L0_attn_all

    def _L0_ffn_setup():
        import jax, jax.numpy as jnp
        import numpy as np
        D_MODEL = 64
        EXPERT_DIM = 128
        NUM_EXPERTS = 8
        TOP_K = 2
        SEQ_LEN = 512
        BATCH = 2
        key = jax.random.key(seed)
        ks = jax.random.split(key, 8)
        s = 0.02
        x = jax.random.normal(ks[0], (SEQ_LEN, BATCH, D_MODEL), dtype=jnp.float32)
        Wg = jax.random.normal(ks[1], (D_MODEL, NUM_EXPERTS), dtype=jnp.float32) * s
        bg = jax.random.normal(ks[2], (NUM_EXPERTS,), dtype=jnp.float32) * s
        bias = jnp.zeros((NUM_EXPERTS,), dtype=jnp.float32)
        W1 = jax.random.normal(ks[3], (NUM_EXPERTS, D_MODEL, EXPERT_DIM), dtype=jnp.float32) * s
        b1 = jax.random.normal(ks[4], (NUM_EXPERTS, EXPERT_DIM), dtype=jnp.float32) * s
        W2 = jax.random.normal(ks[5], (NUM_EXPERTS, EXPERT_DIM, D_MODEL), dtype=jnp.float32) * s
        b2 = jax.random.normal(ks[6], (NUM_EXPERTS, D_MODEL), dtype=jnp.float32) * s
        return {'x': x, 'Wg': Wg, 'bg': bg, 'bias': bias, 'W1': W1, 'b1': b1, 'W2': W2, 'b2': b2}
    _L0_ffn_all = _L0_ffn_setup()
    _L0_ffn_in = {k: v for k, v in _L0_ffn_all.items() if k in ('Wg', 'bg', 'bias', 'W1', 'b1', 'W2', 'b2')}
    del _L0_ffn_all

    def _L1_attn_setup():
        import jax, jax.numpy as jnp
        import numpy as np
        key = jax.random.key(seed)
        k1, k2 = jax.random.split(key)
        B, N, D = (4, 1024, 64)
        inp = jax.random.normal(k1, (B, N, D), dtype=jnp.float32)
        q_weight = jax.random.normal(k2, (D, D), dtype=jnp.float32)
        return {'input': inp, 'q_weight': q_weight}
    _L1_attn_all = _L1_attn_setup()
    _L1_attn_in = {k: v for k, v in _L1_attn_all.items() if k in ('q_weight',)}
    del _L1_attn_all

    def _L1_ffn_setup():
        import jax, jax.numpy as jnp
        import numpy as np
        D_IN, D_HID, D_OUT = (64, 128, 64)
        N_EXPERTS, TOP_K = (64, 2)
        B, S = (8, 1024)
        key = jax.random.key(seed)
        ks = jax.random.split(key, 8)
        scale_in = 1.0 / np.sqrt(D_IN)
        scale_hid = 1.0 / np.sqrt(D_HID)
        return {'x': jax.random.normal(ks[0], (B, S, D_IN), dtype=jnp.float32), 'Wr': jax.random.uniform(ks[1], (D_IN, N_EXPERTS), jnp.float32, -scale_in, scale_in), 'br': jax.random.uniform(ks[2], (N_EXPERTS,), jnp.float32, -scale_in, scale_in), 'W1': jax.random.uniform(ks[3], (N_EXPERTS, D_IN, D_HID), jnp.float32, -scale_in, scale_in), 'b1': jax.random.uniform(ks[4], (N_EXPERTS, D_HID), jnp.float32, -scale_in, scale_in), 'W2': jax.random.uniform(ks[5], (N_EXPERTS, D_HID, D_OUT), jnp.float32, -scale_hid, scale_hid), 'b2': jax.random.uniform(ks[6], (N_EXPERTS, D_OUT), jnp.float32, -scale_hid, scale_hid)}
    _L1_ffn_all = _L1_ffn_setup()
    _L1_ffn_in = {k: v for k, v in _L1_ffn_all.items() if k in ('Wr', 'br', 'W1', 'b1', 'W2', 'b2')}
    del _L1_ffn_all
    return {'x': x, 'L0_tok_W': _L0_tok_in['W'], 'L0_tok_b': _L0_tok_in['b'], 'L0_attn_Wq': _L0_attn_in['Wq'], 'L0_attn_Wk': _L0_attn_in['Wk'], 'L0_attn_Wv': _L0_attn_in['Wv'], 'L0_attn_Wo': _L0_attn_in['Wo'], 'L0_ffn_Wg': _L0_ffn_in['Wg'], 'L0_ffn_bg': _L0_ffn_in['bg'], 'L0_ffn_bias': _L0_ffn_in['bias'], 'L0_ffn_W1': _L0_ffn_in['W1'], 'L0_ffn_b1': _L0_ffn_in['b1'], 'L0_ffn_W2': _L0_ffn_in['W2'], 'L0_ffn_b2': _L0_ffn_in['b2'], 'L1_attn_q_weight': _L1_attn_in['q_weight'], 'L1_ffn_Wr': _L1_ffn_in['Wr'], 'L1_ffn_br': _L1_ffn_in['br'], 'L1_ffn_W1': _L1_ffn_in['W1'], 'L1_ffn_b1': _L1_ffn_in['b1'], 'L1_ffn_W2': _L1_ffn_in['W2'], 'L1_ffn_b2': _L1_ffn_in['b2']}

def reference(x, L0_tok_W, L0_tok_b, L0_attn_Wq, L0_attn_Wk, L0_attn_Wv, L0_attn_Wo, L0_ffn_Wg, L0_ffn_bg, L0_ffn_bias, L0_ffn_W1, L0_ffn_b1, L0_ffn_W2, L0_ffn_b2, L1_attn_q_weight, L1_ffn_Wr, L1_ffn_br, L1_ffn_W1, L1_ffn_b1, L1_ffn_W2, L1_ffn_b2):
    import jax
    import jax.numpy as jnp

    def _L0_tok_ref(x, W, b):
        import jax, jax.numpy as jnp
        import numpy as np
        PATCH = 16
        B, C, H, Wd = x.shape
        p = PATCH
        nH, nW = (H // p, Wd // p)
        patches = x.reshape(B, C, nH, p, nW, p)
        patches = patches.transpose(0, 2, 4, 1, 3, 5)
        patches = patches.reshape(B, nH * nW, C * p * p)
        return jnp.einsum('bnk,ek->bne', patches, W) + b

    def _L0_attn_ref(x, Wq, Wk, Wv, Wo):
        import jax, jax.numpy as jnp
        import numpy as np
        N_EMBD = 64
        N_HEAD = 8
        BATCH = 4
        SEQ = 512
        NEG_BIAS = -1000000000.0
        B, L, E = x.shape
        H, D = (N_HEAD, N_EMBD)

        def proj(W):
            y = jnp.einsum('ble,fe->blf', x, W)
            return y.reshape(B, L, H, D).transpose(0, 2, 1, 3)
        q, k, v = (proj(Wq), proj(Wk), proj(Wv))
        scores = jnp.einsum('bhld,bhmd->bhlm', q, k) * E ** (-0.5)
        attn = jax.nn.softmax(scores, axis=-1)
        causal = jnp.tril(jnp.ones((L, L), dtype=bool))
        attn = jnp.where(causal[None, None], attn, jnp.asarray(NEG_BIAS, attn.dtype))
        attn = jax.nn.softmax(attn, axis=-1)
        out = jnp.einsum('bhlm,bhmd->bhld', attn, v)
        out = out.transpose(0, 2, 1, 3).reshape(B, L, H * D)
        return jnp.einsum('blf,ef->ble', out, Wo)

    def _L0_ffn_ref(x, Wg, bg, bias, W1, b1, W2, b2):
        import jax, jax.numpy as jnp
        import numpy as np
        D_MODEL = 64
        EXPERT_DIM = 128
        NUM_EXPERTS = 8
        TOP_K = 2
        SEQ_LEN = 512
        BATCH = 2
        x_flat = x.reshape(-1, D_MODEL)
        gate_logits = x_flat @ Wg + bg + bias
        topk_vals, topk_idx = jax.lax.top_k(gate_logits, TOP_K)
        topk_w = jax.nn.softmax(topk_vals, axis=-1)
        combine = (jax.nn.one_hot(topk_idx, NUM_EXPERTS, dtype=x.dtype) * topk_w[..., None]).sum(axis=1)
        h = jax.nn.relu(jnp.einsum('td,edh->teh', x_flat, W1) + b1)
        y = jnp.einsum('teh,ehd->ted', h, W2) + b2
        out = jnp.einsum('ted,te->td', y, combine)
        return out.reshape(x.shape)

    def _L1_attn_ref(input, q_weight):
        import jax, jax.numpy as jnp
        import numpy as np
        query = jnp.einsum('bnd,de->bne', input, q_weight)
        att = jax.nn.sigmoid(jnp.einsum('bnd,bmd->bnm', query, input))
        value = jnp.einsum('bnm,bmd->bnd', att, input)
        return value

    def _L1_ffn_ref(x, Wr, br, W1, b1, W2, b2):
        import jax, jax.numpy as jnp
        import numpy as np
        D_IN, D_HID, D_OUT = (64, 128, 64)
        N_EXPERTS, TOP_K = (64, 2)
        B, S = (8, 1024)
        Bx, Sx, D = x.shape
        xf = x.reshape(-1, D)
        T = xf.shape[0]
        E = Wr.shape[1]
        logits = xf @ Wr + br
        topk_logits, topk_idx = jax.lax.top_k(logits, TOP_K)
        gates = jax.nn.softmax(topk_logits, axis=1)
        combine = jnp.zeros((T, E), xf.dtype).at[jnp.arange(T)[:, None], topk_idx].add(gates)
        out = jnp.zeros((T, W2.shape[-1]), xf.dtype)
        for e in range(E):
            h = jax.nn.relu(xf @ W1[e] + b1[e])
            y = h @ W2[e] + b2[e]
            out = out + combine[:, e:e + 1] * y
        return out.reshape(Bx, Sx, -1)
    h = _L0_tok_ref(x, L0_tok_W, L0_tok_b)
    h = h + _L0_attn_ref(_layernorm(h, axis=-1), L0_attn_Wq, L0_attn_Wk, L0_attn_Wv, L0_attn_Wo)
    h = h + _L0_ffn_ref(_layernorm(h, axis=-1), L0_ffn_Wg, L0_ffn_bg, L0_ffn_bias, L0_ffn_W1, L0_ffn_b1, L0_ffn_W2, L0_ffn_b2)
    h = h + _L1_attn_ref(_layernorm(h, axis=-1), L1_attn_q_weight)
    h = h + _L1_ffn_ref(_layernorm(h, axis=-1), L1_ffn_Wr, L1_ffn_br, L1_ffn_W1, L1_ffn_b1, L1_ffn_W2, L1_ffn_b2)
    return h

_drawn_inputs = setup_inputs


def setup_inputs(seed=0):
    import zlib

    import numpy as np

    out = dict(_drawn_inputs(seed))
    spreads = {'L0_ffn_bias': (0.0, 0.1)}
    factors = {'L0_attn_Wq': 8.0,
     'L0_attn_Wk': 8.0,
     'L0_ffn_bg': 4.283,
     'L0_ffn_b1': 6.272,
     'L1_ffn_Wr': 5.713,
     'L1_ffn_br': 8.0,
     'L1_ffn_W1': 6.919,
     'L1_ffn_b1': 8.0,
     'L1_ffn_W2': 5.687,
     'L1_ffn_b2': 25.453}
    for name, (base, spread) in spreads.items():
        noise = np.random.default_rng([zlib.crc32(name.encode()), seed]).standard_normal(out[name].shape)
        drawn = base * np.exp(spread * noise) if base else spread * noise
        out[name] = jnp.asarray(drawn.astype(out[name].dtype))
    for name, factor in factors.items():
        out[name] = (out[name] * factor).astype(out[name].dtype)
    return out
```

```python
from contextlib import ExitStack

import concourse.bass as bass
from concourse import mybir

F32 = mybir.dt.float32
F16 = mybir.dt.float16
BF16 = mybir.dt.bfloat16
I32 = mybir.dt.int32
U32 = mybir.dt.uint32
ALU = mybir.AluOpType
ACT = mybir.ActivationFunctionType
AX = mybir.AxisListType.X

PATCH = 16
EPS = 1e-5
NEG = -1e30
B2ROW = 96


class Chain:

    def __init__(self, eng, sem, per_round):
        self.eng, self.sem, self.per, self.n, self.done = eng, sem, per_round, 0, 0

    def start(self, n):
        self.n, self.done = n, 0

    def add(self, instruction):
        instruction.then_inc(self.sem, 1)
        self.done += 1

    def wait(self):
        self.eng.wait_ge(self.sem, self.n * self.per + self.done)

    def end(self):
        assert self.done == self.per, (self.done, self.per)


def vit_tower(nc, x, tokW, tokb, Wq, Wk, Wv, WoT, Wg, bg, bias, W1, b1, b1T, W2, b2,
              qw, Wr, br, E1W, out):
    NIMG, CH, HH, WW = x.shape
    NH, NW = HH // PATCH, WW // PATCH
    L = NH * NW
    LB = L // 2
    NPAIR = NIMG // 2
    T = NIMG * L
    NBLK = T // LB
    E = tokb.shape[0]
    KR = CH * PATCH
    HEADS = Wq.shape[0] // E
    SUB = 2 * HEADS
    X0, HID = W1.shape[0], W1.shape[2]
    X1 = Wr.shape[1]
    TILE = 128
    CAP = (T // TILE + 2) * TILE
    NB2 = 8
    NTILE = -(-(2 * T // TILE + X1 - 1) // NB2) * NB2
    ROW = E + 2
    FAR = 2.0 ** 20
    SC_V, SC_0, SC_R = 64.0, 256.0, 16.0
    assert E == 64 and LB <= 128 and HID == 128 and L % 2 == 0 and 2 * T < FAR and X1 * CAP < 2 ** 24

    with ExitStack() as ctx:
        def sb(name, shape, dt=F32):
            return ctx.enter_context(nc.sbuf_tensor(name, shape, dt))

        def sem(name):
            return ctx.enter_context(nc.semaphore(name))

        def bank(name):
            return ctx.enter_context(nc.psum_tensor(name, [128, 512], F32))
        ps_s = [bank("ps_s0"), bank("ps_s1")]
        ps_u, ps_t, ps_o, ps_e = bank("ps_u"), bank("ps_t"), bank("ps_o"), bank("ps_e")
        ps_b = [bank("ps_b0"), bank("ps_b1")]

        rows_d = nc.dram_tensor("rows_scratch", (X1 * CAP + TILE, ROW), F32).ap()
        y_d = nc.dram_tensor("y_scratch", (2 * T, E), F32).ap()
        gate_d = nc.dram_tensor("gate_scratch", (NPAIR, X0, 2 * L), F32).ap()

        ident = sb("ident", [128, 128])
        center = [sb("center_a", [128, 128]), sb("center_b", [128, 128])]
        average = sb("average", [128, 128])
        before = sb("before", [128, 128], BF16)
        ones16 = sb("ones16", [128, 128], BF16)
        upto = sb("upto", [X1, X1])
        onesf = sb("onesf", [128, 8])
        power = sb("power", [128, 4])
        ident16 = sb("ident16", [LB, LB], F16)
        eps = sb("eps", [128, 1])
        iota_i = sb("iota_i", [128, NTILE], I32)
        iota = sb("iota", [128, NTILE])
        iota_p_i = sb("iota_p_i", [128, 1], I32)
        iota_p = sb("iota_p", [128, 1])
        region = sb("region", [LB, X1])
        place = sb("place", [LB, 8])
        tokw = sb("tokw", [128, PATCH, 128])
        tokbias = sb("tokbias", [128, 1])
        raw = sb("raw", [128, 2048])
        raw2 = sb("raw2", [128, 1024])
        g16 = sb("g16", [128, HEADS, 128], F16)
        v16 = sb("v16", [128, HEADS * E], F16)
        wg16 = sb("wg16", [128, X0], F16)
        w116 = sb("w116", [128, X0 * HID], F16)
        qw16 = sb("qw16", [128, 128], F16)
        wr16 = sb("wr16", [128, X1], F16)
        w2s = sb("w2s", [HID, X0, E])
        b1raw = sb("b1raw", [HID, X0])
        nb1 = sb("nb1", [HID, X0])
        b1diag = sb("b1diag", [HID, X0, X0])
        b2raw = sb("b2raw", [X0, E])
        b2p = sb("b2p", [X0, E])
        bgb = sb("bgb", [LB, 2, X0])
        brb = sb("brb", [LB, X1])
        tail = sb("tail", [TILE, ROW])

        xin = sb("xin", [128, NH, WW])
        NA = 4
        h_a = sb("h_a", [128, L])
        sq_a = sb("sq_a", [128, 2 * L])
        rs_a = sb("rs_a", [128, 2 * L])
        st_a = sb("st_a", [LB, 4])
        sth_a = sb("sth_a", [LB, 2, 4], F16)
        xf_a = sb("xf_a", [128, 2 * L])
        xh_a = sb("xh_a", [128, 2 * L], F16)
        xl_a = sb("xl_a", [128, 2 * L], F16)
        vt = sb("vt", [LB, 4, HEADS * E])
        us = [sb(f"us{i}", [128, 2 * L], F16) for i in range(2)]
        e1 = [sb(f"e1{i}", [LB, 2, L]) for i in range(NA)]
        nmax = [sb(f"nmax{i}", [LB, 2]) for i in range(NA)]
        sum1 = [sb(f"sum1{i}", [LB, 2]) for i in range(NA)]
        rin1 = [sb(f"rin1{i}", [LB, 2]) for i in range(NA)]
        sum2 = [sb(f"sum2{i}", [LB, 2]) for i in range(NA)]
        rin2 = [sb(f"rin2{i}", [LB, 2]) for i in range(NA)]
        p2 = [sb(f"p2{i}", [LB, 3 * LB]) for i in range(NA)]
        pt = [sb(f"pt{i}", [LB, 3 * LB]) for i in range(NA)]

        h_b = sb("h_b", [128, L])
        sq_b = sb("sq_b", [128, 2 * L])
        rs_b = sb("rs_b", [128, 2 * L])
        st_b = sb("st_b", [LB, 4])
        sth_b = sb("sth_b", [LB, 2, 4], F16)
        xf_b = sb("xf_b", [128, 2 * L])
        xh_b = sb("xh_b", [128, 2 * L], F16)
        xl_b = sb("xl_b", [128, 2 * L], F16)
        lg = sb("lg", [LB, 4, X1])
        mx8 = sb("mx8", [LB, 4, 8])
        ix8 = sb("ix8", [LB, 4, 8], U32)
        ixf = sb("ixf", [LB, 8])
        dif = sb("dif", [LB, 4])
        edif = sb("edif", [LB, 4])
        eone = sb("eone", [LB, 4])
        gates = sb("gates", [LB, 4, 2])
        onehot = sb("onehot", [LB, 8, X1])
        weighed = sb("weighed", [LB, 8, X1])
        comb = sb("comb", [LB, 4, X0])
        combT = sb("combT", [X0, 2 * L])
        combB = sb("combB", [128, X0, 2 * L])
        hid = [sb(f"hid{i}", [HID, 2 * L]) for i in range(2)]
        q16 = sb("q16", [128, 2 * L], F16)
        x3t = sb("x3t", [LB, 4, E])
        th = [sb(f"th{i}", [LB, 2 * L]) for i in range(2)]
        colsum = sb("colsum", [128, 1])
        half = sb("half", [128, L])
        hres = sb("hres", [LB, NBLK, E])
        rows = sb("rows", [LB, 8, ROW])
        chosen = sb("chosen", [LB, 4, X1], BF16)
        seen = sb("seen", [LB, X1])
        seen16 = sb("seen16", [LB, X1], BF16)
        added = sb("added", [LB, X1])
        ranked = sb("ranked", [LB, 4, X1])
        posf = sb("posf", [LB, 8])
        posi = sb("posi", [LB, 8], U32)

        cnt = sb("cnt", [X1, 1])
        steps = sb("steps", [X1, T // TILE + 1])
        less = sb("less", [X1, T // TILE + 1])
        ntl = sb("ntl", [X1, 1])
        cum = sb("cum", [X1, 1])
        past = sb("past", [X1, NTILE])
        skip = sb("skip", [X1, 1])
        fillf = sb("fillf", [1, X1])
        filli = sb("filli", [1, X1], I32)
        metaf = sb("metaf", [1, 2, NTILE])
        metai = sb("metai", [1, NTILE // NB2, NB2, 2], I32)

        xr = [sb(f"xr{i}", [TILE, ROW]) for i in range(NB2)]
        wt = [sb(f"wt{i}", [128, HID + E]) for i in range(NB2)]
        ones_row = sb("ones_row", [128, TILE])
        xT = [sb(f"xT{i}", [E + 1, TILE]) for i in range(2)]
        hT = [sb(f"hT{i}", [HID, TILE]) for i in range(2)]
        yo = [sb(f"yo{i}", [TILE, E]) for i in range(NB2)]
        dst = [sb(f"dst{i}", [TILE, 1], U32) for i in range(NB2)]
        CB = 8
        yin = [sb(f"yin{i}", [LB, 2, CB, E]) for i in range(2)]
        ysum = [sb(f"ysum{i}", [LB, CB, E]) for i in range(2)]
        yfin = [sb(f"yfin{i}", [LB, CB, E]) for i in range(2)]

        w_qk, w_vo, w_rest, w_emb, w_misc = sem("w_qk"), sem("w_vo"), sem("w_rest"), sem("w_emb"), sem("w_misc")
        zeroed, consts, pool_c, emb_zero = sem("zeroed"), sem("consts"), sem("pool_c"), sem("emb_zero")
        g_mm, g_hi, g_lo, prep = sem("g_mm"), sem("g_hi"), sem("g_lo"), sem("prep")
        raw_free, bias_mm = sem("raw_free"), sem("bias_mm")
        x_in, emb_done, h_ready, hb_ready = sem("x_in"), sem("emb_done"), sem("h_ready"), sem("hb_ready")
        a_vs, a_rs, b_vs, b_rs = sem("a_vs"), sem("a_rs"), sem("b_vs"), sem("b_rs")
        a_rb, a_rbs, b_rb, b_rbs, pa_self, pb_self = sem("a_rb"), sem("a_rbs"), sem("b_rb"), sem("b_rbs"), sem("pa_self"), sem("pb_self")
        a_cen, a_sq, a_var, a_x, a_self = sem("a_cen"), sem("a_sq"), sem("a_var"), sem("a_x"), sem("a_self")
        v_mm, v_evac, u_mm, u_hi, u_lo = sem("v_mm"), sem("v_evac"), sem("u_mm"), sem("u_hi"), sem("u_lo")
        s_mm, max_done, e1_done, mask_done, r1_done = sem("s_mm"), sem("max_done"), sem("e1_done"), sem("mask_done"), sem("r1_done")
        e2_done, p2_done, t_mm, t_evac, pv_mm = sem("e2_done"), sem("p2_done"), sem("t_mm"), sem("t_evac"), sem("pv_mm")
        b_cen, b_sq, b_var, b_x, b_self = sem("b_cen"), sem("b_sq"), sem("b_var"), sem("b_x"), sem("b_self")
        g0_mm, g0_dif, g0_exp, comb_done, cT_mm, cT_sb = sem("g0_mm"), sem("g0_dif"), sem("g0_exp"), sem("comb_done"), sem("cT_mm"), sem("cT_sb")
        cT_out, comb_in, z_mm, hid_done, y_mm, h2_done = sem("cT_out"), sem("comb_in"), sem("z_mm"), sem("hid_done"), sem("y_mm"), sem("h2_done")
        q_mm, q_hi, q_lo, x3_mm, x3_sb, s3_mm, th_done = sem("q_mm"), sem("q_hi"), sem("q_lo"), sem("x3_mm"), sem("x3_sb"), sem("s3_mm"), sem("th_done")
        val_mm, h3_done, h3T_mm, h3T_sb, g1_mm, g1_dif, g1_exp = sem("val_mm"), sem("h3_done"), sem("h3T_mm"), sem("h3T_sb"), sem("g1_mm"), sem("g1_dif"), sem("g1_exp")
        chosen_done, rank_mm, rows_done, rows_out = sem("chosen_done"), sem("rank_mm"), sem("rows_done"), sem("rows_out")
        cnt_mm, cum_in, cum_mm, past_in, meta_mm, meta_done, fill_out, d_self = sem("cnt_mm"), sem("cum_in"), sem("cum_mm"), sem("past_in"), sem("meta_mm"), sem("meta_done"), sem("fill_out"), sem("d_self")
        x_tile = [sem(f"x_tile{i}") for i in range(NB2)]
        xT_mm, xT_sb, zt_mm, hT_sb, yt_mm, yo_done = sem("xT_mm"), sem("xT_sb"), sem("zt_mm"), sem("hT_sb"), sem("yt_mm"), sem("yo_done")
        y_out = [sem(f"y_out{i}") for i in range(NB2)]
        y_in = [sem(f"y_in{i}") for i in range(2)]
        ys_done, fin_done = sem("ys_done"), sem("fin_done")
        fin_out = [sem(f"fin_out{i}") for i in range(2)]

        passed = {e: sem(f"passed_{n}") for e, n in ((mybir.EngineType.SP, "sp"), (mybir.EngineType.Pool, "pool"),
                                                     (mybir.EngineType.PE, "pe"), (mybir.EngineType.DVE, "dve"))}
        A_LINKS, B_LINKS = 2 + SUB, 33
        PREP = 11
        CONSTS = 18
        block = ctx.enter_context(nc.Block())

        def alone(eng):
            eng.sem_inc(passed[eng.engine], 1)

        def x_rows(img):
            return x[img:img + 1] if isinstance(img, int) else x[bass.ds(img, 1)]

        @block.sync
        def _(sp):
            def load_images(n):
                for img in range(2):
                    for c in range(CH):
                        src = x_rows(2 * n + img)[:, c].rearrange("o (a p) w -> p (o a) w", p=PATCH)
                        r = 64 * img + c * PATCH
                        sp.dma_start(xin[r:r + PATCH], src).then_inc(x_in, 16)

            sp.wait_ge(zeroed, 1)
            load_images(0)
            sp.wait_ge(emb_zero, 1)
            for r in range(2):
                sp.dma_start(tokw[64 * r:64 * r + KR, :, 64 * r:64 * r + E], tokW).then_inc(w_emb, 16)
                sp.dma_start(tokbias[64 * r:64 * r + E], tokb.rearrange("(e o) -> e o", o=1)).then_inc(w_emb, 16)
            for r in range(2):
                sp.dma_start(raw[0:E, 0:1024].rearrange("d (h i) -> d h i", h=HEADS)[:, :, 64 * r:64 * r + E],
                             Wq.rearrange("(h d) i -> d h i", d=E)).then_inc(w_qk, 16)
                sp.dma_start(raw[0:E, 1024:2048].rearrange("d (h i) -> d h i", h=HEADS)[:, :, 64 * r:64 * r + E],
                             Wk.rearrange("(h d) i -> d h i", d=E)).then_inc(w_qk, 16)
            for r in range(2):
                lo, hi = 64 * r, 64 * r + E
                sp.dma_start(raw2[lo:hi, 0:X0], Wg).then_inc(w_misc, 16)
                sp.dma_start(raw2[lo:hi, X0:X0 + X1], Wr).then_inc(w_misc, 16)
                for c in range(2):
                    sp.dma_start(raw2[lo:hi, 128 + E * c:128 + E * (c + 1)], qw).then_inc(w_misc, 16)
            sp.dma_start(b1raw[:], b1T).then_inc(w_misc, 16)
            sp.dma_start(b2raw[:], b2).then_inc(w_misc, 16)
            sp.dma_start(w2s[:], W2.rearrange("x h e -> h x e")).then_inc(w_misc, 16)
            sp.dma_start(bgb[:, 0, :], bg.partition_broadcast(LB)).then_inc(w_misc, 16)
            sp.dma_start(bgb[:, 1, :], bias.partition_broadcast(LB)).then_inc(w_misc, 16)
            sp.dma_start(brb[:], br.partition_broadcast(LB)).then_inc(w_misc, 16)
            sp.wait_ge(g_mm, 2)
            for r in range(2):
                sp.dma_start(raw[0:E, 0:1024].rearrange("d (h i) -> d h i", h=HEADS)[:, :, 64 * r:64 * r + E],
                             Wv.rearrange("(h d) i -> d h i", d=E)).then_inc(w_vo, 16)
            sp.dma_start(raw[0:E, 1024:1024 + HEADS * E].rearrange("d (h e) -> d h e", h=HEADS),
                         WoT.rearrange("(h d) e -> d h e", d=E)).then_inc(w_vo, 16)
            sp.wait_ge(g_mm, 3)
            for r in range(2):
                sp.dma_start(raw[64 * r:64 * r + E, 0:X0 * HID].rearrange("d (x h) -> d x h", x=X0),
                             W1.rearrange("x d h -> d x h")).then_inc(w_rest, 16)

            def sp_stage_a(n, more=True):
                if more:
                    sp.wait_ge(emb_done, n + 2)
                    load_images(n + 2)

            def sp_stage_b(n):
                sp.wait_ge(cT_sb, n + 1)
                sp.dma_start(gate_d[n] if isinstance(n, int) else gate_d[bass.ds(n, 1)].rearrange("o x t -> (o x) t"),
                             combT[:]).then_inc(cT_out, 16)
                sp.wait_ge(cT_out, 16 * (n + 1))
                alone(sp)
                sp.wait_ge(hid_done, X0 * n) if not (isinstance(n, int) and n == 0) else None
                src = gate_d[n] if isinstance(n, int) else gate_d[bass.ds(n, 1)].rearrange("o x t -> (o x) t")
                sp.dma_start(combB[:].rearrange("p x t -> p (x t)"),
                             src.rearrange("x t -> (x t)").partition_broadcast(128)).then_inc(comb_in, 16)

            sp.wait_ge(emb_done, 1)
            load_images(1)
            sp_stage_a(0)
            sp_stage_b(0)
            sp_stage_a(1)
            with sp.Fori(1, NPAIR - 3) as t:
                sp_stage_b(t)
                sp_stage_a(t + 1)
            sp_stage_b(NPAIR - 3)
            sp_stage_b(NPAIR - 2)
            sp_stage_b(NPAIR - 1)

            sp.wait_ge(rows_out, 16 * 8 * NPAIR)
            sp.wait_ge(meta_done, 1)
            sp.dma_start(rows_d[X1 * CAP:X1 * CAP + TILE], tail[:]).then_inc(fill_out, 16)
            FG = 16
            with sp.Fori(0, X1 // FG) as e:
                alone(sp)
                _, ends = nc.values_load_multi_w_load_instructions(filli[0:1, bass.ds(e * FG, FG)], engines=[mybir.EngineType.SP],
                                                                   min_val=0, max_val=X1 * CAP - TILE,
                                                                   skip_runtime_bounds_check_because="an expert has at most T rows, below CAP - TILE")
                for i in range(FG):
                    sp.dma_start(rows_d[bass.ds(ends[i], TILE)], tail[:]).then_inc(fill_out, 16)
            sp.wait_ge(fill_out, 16 * (X1 + 1))

            def load_tiles(g, reuse):
                src = metai[0:1, g] if isinstance(g, int) else metai[0:1, bass.ds(g, 1)].rearrange("o g i k -> o (g i) k")
                alone(sp)
                _, at = nc.values_load_multi_w_load_instructions(src.rearrange("o i k -> o (i k)"), engines=[mybir.EngineType.SP],
                                                                 min_val=0, max_val=X1 * CAP,
                                                                 skip_runtime_bounds_check_because="metai is clamped")
                for i in range(NB2):
                    if reuse:
                        sp.wait_ge(yo_done, g * NB2 + i - (NB2 - 1))
                        alone(sp)
                    row, ex = at[2 * i], nc.s_assert_within(at[2 * i + 1], 0, X1 - 1, skip_runtime_bounds_check_because="metai's experts are clamped to X1 - 1")
                    sp.dma_start(xr[i][:], rows_d[bass.ds(row, TILE)]).then_inc(x_tile[i], 16)
                    sp.dma_start(wt[i][:], E1W[bass.ds(ex, 1)].rearrange("o d h -> (o d) h")).then_inc(x_tile[i], 16)

            load_tiles(0, False)
            with sp.Fori(1, NTILE // NB2) as g:
                load_tiles(g, True)

            for i in range(NB2):
                sp.wait_ge(y_out[i], 16 * (NTILE // NB2))

            def load_y(s, i, reuse):
                if reuse:
                    sp.wait_ge(ys_done, s - 1)
                for c in range(2):
                    src = y_d[bass.ds(T * c + s * (CB * LB), CB * LB)].rearrange("(b p) e -> p b e", p=LB)
                    sp.dma_start(yin[i][:, c], src).then_inc(y_in[i], 16)

            load_y(0, 0, False)
            load_y(1, 1, False)
            out_rows = out.rearrange("i t e -> (i t) e")

            def store(s, i):
                sp.wait_ge(fin_done, s + 1)
                sp.dma_start(out_rows[bass.ds(s * (CB * LB), CB * LB)].rearrange("(b p) e -> p b e", p=LB),
                             yfin[i][:]).then_inc(fin_out[i], 16)

            NS = NBLK // CB
            with sp.Fori(0, NS // 2 - 1) as g:
                s = g * 2
                for i in range(2):
                    load_y(s + 2 + i, i, True)
                    store(s + i, i)
            for i in range(2):
                store(NS - 2 + i, i)
            for i in range(2):
                sp.wait_ge(fin_out[i], 16 * (NS // 2))

        @block.gpsimd
        def _(pool):
            pool.memset(xin[:], 0.0).then_inc(zeroed, 1)
            pool.memset(tokw[:], 0.0).then_inc(emb_zero, 1)
            made = [0]

            def own(ins):
                ins.then_inc(pool_c, 1)
                made[0] += 1
                pool.wait_ge(pool_c, made[0])

            def diagonal(m, fill, base=0):
                n = m.shape[1]
                return pool.affine_select(out=m, in_=m, compare_op=ALU.not_equal, fill=fill, base=base,
                                          pattern=[[-1, n]], channel_multiplier=1)

            own(pool.memset(ident[:], 0.0))
            diagonal(ident[:], 1.0).then_inc(consts, 1)
            for img in range(2):
                own(pool.memset(center[img][:], 0.0))
                own(pool.memset(center[img][64 * img:64 * img + 64], -1.0 / E))
                for c in range(2):
                    part = center[img][64 * img:64 * img + 64, 64 * c:64 * c + 64]
                    diagonal(part, 1.0 - 1.0 / E).then_inc(consts, 1)
                    pool.wait_ge(consts, 2 + 2 * img + c)
            pool.memset(average[:], 0.5 / E).then_inc(consts, 1)
            own(pool.memset(before[:], 1.0))
            pool.affine_select(out=before[:], in_=before[:], compare_op=ALU.is_gt, fill=0.0, base=0,
                               pattern=[[1, 128]], channel_multiplier=-1).then_inc(consts, 1)
            pool.memset(ones16[:], 1.0).then_inc(consts, 1)
            own(pool.memset(upto[:], 1.0))
            pool.affine_select(out=upto[:], in_=upto[:], compare_op=ALU.is_ge, fill=0.0, base=0,
                               pattern=[[1, X1]], channel_multiplier=-1).then_inc(consts, 1)
            pool.memset(onesf[:], 1.0).then_inc(consts, 1)
            pool.memset(ones_row[:], 1.0).then_inc(consts, 1)
            pool.memset(power[:], -0.5).then_inc(consts, 1)
            pool.memset(eps[:], EPS).then_inc(consts, 1)
            own(pool.memset(ident16[:], 0.0))
            diagonal(ident16[:], 1.0).then_inc(consts, 1)
            pool.iota(iota_i[:], pattern=[[1, NTILE]], base=0, channel_multiplier=0).then_inc(consts, 1)
            pool.iota(iota_p_i[:], pattern=[[0, 1]], base=0, channel_multiplier=1).then_inc(consts, 1)
            own(pool.memset(tail[:], 0.0))
            pool.memset(tail[:, E + 1:E + 2], FAR).then_inc(consts, 1)
            pool.memset(seen[:], 0.0).then_inc(consts, 1)
            pool.memset(seen16[:], 0.0).then_inc(consts, 1)

            def pool_stage_a(n, k):
                pool.wait_ge(e1_done, SUB * n + k + 1)
                alone(pool)
                view = e1[k % NA][:].rearrange("p b m -> p (b m)")
                diag = bass.AP(view.tensor, view.offset, [list(view.ap[0]), [3 * LB, 2], [1, LB]])
                pool.affine_select(out=diag, in_=diag, compare_op=ALU.is_ge, fill=NEG, base=0,
                                   pattern=[[0, 2], [-1, LB]], channel_multiplier=1).then_inc(mask_done, 1)

            def pool_stage_b(n):
                pool.wait_ge(rows_done, n + 1)
                alone(pool)
                for c in range(8):
                    pool.indirect_dma_start(out=rows_d, out_offset=bass.IndirectOffsetOnAxis(ap=posi[:, c:c + 1], axis=0),
                                            in_=rows[:, c, :], in_offset=None).then_inc(rows_out, 16)

            pool.wait_ge(consts, CONSTS)

            PA, PB = Chain(pool, pa_self, 2), Chain(pool, pb_self, 6)

            def rstd(P, st, sth, done):
                P.add(pool.tensor_tensor(st[:], st[:], power[0:LB], ALU.pow))
                P.wait()
                alone(pool)
                P.add(pool.tensor_copy(sth[:, 0, :], st[:]))
                P.wait()
                pool.tensor_tensor(sth[:, 1, :], st[:], sth[:, 0, :], ALU.subtract).then_inc(done, 1)

            def rstd_a(n):
                pool.wait_ge(a_vs, n + 1)
                PA.start(n)
                rstd(PA, st_a, sth_a, a_rs)

            def rstd_b(n, r):
                pool.wait_ge(b_vs, 3 * n + r + 1)
                if r == 0:
                    PB.start(n)
                rstd(PB, st_b, sth_b, b_rs)

            def round_(n, a, nb):
                if a:
                    rstd_a(n)
                if nb is not None:
                    rstd_b(nb, 0)
                for k in range(SUB):
                    if a:
                        pool_stage_a(n, k)
                    if nb is not None and k in (9, 14):
                        rstd_b(nb, 1 if k == 9 else 2)
                if nb is not None:
                    pool_stage_b(nb)

            round_(0, True, None)
            round_(1, True, 0)
            with pool.Fori(1, NPAIR - 1) as t:
                round_(t + 1, True, t)
            round_(NPAIR, False, NPAIR - 1)

            def send(t, i):
                pool.wait_ge(yo_done, t + 1)
                alone(pool)
                pool.indirect_dma_start(out=y_d, out_offset=bass.IndirectOffsetOnAxis(ap=dst[i][:, 0:1], axis=0),
                                        in_=yo[i][:], in_offset=None, bounds_check=2 * T - 1, oob_is_err=False).then_inc(y_out[i], 16)

            with pool.Fori(0, NTILE // NB2) as g:
                t = g * NB2
                for i in range(NB2):
                    send(t + i, i)

        @block.tensor
        def _(pe):
            mm = pe.matmul

            pe.wait_ge(w_qk, 64)
            wq = raw[0:E, 0:1024].rearrange("d (h i) -> d h i", h=HEADS)
            wk = raw[0:E, 1024:2048].rearrange("d (h i) -> d h i", h=HEADS)
            for h in range(HEADS):
                last = mm(ps_s[h // 4][:, 128 * (h % 4):128 * (h % 4) + 128], wq[:, h], wk[:, h], start=True, stop=True)
                if h % 4 == 3:
                    last.then_inc(g_mm, 1)
            pe.wait_ge(w_vo, 48)
            wo = raw[0:E, 1024:1024 + HEADS * E].rearrange("d (h e) -> d h e", h=HEADS)
            for h in range(HEADS):
                last = mm(ps_u[:, E * h:E * h + E], wq[:, h], wo[:, h], start=True, stop=True)
            last.then_inc(g_mm, 1)
            pe.wait_ge(prep, 3)
            for e in range(X0):
                last = mm(ps_t[0:X0, 0:E], b1diag[:, e, :], w2s[:, e, :], start=e == 0, stop=e == X0 - 1)
            last.then_inc(bias_mm, 1)
            pe.wait_ge(consts, CONSTS)
            pe.wait_ge(w_emb, 64)
            pe.wait_ge(prep, PREP)
            pe.wait_ge(g_lo, 3)

            def embed(n, part):
                if part == 0:
                    pe.wait_ge(x_in, 16 * 2 * CH * (n + 1))
                    if not (isinstance(n, int) and n == 0):
                        pe.wait_ge(h_ready, n)
                for px in range(2 * part, 2 * part + 2):
                    last = mm(ps_e[:, 0:L], tokw[0:64 + KR, px, :],
                              xin[0:64 + KR].rearrange("p a (b q) -> p a b q", q=PATCH)[:, :, :, px],
                              start=px == 0, stop=px == PATCH - 1)
                if part == 7:
                    last.then_inc(emb_done, 1)

            def centered(dest, h):
                mm(dest[:, 0:L], center[0][:], h, start=True, stop=True)
                return mm(dest[:, L:2 * L], center[1][:], h, start=True, stop=True)

            def variances(dest, sq):
                for c in range(4):
                    last = mm(dest[0:LB, c:c + 1], sq[:, LB * c:LB * c + LB], average[:, 0:1], start=True, stop=True)
                return last

            def spread(dest, sth):
                for c in range(4):
                    for half_ in range(2):
                        last = mm(dest[:, LB * c:LB * c + LB], sth[:, half_, c:c + 1].to_broadcast([LB, 128]), ident16[:],
                                  start=half_ == 0, stop=half_ == 1)
                return last

            def start_a(n, step):
                if step == 0:
                    pe.wait_ge(h_ready, n + 1)
                    if not (isinstance(n, int) and n == 0):
                        pe.wait_ge(e1_done, SUB * n)
                    else:
                        pe.wait_ge(g_lo, 3)
                    centered(ps_s[0], h_a[:]).then_inc(a_cen, 1)
                if step == 1:
                    pe.wait_ge(a_sq, n + 1)
                    variances(ps_s[1], sq_a).then_inc(a_var, 1)
                if step == 2:
                    pe.wait_ge(a_rs, n + 1)
                    spread(ps_s[1], sth_a).then_inc(a_rb, 1)
                if step == 3:
                    pe.wait_ge(a_x, n + 1)
                    for c in range(4):
                        if c >= 2:
                            pe.wait_ge(v_evac, 4 * n + c - 1)
                        mm(ps_s[c % 2][0:LB, :], xh_a[:, LB * c:LB * c + LB], v16[:], start=True, stop=False)
                        mm(ps_s[c % 2][0:LB, :], xl_a[:, LB * c:LB * c + LB], v16[:], start=False, stop=True).then_inc(v_mm, 1)

            def u_step(n, h):
                if not (isinstance(n, int) and n == 0 and h == 0):
                    pe.wait_ge(u_lo, HEADS * n + h)
                mm(ps_u[:, 0:2 * L], g16[:, h, :], xh_a[:], start=True, stop=False)
                mm(ps_u[:, 0:2 * L], g16[:, h, :], xl_a[:], start=False, stop=True).then_inc(u_mm, 1)

            def s_step(n, k):
                h, img = k // 2, k % 2
                pe.wait_ge(u_lo, HEADS * n + h + 1)
                if k == 0:
                    pe.wait_ge(v_evac, 4 * n + 4)
                if k >= 2:
                    pe.wait_ge(e1_done, SUB * n + k - 1)
                u, sl = us[h % 2], slice(img * L, img * L + L)
                for b in range(2):
                    uu = u[:, img * L + LB * b:img * L + LB * b + LB]
                    mm(ps_s[k % 2][0:LB, L * b:L * b + L], uu, xh_a[:, sl], start=True, stop=False)
                    last = mm(ps_s[k % 2][0:LB, L * b:L * b + L], uu, xl_a[:, sl], start=False, stop=True)
                last.then_inc(s_mm, 1)

            def t_step(n, k):
                pe.wait_ge(p2_done, SUB * n + k + 1)
                if not (isinstance(n, int) and n == 0 and k == 0):
                    pe.wait_ge(t_evac, SUB * n + k)
                for c in range(3):
                    last = pe.transpose(ps_t[0:LB, LB * c:LB * c + LB], p2[k % NA][:, LB * c:LB * c + LB], ident[0:LB, 0:LB])
                last.then_inc(t_mm, 1)

            def pv_step(n, k):
                h, img = k // 2, k % 2
                pe.wait_ge(t_evac, SUB * n + k + 1)
                if k == 0 and not (isinstance(n, int) and n == 0):
                    pe.wait_ge(hb_ready, n)
                o = ps_o[64 * img:64 * img + E]
                mm(o[:, 0:L], vt[:, 2 * img, E * h:E * h + E], pt[k % NA][:, 0:L], start=h == 0, stop=False,
                   skip_group_check=True)
                mm(o[:, LB:L], vt[:, 2 * img + 1, E * h:E * h + E], pt[k % NA][:, L:L + LB], start=False,
                   stop=h == HEADS - 1, skip_group_check=True).then_inc(pv_mm, 1)

            def stage_b(n, j):
                X, Y = ps_b
                if j in (0, 22, 36):
                    r = {0: 0, 22: 1, 36: 2}[j]
                    if r == 0:
                        pe.wait_ge(hb_ready, n + 1)
                        if not (isinstance(n, int) and n == 0):
                            pe.wait_ge(rows_done, n)
                    elif r == 1:
                        pe.wait_ge(h2_done, n + 1)
                    else:
                        pe.wait_ge(h3_done, n + 1)
                    centered(X, h_b[:]).then_inc(b_cen, 1)
                if j in (1, 24, 38):
                    r = {1: 0, 24: 1, 38: 2}[j]
                    pe.wait_ge(b_sq, 3 * n + r + 1)
                    variances(Y, sq_b).then_inc(b_var, 1)
                if j in (3, 26, 41):
                    pe.wait_ge(b_rs, 3 * n + {3: 0, 26: 1, 41: 2}[j] + 1)
                    spread(Y, sth_b).then_inc(b_rb, 1)
                if j == 5:
                    pe.wait_ge(b_x, 3 * n + 1)
                    for c in range(4):
                        mm(X[0:LB, X0 * c:X0 * c + X0], xh_b[:, LB * c:LB * c + LB], wg16[:], start=True, stop=False)
                        last = mm(X[0:LB, X0 * c:X0 * c + X0], xl_b[:, LB * c:LB * c + LB], wg16[:], start=False, stop=True)
                    last.then_inc(g0_mm, 1)
                if j == 9:
                    pe.wait_ge(comb_done, n + 1)
                    for c in range(4):
                        last = pe.transpose(Y[0:X0, LB * c:LB * c + LB], comb[:, c, :], ident[0:LB, 0:LB])
                    last.then_inc(cT_mm, 1)
                if j == 12:
                    pe.wait_ge(cT_sb, n + 1)
                    for img in range(2):
                        mm(Y[64 * img:64 * img + E, 0:L], b2p[:], combT[:, img * L:img * L + L], start=True, stop=False,
                           skip_group_check=True)
                if 13 <= j <= 13 + X0:
                    e = j - 13
                    if e >= 1:
                        pe.wait_ge(hid_done, X0 * n + e)
                        for img in range(2):
                            last = mm(Y[64 * img:64 * img + E, 0:L], w2s[:, e - 1, :], hid[(e - 1) % 2][:, img * L:img * L + L],
                                      start=False, stop=e == X0, skip_group_check=True)
                        last.then_inc(y_mm, 1)
                    if e < X0:
                        mm(X[:, 0:2 * L], w116[:, HID * e:HID * e + HID], xh_b[:], start=True, stop=False)
                        mm(X[:, 0:2 * L], w116[:, HID * e:HID * e + HID], xl_b[:], start=False, stop=True).then_inc(z_mm, 1)
                if j == 29:
                    pe.wait_ge(b_x, 3 * n + 2)
                    mm(X[:, 0:2 * L], qw16[:], xh_b[:], start=True, stop=False)
                    mm(X[:, 0:2 * L], qw16[:], xl_b[:], start=False, stop=True).then_inc(q_mm, 1)
                    for c in range(4):
                        last = pe.transpose(Y[0:LB, E * c:E * c + E], xf_b[0:E, LB * c:LB * c + LB], ident[0:E, 0:E])
                    last.then_inc(x3_mm, 1)
                if j in (31, 32):
                    img = j - 31
                    pe.wait_ge(q_lo, n + 1)
                    pe.wait_ge(x3_sb, n + 1)
                    for c in range(2):
                        s = slice(img * L + LB * c, img * L + LB * c + LB)
                        mm(ps_b[img][0:LB, L * c:L * c + L], xh_b[:, s], q16[:, img * L:img * L + L], start=True, stop=False)
                        last = mm(ps_b[img][0:LB, L * c:L * c + L], xl_b[:, s], q16[:, img * L:img * L + L], start=False, stop=True)
                    last.then_inc(s3_mm, 1)
                if j == 34:
                    pe.wait_ge(th_done, 2 * n + 2)
                    for img in range(2):
                        for c in range(2):
                            last = mm(X[64 * img:64 * img + E, 0:L], x3t[:, 2 * img + c, :], th[img][:, L * c:L * c + L],
                                      start=c == 0, stop=c == 1)
                    last.then_inc(val_mm, 1)
                if j == 44:
                    pe.wait_ge(b_x, 3 * n + 3)
                    alone(pe)
                    for c in range(4):
                        pe.transpose(X[0:LB, 256 + E * c:256 + E * c + E], xf_b[0:E, LB * c:LB * c + LB], ident[0:E, 0:E])
                    for b in range(2):
                        last = pe.transpose(X[0:LB, 128 * b:128 * b + 128], h_b[:, LB * b:LB * b + LB], ident[:])
                    last.then_inc(h3T_mm, 1)
                    for c in range(4):
                        mm(Y[0:LB, X1 * c:X1 * c + X1], xh_b[:, LB * c:LB * c + LB], wr16[:], start=True, stop=False)
                        last = mm(Y[0:LB, X1 * c:X1 * c + X1], xl_b[:, LB * c:LB * c + LB], wr16[:], start=False, stop=True)
                    last.then_inc(g1_mm, 1)
                if j == 46:
                    pe.wait_ge(chosen_done, n + 1)
                    for c in range(4):
                        o = Y[0:LB, X1 * c:X1 * c + X1]
                        mm(o, ones16[0:LB, 0:LB], seen16[:], start=True, stop=False)
                        for d in range(c):
                            mm(o, ones16[0:LB, 0:LB], chosen[:, d, :], start=False, stop=False)
                        last = mm(o, before[0:LB, 0:LB], chosen[:, c, :], start=False, stop=True)
                    last.then_inc(rank_mm, 1)

            def round_(n, a, b, e):
                nb = b
                j = 0
                for step in range(4):
                    if a:
                        start_a(n, step)
                    if nb is not None:
                        stage_b(nb, j)
                        stage_b(nb, j + 1)
                    j += 2
                if a:
                    u_step(n, 0)
                    s_step(n, 0)
                for k in range(SUB + 4):
                    if a:
                        if k + 1 < SUB:
                            s_step(n, k + 1)
                        if k % 2 == 0 and k // 2 + 1 < HEADS:
                            u_step(n, k // 2 + 1)
                    if nb is not None:
                        stage_b(nb, j)
                    if a and 0 <= k - 3 < SUB:
                        t_step(n, k - 3)
                    if e is not None and k < 8:
                        embed(e, k)
                    if nb is not None:
                        stage_b(nb, j + 1)
                    if a and 0 <= k - 4 < SUB:
                        pv_step(n, k - 4)
                    j += 2

            for part in range(8):
                embed(0, part)
            round_(0, True, None, 1)
            round_(1, True, 0, 2)
            with pe.Fori(1, NPAIR - 2) as t:
                round_(t + 1, True, t, t + 2)
            round_(NPAIR - 1, True, NPAIR - 2, None)
            round_(NPAIR, False, NPAIR - 1, None)

            pe.wait_ge(rows_done, NPAIR)
            mm(ps_b[0][0:X1, 0:LB], seen16[:], ones16[0:LB, 0:LB], start=True, stop=True)
            mm(ps_b[1][0:1, 0:X1], ones16[0:LB, 0:1], seen16[:], start=True, stop=True).then_inc(cnt_mm, 1)
            pe.wait_ge(cum_in, 1)
            mm(ps_u[0:X1, 0:1], upto[:], ntl[:], start=True, stop=True).then_inc(cum_mm, 1)
            pe.wait_ge(past_in, 1)
            mm(ps_s[0][0:1, 0:NTILE], skip[:], past[:], start=True, stop=True)
            mm(ps_s[1][0:1, 0:NTILE], onesf[0:X1, 0:1], past[:], start=True, stop=True).then_inc(meta_mm, 1)
            pe.wait_ge(meta_done, 1)

            def x_step(t, i):
                pe.wait_ge(x_tile[i % NB2], 32 * ((t - i) // NB2 + 1) if isinstance(t, int) else (t - i) * (32 // NB2) + 32)
                if not (isinstance(t, int) and t < 2):
                    pe.wait_ge(xT_sb, t - 1)
                alone(pe)
                pe.transpose(ps_s[i % 2][0:E, 0:TILE], xr[i][:, 0:E], ident[:]).then_inc(xT_mm, 1)

            def z_step(t, i):
                pe.wait_ge(xT_sb, t + 1)
                if not (isinstance(t, int) and t < 2):
                    pe.wait_ge(hT_sb, t - 1)
                mm(ps_b[i % 2][:, 0:TILE], wt[i][0:E + 1, 0:HID], xT[i % 2][:], start=True, stop=True).then_inc(zt_mm, 1)

            def y_step(t, i):
                pe.wait_ge(hT_sb, t + 1)
                if not (isinstance(t, int) and t < 2):
                    pe.wait_ge(yo_done, t - 1)
                o = [ps_u, ps_t][i % 2][:, 0:E]
                mm(o, hT[i % 2][:], wt[i][:, HID:HID + E], start=True, stop=False)
                mm(o, ones_row[B2ROW:B2ROW + 1, :], wt[i][B2ROW:B2ROW + 1, 0:E], start=False, stop=True).then_inc(yt_mm, 1)

            for t in range(2 * NB2):
                x_step(t, t % NB2)
                if t >= 1:
                    z_step(t - 1, (t - 1) % NB2)
                if t >= 2:
                    y_step(t - 2, (t - 2) % NB2)
            with pe.Fori(2, NTILE // NB2) as g:
                t = g * NB2
                for i in range(NB2):
                    x_step(t + i, i)
                    z_step(t + i - 1, (i - 1) % NB2)
                    y_step(t + i - 2, (i - 2) % NB2)
            z_step(NTILE - 1, NB2 - 1)
            y_step(NTILE - 2, NB2 - 2)
            y_step(NTILE - 1, NB2 - 1)

        @block.scalar
        def _(act):
            def copy(dest, src, scale=1.0):
                return act.activation(dest, src, ACT.Copy, scale=scale)

            for g in range(2):
                act.wait_ge(g_mm, g + 1)
                copy(g16[:, 4 * g:4 * g + 4, :].rearrange("p h i -> p (h i)"), ps_s[g][:], E ** -0.5).then_inc(g_hi, 1)
            act.wait_ge(g_mm, 3)
            copy(v16[:], ps_u[:], SC_V).then_inc(g_hi, 1)
            act.wait_ge(consts, CONSTS)
            act.wait_ge(w_emb, 64)

            def start_a(n, step):
                if step == 0:
                    act.wait_ge(emb_done, n + 1)
                    if not (isinstance(n, int) and n == 0):
                        act.wait_ge(hb_ready, n)
                    act.activation(h_a[:], ps_e[:, 0:L], ACT.Identity, bias=tokbias[:, 0:1]).then_inc(h_ready, 1)
                    act.wait_ge(a_cen, n + 1)
                    act.activation(sq_a[:], ps_s[0][:, 0:2 * L], ACT.Square).then_inc(a_sq, 1)
                if step == 1:
                    act.wait_ge(a_var, n + 1)
                    act.activation(st_a[:], ps_s[1][0:LB, 0:4], ACT.Identity, bias=eps[0:LB, 0:1]).then_inc(a_vs, 1)
                if step == 2:
                    act.wait_ge(a_rb, n + 1)
                    copy(rs_a[:], ps_s[1][:, 0:2 * L]).then_inc(a_rbs, 1)
                if step == 3:
                    for c in range(4):
                        act.wait_ge(v_mm, 4 * n + c + 1)
                        copy(vt[:, c, :], ps_s[c % 2][0:LB, :], 1.0 / SC_V).then_inc(v_evac, 1)

            def u_hi_step(n, h):
                act.wait_ge(u_mm, HEADS * n + h + 1)
                copy(us[h % 2][:], ps_u[:, 0:2 * L]).then_inc(u_hi, 1)

            def exp1(n, k):
                act.wait_ge(max_done, SUB * n + k + 1)
                if not (isinstance(n, int) and n == 0 and k < NA):
                    act.wait_ge(e2_done, SUB * n + k - NA + 1)
                for b in range(2):
                    last = act.activation(e1[k % NA][:, b, :], ps_s[k % 2][0:LB, L * b:L * b + L], ACT.Exp,
                                          bias=nmax[k % NA][:, b:b + 1], accum_out=sum1[k % NA][:, b:b + 1])
                last.then_inc(e1_done, 1)

            def exp2(n, k):
                act.wait_ge(mask_done, SUB * n + k + 1)
                act.wait_ge(r1_done, SUB * n + k + 1)
                if not (isinstance(n, int) and n == 0 and k < NA):
                    act.wait_ge(t_mm, SUB * n + k - NA + 1)
                for b in range(2):
                    last = act.activation(p2[k % NA][:, LB * b:LB * b + LB * (b + 1)], e1[k % NA][:, b, 0:LB * (b + 1)],
                                          ACT.Exp, scale=rin1[k % NA][:, b:b + 1], accum_out=sum2[k % NA][:, b:b + 1])
                last.then_inc(e2_done, 1)

            def t_out(n, k):
                act.wait_ge(t_mm, SUB * n + k + 1)
                if not (isinstance(n, int) and n == 0 and k < NA):
                    act.wait_ge(pv_mm, SUB * n + k - NA + 1)
                copy(pt[k % NA][:], ps_t[0:LB, 0:3 * LB]).then_inc(t_evac, 1)

            def stage_b(n, j):
                X, Y = ps_b
                if j in (0, 23, 37):
                    r = {0: 0, 23: 1, 37: 2}[j]
                    act.wait_ge(b_cen, 3 * n + r + 1)
                    act.activation(sq_b[:], X[:, 0:2 * L], ACT.Square).then_inc(b_sq, 1)
                if j in (1, 25, 39):
                    r = {1: 0, 25: 1, 39: 2}[j]
                    act.wait_ge(b_var, 3 * n + r + 1)
                    act.activation(st_b[:], Y[0:LB, 0:4], ACT.Identity, bias=eps[0:LB, 0:1]).then_inc(b_vs, 1)
                if j in (3, 27, 42):
                    act.wait_ge(b_rb, 3 * n + {3: 0, 27: 1, 42: 2}[j] + 1)
                    copy(rs_b[:], Y[:, 0:2 * L]).then_inc(b_rbs, 1)
                if j in (7, 46):
                    act.wait_ge(*((g0_dif, n + 1) if j == 7 else (g1_dif, n + 1)))
                    act.activation(edif[:], dif[:], ACT.Exp).then_inc(g0_exp if j == 7 else g1_exp, 1)
                if j == 10:
                    act.wait_ge(cT_mm, n + 1)
                    if not (isinstance(n, int) and n == 0):
                        act.wait_ge(cT_out, 16 * n)
                    copy(combT[:], Y[0:X0, 0:2 * L]).then_inc(cT_sb, 1)
                if j == 30:
                    act.wait_ge(q_mm, n + 1)
                    copy(q16[:], X[:, 0:2 * L]).then_inc(q_hi, 1)
                    act.wait_ge(x3_mm, n + 1)
                    copy(x3t[:].rearrange("p c e -> p (c e)"), Y[0:LB, 0:4 * E]).then_inc(x3_sb, 1)
                if j in (32, 33):
                    img = j - 32
                    act.wait_ge(s3_mm, 2 * n + img + 1)
                    act.activation(th[img][:], ps_b[img][0:LB, 0:2 * L], ACT.Tanh, scale=0.5).then_inc(th_done, 1)
                if j == 45:
                    act.wait_ge(h3T_mm, n + 1)
                    if not (isinstance(n, int) and n == 0):
                        act.wait_ge(rows_out, 16 * 8 * n)
                    src = X[0:LB, 256:512].rearrange("p (c e) -> p c e", e=E)
                    for choice in range(2):
                        copy(rows[:].rearrange("p (c o) r -> p c o r", o=2)[:, :, choice, 0:E], src)
                    dest = hres[:, 4 * n:4 * n + 4, :] if isinstance(n, int) else hres[:, bass.ds(4 * n, 4), :]
                    for img in range(2):
                        d2 = hres[:, 4 * n + 2 * img:4 * n + 2 * img + 2, :] if isinstance(n, int) else hres[:, bass.ds(4 * n + 2 * img, 2), :]
                        last = copy(d2, X[0:LB, 0:256].rearrange("p (b i e) -> p i b e", b=2, i=2)[:, img])
                    last.then_inc(h3T_sb, 1)

            def round_(n, a, nb):
                j = 0
                for step in range(4):
                    if a:
                        start_a(n, step)
                    if nb is not None:
                        stage_b(nb, j)
                        stage_b(nb, j + 1)
                    j += 2
                if a:
                    u_hi_step(n, 0)
                for k in range(SUB + 4):
                    if a:
                        if k < SUB:
                            exp1(n, k)
                        if 0 <= k - 1 < SUB:
                            exp2(n, k - 1)
                        if k % 2 == 0 and k // 2 + 1 < HEADS:
                            u_hi_step(n, k // 2 + 1)
                    if nb is not None:
                        stage_b(nb, j)
                        stage_b(nb, j + 1)
                    if a and 0 <= k - 3 < SUB:
                        t_out(n, k - 3)
                    j += 2

            round_(0, True, None)
            round_(1, True, 0)
            with act.Fori(1, NPAIR - 1) as t:
                round_(t + 1, True, t)
            round_(NPAIR, False, NPAIR - 1)

            def h_out(t, i):
                act.wait_ge(zt_mm, t + 1)
                if not (isinstance(t, int) and t < 2):
                    act.wait_ge(yt_mm, t - 1)
                act.activation(hT[i % 2][:], ps_b[i % 2][:, 0:TILE], ACT.Relu).then_inc(hT_sb, 1)

            for i in range(NB2):
                h_out(i, i)
            with act.Fori(0, NTILE // NB2 - 1) as g:
                t = g * NB2
                for i in range(NB2):
                    h_out(t + NB2 + i, i)

        @block.vector
        def _(dve):
            dve.wait_ge(consts, CONSTS)
            dve.tensor_copy(iota[:], iota_i[:]).then_inc(prep, 1)
            dve.wait_ge(w_misc, 16 * 14)
            dve.tensor_copy(iota_p[:], iota_p_i[:]).then_inc(prep, 1)
            for e in range(X0):
                last = dve.tensor_scalar(b1diag[:, e, :], ident[:, 0:X0], 0.0, None, ALU.mult)
            last.then_inc(d_self, 1)
            dve.wait_ge(d_self, 1)
            dve.tensor_copy(b1diag[:].rearrange("p a b -> p (a b)")[:, 0:X0 * X0:X0 + 1], b1raw[:]).then_inc(prep, 1)
            dve.wait_ge(bias_mm, 1)
            dve.tensor_scalar(w2s[:].rearrange("p x e -> p (x e)"), w2s[:].rearrange("p x e -> p (x e)"), 1.0 / SC_0, None, ALU.mult).then_inc(prep, 1)
            dve.tensor_scalar(nb1[:], b1raw[:], -SC_0, None, ALU.mult).then_inc(prep, 1)
            dve.tensor_tensor(b2p[:], ps_t[0:X0, 0:E], b2raw[:], ALU.add).then_inc(prep, 1)
            dve.tensor_tensor(bgb[:, 0, :], bgb[:, 0, :], bgb[:, 1, :], ALU.add).then_inc(prep, 1)
            chain = [1]

            def own(ins):
                ins.then_inc(d_self, 1)
                chain[0] += 1
                dve.wait_ge(d_self, chain[0])

            def split(dest, src, scale):
                own(dve.tensor_scalar(dest, src, scale, None, ALU.mult))
                return dve.scalar_tensor_tensor(dest[64:128], src[64:128], scale, dest[64:128], ALU.mult, ALU.subtract)

            split(wg16[:], raw2[:, 0:X0], SC_0).then_inc(prep, 1)
            split(wr16[:], raw2[:, X0:X0 + X1], SC_R).then_inc(prep, 1)
            split(qw16[:], raw2[:, 128:256], 1.0).then_inc(prep, 1)
            for g in range(2):
                dve.wait_ge(g_hi, g + 1)
                d = g16[64:128, 4 * g:4 * g + 4, :].rearrange("p h i -> p (h i)")
                dve.scalar_tensor_tensor(d, ps_s[g][64:128, :], E ** -0.5, d, ALU.mult, ALU.subtract).then_inc(g_lo, 1)
            dve.wait_ge(g_hi, 3)
            dve.scalar_tensor_tensor(v16[64:128], ps_u[64:128], SC_V, v16[64:128], ALU.mult, ALU.subtract).then_inc(g_lo, 1)
            dve.wait_ge(w_rest, 32)
            split(w116[:], raw[:, 0:X0 * HID], SC_0).then_inc(prep, 1)
            own(dve.tensor_scalar(region[:], iota[0:LB, 0:X1], float(CAP), None, ALU.mult))
            for c in range(4):
                for choice in range(2):
                    last = dve.tensor_scalar(place[:, 2 * c + choice:2 * c + choice + 1], iota_p[0:LB], float(choice * T + c * LB), None, ALU.add)
            own(last)
            own(dve.memset(xT[0][E:E + 1, :], 1.0))
            own(dve.memset(xT[1][E:E + 1, :], 1.0))
            A, B = Chain(dve, a_self, A_LINKS), Chain(dve, b_self, B_LINKS)

            def start_a(n, step):
                if step == 2:
                    A.start(n)
                    dve.wait_ge(a_rbs, n + 1)
                    A.add(dve.tensor_tensor(xf_a[:], ps_s[0][:, 0:2 * L], rs_a[:], ALU.mult))
                    A.wait()
                    A.add(dve.tensor_copy(xh_a[:], xf_a[:]))
                    A.wait()
                    dve.tensor_tensor(xl_a[:], xf_a[:], xh_a[:], ALU.subtract).then_inc(a_x, 1)

            def u_lo_step(n, h):
                dve.wait_ge(u_hi, HEADS * n + h + 1)
                u = us[h % 2]
                dve.tensor_tensor(u[64:128], ps_u[64:128, 0:2 * L], u[64:128], ALU.subtract).then_inc(u_lo, 1)

            def max_step(n, k):
                dve.wait_ge(s_mm, SUB * n + k + 1)
                dve.tensor_reduce(nmax[k % NA][:], ps_s[k % 2][0:LB, 0:2 * L].rearrange("p (b m) -> p b m", b=2), AX, ALU.max,
                                  negate=True).then_inc(max_done, 1)

            def r1_step(n, k):
                dve.wait_ge(e1_done, SUB * n + k + 1)
                dve.reciprocal(rin1[k % NA][:], sum1[k % NA][:]).then_inc(r1_done, 1)

            def scale_step(n, k):
                dve.wait_ge(e2_done, SUB * n + k + 1)
                A.add(dve.reciprocal(rin2[k % NA][:], sum2[k % NA][:]))
                A.wait()
                for b in range(2):
                    part = p2[k % NA][:, LB * b:LB * b + LB * (b + 1)]
                    last = dve.tensor_scalar(part, part, rin2[k % NA][:, b:b + 1], None, ALU.mult)
                last.then_inc(p2_done, 1)

            def top2(X, dif_sem):
                alone(dve)
                for c in range(4):
                    last = dve.max(mx8[:, c, :], lg[:, c, 0:X])
                B.add(last)
                B.wait()
                dve.tensor_tensor(dif[:], mx8[:, :, 1], mx8[:, :, 0], ALU.subtract).then_inc(dif_sem, 1)
                for c in range(4):
                    last = dve.max_index(ix8[:, c, :], mx8[:, c, :], lg[:, c, 0:X])
                B.add(last)
                B.wait()
                B.add(dve.tensor_copy(ixf[:].rearrange("p (c o) -> p c o", o=2), ix8[:, :, 0:2]))
                B.wait()
                B.add(dve.tensor_tensor(onehot[:, :, 0:X], iota[0:LB, 0:X].unsqueeze(1).to_broadcast([LB, 8, X]),
                                        ixf[:].unsqueeze(2).to_broadcast([LB, 8, X]), ALU.is_equal))
                B.wait()

            def gate_weights():
                B.add(dve.tensor_scalar(eone[:], edif[:], 1.0, None, ALU.add))
                B.wait()
                B.add(dve.reciprocal(gates[:, :, 0], eone[:]))
                B.wait()
                B.add(dve.tensor_tensor(gates[:, :, 1], edif[:], gates[:, :, 0], ALU.mult))
                B.wait()

            def stage_b(n, j):
                X, Y = ps_b
                if j in (4, 28, 43):
                    r = {4: 0, 28: 1, 43: 2}[j]
                    if r == 0:
                        B.start(n)
                    dve.wait_ge(b_rbs, 3 * n + r + 1)
                    B.add(dve.tensor_tensor(xf_b[:], X[:, 0:2 * L], rs_b[:], ALU.mult))
                    B.wait()
                    B.add(dve.tensor_copy(xh_b[:], xf_b[:]))
                    B.wait()
                    dve.tensor_tensor(xl_b[:], xf_b[:], xh_b[:], ALU.subtract).then_inc(b_x, 1)
                if j == 6:
                    dve.wait_ge(g0_mm, n + 1)
                    B.add(dve.scalar_tensor_tensor(lg[:, :, 0:X0], X[0:LB, 0:4 * X0].rearrange("p (c x) -> p c x", x=X0),
                                                   1.0 / SC_0, bgb[:, 0:1, :].to_broadcast([LB, 4, X0]), ALU.mult, ALU.add))
                    B.wait()
                    top2(X0, g0_dif)
                if j == 8:
                    dve.wait_ge(g0_exp, n + 1)
                    gate_weights()
                    B.add(dve.tensor_tensor(weighed[:, :, 0:X0], onehot[:, :, 0:X0],
                                            gates[:].rearrange("p c o -> p (c o)").unsqueeze(2).to_broadcast([LB, 8, X0]), ALU.mult))
                    B.wait()
                    w = weighed[:].rearrange("p (c o) x -> p c o x", o=2)
                    dve.tensor_tensor(comb[:], w[:, :, 0, 0:X0], w[:, :, 1, 0:X0], ALU.add).then_inc(comb_done, 1)
                if 13 <= j < 13 + X0:
                    e = j - 13
                    dve.wait_ge(z_mm, X0 * n + e + 1)
                    if e == 0:
                        dve.wait_ge(comb_in, 16 * (n + 1))
                    if e >= 2:
                        dve.wait_ge(y_mm, X0 * n + e - 1)
                    dve.scalar_tensor_tensor(hid[e % 2][:], X[:, 0:2 * L], nb1[:, e:e + 1], combB[:, e, :], ALU.max, ALU.mult).then_inc(hid_done, 1)
                if j == 21:
                    dve.wait_ge(y_mm, X0 * n + X0)
                    dve.tensor_tensor(h_b[:], Y[:, 0:L], h_b[:], ALU.add).then_inc(h2_done, 1)
                if j == 30:
                    dve.wait_ge(q_hi, n + 1)
                    dve.tensor_tensor(q16[64:128], X[64:128, 0:2 * L], q16[64:128], ALU.subtract).then_inc(q_lo, 1)
                    for img in range(2):
                        sl = slice(64 * img, 64 * img + 64)
                        last = dve.reduce_sum(colsum[sl, 0:1], xf_b[sl, img * L:img * L + L], AX)
                    B.add(last)
                if j == 35:
                    B.wait()
                    dve.wait_ge(val_mm, n + 1)
                    B.add(dve.tensor_scalar(half[:], X[:, 0:L], colsum[:, 0:1], 0.5, ALU.add, ALU.mult))
                    B.wait()
                    dve.tensor_tensor(h_b[:], half[:], h_b[:], ALU.add).then_inc(h3_done, 1)
                if j == 45:
                    dve.wait_ge(g1_mm, n + 1)
                    B.add(dve.scalar_tensor_tensor(lg[:], Y[0:LB, 0:4 * X1].rearrange("p (c x) -> p c x", x=X1),
                                                   1.0 / SC_R, brb[:].unsqueeze(1).to_broadcast([LB, 4, X1]), ALU.mult, ALU.add))
                    B.wait()
                    top2(X1, g1_dif)
                    oh = onehot[:].rearrange("p (c o) x -> p c o x", o=2)
                    dve.tensor_tensor(chosen[:], oh[:, :, 0, :], oh[:, :, 1, :], ALU.add).then_inc(chosen_done, 1)
                if j == 47:
                    dve.wait_ge(g1_exp, n + 1)
                    gate_weights()
                    dve.wait_ge(h3T_sb, n + 1)
                    dve.tensor_copy(rows[:, :, E:E + 1], gates[:].rearrange("p c o -> p (c o)").unsqueeze(2))
                    B.add(dve.tensor_copy(rows[:, :, E + 1:E + 2], place[:].unsqueeze(2)))
                    B.wait()
                    B.add(dve.tensor_scalar(place[:], place[:], 4.0 * LB, None, ALU.add))
                    dve.wait_ge(rank_mm, n + 1)
                    B.add(dve.tensor_tensor(ranked[:], Y[0:LB, 0:4 * X1].rearrange("p (c x) -> p c x", x=X1),
                                            region[:].unsqueeze(1).to_broadcast([LB, 4, X1]), ALU.add))
                    B.wait()
                    B.add(dve.tensor_tensor(weighed[:].rearrange("p (c o) x -> p c o x", o=2), onehot[:].rearrange("p (c o) x -> p c o x", o=2),
                                            ranked[:].unsqueeze(2).to_broadcast([LB, 4, 2, X1]), ALU.mult))
                    B.wait()
                    B.add(dve.reduce_sum(posf[:], weighed[:], AX))
                    B.wait()
                    B.add(dve.tensor_copy(posi[:], posf[:]))
                    B.add(dve.reduce_sum(added[:], chosen[:].rearrange("p c x -> p x c"), AX))
                    B.wait()
                    B.add(dve.tensor_tensor(seen[:], seen[:], added[:], ALU.add))
                    B.wait()
                    dve.tensor_copy(seen16[:], seen[:]).then_inc(rows_done, 1)
                    B.end()

            def round_(n, a, nb):
                j = 0
                for step in range(4):
                    if a:
                        start_a(n, step)
                    if nb is not None:
                        stage_b(nb, j)
                        stage_b(nb, j + 1)
                    j += 2
                if a:
                    u_lo_step(n, 0)
                for k in range(SUB + 4):
                    if a:
                        if k < SUB:
                            max_step(n, k)
                        if 0 <= k - 1 < SUB:
                            r1_step(n, k - 1)
                        if 0 <= k - 2 < SUB:
                            scale_step(n, k - 2)
                        if k % 2 == 0 and k // 2 + 1 < HEADS:
                            u_lo_step(n, k // 2 + 1)
                    if nb is not None:
                        stage_b(nb, j)
                        stage_b(nb, j + 1)
                    j += 2
                if a:
                    A.end()
                    dve.wait_ge(pv_mm, SUB * (n + 1))
                    dve.tensor_tensor(h_b[:], ps_o[:, 0:L], h_a[:], ALU.add).then_inc(hb_ready, 1)

            round_(0, True, None)
            round_(1, True, 0)
            with dve.Fori(1, NPAIR - 1) as t:
                round_(t + 1, True, t)
            round_(NPAIR, False, NPAIR - 1)

            dve.wait_ge(cnt_mm, 1)
            own(dve.tensor_copy(cnt[:], ps_b[0][0:X1, 0:1]))
            own(dve.tensor_scalar(steps[:], iota[0:X1, 0:T // TILE + 1], float(TILE), None, ALU.mult))
            own(dve.tensor_scalar(less[:], steps[:], cnt[:, 0:1], None, ALU.is_lt))
            dve.reduce_sum(ntl[:], less[:], AX).then_inc(cum_in, 1)
            own(dve.tensor_tensor(fillf[:], ps_b[1][0:1, 0:X1], region[0:1, :], ALU.add))
            own(dve.tensor_copy(filli[:], fillf[:]))
            dve.wait_ge(cum_in, 1)
            own(dve.tensor_scalar(skip[:], ntl[:], -float(TILE), float(CAP), ALU.mult, ALU.add))
            dve.wait_ge(cum_mm, 1)
            own(dve.tensor_copy(cum[:], ps_u[0:X1, 0:1]))
            dve.tensor_scalar(past[:], iota[0:X1, :], cum[:, 0:1], None, ALU.is_ge).then_inc(past_in, 1)
            dve.wait_ge(meta_mm, 1)
            own(dve.scalar_tensor_tensor(metaf[:, 0, :], iota[0:1, :], float(TILE), ps_s[0][0:1, 0:NTILE], ALU.mult, ALU.add))
            own(dve.tensor_scalar(metaf[:, 0, :], metaf[:, 0, :], float(X1 * CAP), None, ALU.min))
            own(dve.tensor_scalar(metaf[:, 1, :], ps_s[1][0:1, 0:NTILE], float(X1 - 1), None, ALU.min))
            dve.tensor_copy(metai[:].rearrange("o g i k -> o k (g i)"), metaf[:]).then_inc(meta_done, 1)

            def x_out(t, i):
                dve.wait_ge(xT_mm, t + 1)
                if not (isinstance(t, int) and t < 2):
                    dve.wait_ge(zt_mm, t - 1)
                dve.tensor_copy(xT[i % 2][0:E], ps_s[i % 2][0:E, 0:TILE]).then_inc(xT_sb, 1)

            def y_rows(t, i):
                dve.wait_ge(yt_mm, t + 1)
                if not (isinstance(t, int) and t < NB2):
                    dve.wait_ge(y_out[i], (t - i) * (16 // NB2))
                dve.tensor_copy(dst[i][:], xr[i][:, E + 1:E + 2])
                dve.tensor_scalar(yo[i][:], [ps_u, ps_t][i % 2][:, 0:E], xr[i][:, E:E + 1], None, ALU.mult).then_inc(yo_done, 1)

            for t in range(2 * NB2):
                x_out(t, t % NB2)
                if t >= 2:
                    y_rows(t - 2, (t - 2) % NB2)
            with dve.Fori(2, NTILE // NB2) as g:
                t = g * NB2
                for i in range(NB2):
                    x_out(t + i, i)
                    y_rows(t + i - 2, (i - 2) % NB2)
            y_rows(NTILE - 2, NB2 - 2)
            y_rows(NTILE - 1, NB2 - 1)

            NS = NBLK // CB

            def finish(s, i, first):
                dve.wait_ge(y_in[i], 16 * (s - i) + 32)
                dve.tensor_tensor(ysum[i][:], yin[i][:, 0], yin[i][:, 1], ALU.add).then_inc(ys_done, 1)
                dve.wait_ge(ys_done, s + 1)
                if not first:
                    dve.wait_ge(fin_out[i], (s - i) * 8)
                src = hres[:, CB * s:CB * s + CB, :] if isinstance(s, int) else hres[:, bass.ds(CB * s, CB), :]
                dve.tensor_tensor(yfin[i][:], ysum[i][:], src, ALU.add).then_inc(fin_done, 1)

            finish(0, 0, True)
            finish(1, 1, True)
            with dve.Fori(0, NS // 2 - 1) as g:
                s = g * 2
                for i in range(2):
                    finish(s + 2 + i, i, False)


_ORDER = ["x", "tokW", "tokb", "Wq", "Wk", "Wv", "WoT", "Wg", "bg", "bias", "W1", "b1", "b1T", "W2", "b2",
          "qw", "Wr", "br", "E1W"]


def kernel(**inputs):
    import numpy as _np
    import concourse.bacc as _bacc
    from concourse import mybir as _mybir
    from concourse.bass_utils import run_bass_kernel_spmd as _run

    i = {k: _np.asarray(v) for k, v in inputs.items()}
    E, K = i["L0_tok_W"].shape
    CH = i["x"].shape[1]
    X, _, HID = i["L1_ffn_W1"].shape
    packed = _np.zeros((X, 128, HID + E), i["L1_ffn_W1"].dtype)
    packed[:, 0:E, 0:HID] = i["L1_ffn_W1"]
    packed[:, E, 0:HID] = i["L1_ffn_b1"]
    packed[:, B2ROW, 0:E] = i["L1_ffn_b2"]
    packed[:, :, HID:] = i["L1_ffn_W2"]
    laid = {
        "x": i["x"],
        "tokW": i["L0_tok_W"].reshape(E, CH * PATCH, PATCH).transpose(1, 2, 0),
        "tokb": i["L0_tok_b"], "Wq": i["L0_attn_Wq"], "Wk": i["L0_attn_Wk"], "Wv": i["L0_attn_Wv"],
        "WoT": i["L0_attn_Wo"].T, "Wg": i["L0_ffn_Wg"], "bg": i["L0_ffn_bg"], "bias": i["L0_ffn_bias"],
        "W1": i["L0_ffn_W1"], "b1": i["L0_ffn_b1"], "b1T": i["L0_ffn_b1"].T, "W2": i["L0_ffn_W2"], "b2": i["L0_ffn_b2"],
        "qw": i["L1_attn_q_weight"], "Wr": i["L1_ffn_Wr"], "br": i["L1_ffn_br"],
        "E1W": packed,
    }
    nc = _bacc.Bacc("TRN2", target_bir_lowering=False, num_devices=1)
    arrays, args = {}, []
    for name in _ORDER:
        a = _np.ascontiguousarray(laid[name])
        arrays[f"in_{name}"] = a
        args.append(nc.dram_tensor(f"in_{name}", a.shape, _mybir.dt.from_np(a.dtype), kind="ExternalInput").ap())
    n_img = i["x"].shape[0]
    tokens = (i["x"].shape[2] // PATCH) * (i["x"].shape[3] // PATCH)
    out = nc.dram_tensor("out_0", (n_img, tokens, E), F32, kind="ExternalOutput").ap()
    vit_tower(nc, *args, out)
    r = _run(nc, [arrays], core_ids=[0])
    return r.results[0]["out_0"]
```

```python
from contextlib import ExitStack

import concourse.bass as bass
from concourse import mybir

F32 = mybir.dt.float32
F16 = mybir.dt.float16
BF16 = mybir.dt.bfloat16
I32 = mybir.dt.int32
U32 = mybir.dt.uint32
ALU = mybir.AluOpType
ACT = mybir.ActivationFunctionType
AX = mybir.AxisListType.X

PATCH = 16
EPS = 1e-5
NEG = -1e30
B2ROW = 96


ORD_PE = "USVbTcEBPN"
ORD_ACT = "tuvbecxNB"
ORD_DVE = "rmswbuNcB"


class Chain:

    def __init__(self, eng, sem, per_round):
        self.eng, self.sem, self.per, self.n, self.done = eng, sem, per_round, 0, 0

    def start(self, n, done=0):
        self.n, self.done = n, done

    def add(self, instruction):
        instruction.then_inc(self.sem, 1)
        self.done += 1

    def wait(self):
        self.eng.wait_ge(self.sem, self.n * self.per + self.done)

    def end(self):
        assert self.done == self.per, (self.done, self.per)


def vit_tower(nc, x, tokW, tokb, Wq, Wk, Wv, WoT, Wg, bg, bias, W1, b1, b1T, W2, b2,
              qw, Wr, br, E1W, out):
    NIMG, CH, HH, WW = x.shape
    NH, NW = HH // PATCH, WW // PATCH
    L = NH * NW
    LB = L // 2
    NPAIR = NIMG // 2
    T = NIMG * L
    NBLK = T // LB
    E = tokb.shape[0]
    KR = CH * PATCH
    HEADS = Wq.shape[0] // E
    SUB = 2 * HEADS
    X0, HID = W1.shape[0], W1.shape[2]
    X1 = Wr.shape[1]
    TILE = 128
    CAP = (T // TILE + 2) * TILE
    NB2 = 8
    NTILE = -(-(2 * T // TILE + X1 - 1) // NB2) * NB2
    ROW = E + 2
    FAR = 2.0 ** 20
    SC_V, SC_0, SC_R = 64.0, 256.0, 16.0
    assert E == 64 and LB <= 128 and HID == 128 and L % 2 == 0 and 2 * T < FAR and X1 * CAP < 2 ** 24

    with ExitStack() as ctx:
        def sb(name, shape, dt=F32):
            return ctx.enter_context(nc.sbuf_tensor(name, shape, dt))

        def sem(name):
            return ctx.enter_context(nc.semaphore(name))

        def bank(name):
            return ctx.enter_context(nc.psum_tensor(name, [128, 512], F32))
        ps_s = [bank("ps_s0"), bank("ps_s1")]
        ps_u, ps_t, ps_o, ps_e = bank("ps_u"), bank("ps_t"), bank("ps_o"), bank("ps_e")
        ps_b = [bank("ps_b0"), bank("ps_b1")]

        rows_d = nc.dram_tensor("rows_scratch", (X1 * CAP + TILE, ROW), F32).ap()
        y_d = nc.dram_tensor("y_scratch", (2 * T, E), F32).ap()

        ident = sb("ident", [128, 128])
        center = [sb("center_a", [128, 128]), sb("center_b", [128, 128])]
        average = sb("average", [128, 128])
        before = sb("before", [128, 128], BF16)
        ones16 = sb("ones16", [128, 128], BF16)
        upto = sb("upto", [X1, X1])
        onesf = sb("onesf", [128, 8])
        power = sb("power", [128, 4])
        ident16 = sb("ident16", [LB, LB], F16)
        eps = sb("eps", [128, 1])
        iota_i = sb("iota_i", [128, NTILE], I32)
        iota = sb("iota", [128, NTILE])
        iota_p_i = sb("iota_p_i", [128, 1], I32)
        iota_p = sb("iota_p", [128, 1])
        region = sb("region", [LB, X1])
        place = sb("place", [LB, 8])
        tokw = sb("tokw", [128, PATCH, 128])
        tokbias = sb("tokbias", [128, 1])
        raw = sb("raw", [128, 2048])
        raw2 = sb("raw2", [128, 1024])
        g16 = sb("g16", [128, HEADS, 128], F16)
        v16 = sb("v16", [128, HEADS * E], F16)
        wg16 = sb("wg16", [128, X0], F16)
        w116 = sb("w116", [128, X0 * HID], F16)
        qw16 = sb("qw16", [128, 128], F16)
        wr16 = sb("wr16", [128, X1], F16)
        w2s = sb("w2s", [HID, X0, E])
        b1raw = sb("b1raw", [HID, X0])
        nb1 = sb("nb1", [HID, X0])
        b1diag = sb("b1diag", [HID, X0, 2 * X0])
        b2raw = sb("b2raw", [2 * X0, E])
        b2p = sb("b2p", [2 * X0, E])
        bgb = sb("bgb", [LB, 2, X0])
        brb = sb("brb", [LB, X1])
        tail = sb("tail", [TILE, ROW])

        xin = sb("xin", [128, NH, WW])
        NA = 4
        h_a = sb("h_a", [128, L])
        sq_a = sb("sq_a", [128, 2 * L])
        st_a = sb("st_a", [LB, 4])
        xf_a = sb("xf_a", [128, 2 * L])
        xh_a = sb("xh_a", [128, 2 * L], F16)
        xl_a = sb("xl_a", [128, 2 * L], F16)
        vt = sb("vt", [LB, 4, HEADS * E])
        us = [sb(f"us{i}", [128, 2 * L], F16) for i in range(2)]
        e1 = [sb(f"e1{i}", [LB, 2, L]) for i in range(NA)]
        nmax = [sb(f"nmax{i}", [LB, 2]) for i in range(NA)]
        sum1 = [sb(f"sum1{i}", [LB, 2]) for i in range(NA)]
        rin1 = [sb(f"rin1{i}", [LB, 2]) for i in range(NA)]
        sum2 = [sb(f"sum2{i}", [LB, 2]) for i in range(NA)]
        rin2 = [sb(f"rin2{i}", [LB, 2]) for i in range(NA)]
        p2 = [sb(f"p2{i}", [LB, 3 * LB]) for i in range(NA)]
        pt = [sb(f"pt{i}", [LB, 3 * LB]) for i in range(NA)]

        h_b = sb("h_b", [128, L])
        sq_b = sb("sq_b", [128, 2 * L])
        st_b = sb("st_b", [LB, 4])
        xf_b = sb("xf_b", [128, 2 * L])
        xh_b = sb("xh_b", [128, 2 * L], F16)
        xl_b = sb("xl_b", [128, 2 * L], F16)
        lg = sb("lg", [LB, 4, X1])
        mx8 = sb("mx8", [LB, 4, 8])
        ix8 = sb("ix8", [LB, 4, 8], U32)
        ixf = sb("ixf", [LB, 8])
        dif = sb("dif", [LB, 4])
        edif = sb("edif", [LB, 4])
        eone = sb("eone", [LB, 4])
        gates = sb("gates", [LB, 4, 2])
        onehot = sb("onehot", [LB, 8, X1])
        weighed = sb("weighed", [LB, 8, X1])
        comb = sb("comb", [LB, 4, X0])
        comb16 = sb("comb16", [LB, 4, 2 * X0], F16)
        combT = sb("combT", [2 * X0, 2 * L])
        combT16 = sb("combT16", [2 * X0, 2 * L], F16)
        pick = sb("pick", [2 * X0, X0, 128], F16)
        gate = [sb(f"gate{i}", [HID, 2 * L]) for i in range(2)]
        hid = [sb(f"hid{i}", [HID, 2 * L]) for i in range(2)]
        q16 = sb("q16", [128, 2 * L], F16)
        x3t = sb("x3t", [LB, 4, E])
        th = [sb(f"th{i}", [LB, 2 * L]) for i in range(2)]
        colsum = sb("colsum", [128, 1])
        half = sb("half", [128, L])
        hres = sb("hres", [LB, NBLK, E])
        rows = sb("rows", [LB, 8, ROW])
        chosen = sb("chosen", [LB, 4, X1], BF16)
        seen = sb("seen", [LB, X1])
        seen16 = sb("seen16", [LB, X1], BF16)
        added = sb("added", [LB, X1])
        ranked = sb("ranked", [LB, 4, X1])
        posf = sb("posf", [LB, 8])
        posi = sb("posi", [LB, 8], U32)

        cnt = sb("cnt", [X1, 1])
        steps = sb("steps", [X1, T // TILE + 1])
        less = sb("less", [X1, T // TILE + 1])
        ntl = sb("ntl", [X1, 1])
        cum = sb("cum", [X1, 1])
        past = sb("past", [X1, NTILE])
        skip = sb("skip", [X1, 1])
        fillf = sb("fillf", [1, X1])
        filli = sb("filli", [1, X1], I32)
        metaf = sb("metaf", [1, 2, NTILE])
        metai = sb("metai", [1, NTILE // NB2, NB2, 2], I32)

        xr = [sb(f"xr{i}", [TILE, ROW]) for i in range(NB2)]
        wt = [sb(f"wt{i}", [128, HID + E]) for i in range(NB2)]
        ones_row = sb("ones_row", [128, TILE])
        xT = [sb(f"xT{i}", [128, TILE]) for i in range(2)]
        hT = [sb(f"hT{i}", [HID, TILE]) for i in range(2)]
        yo = [sb(f"yo{i}", [TILE, E]) for i in range(NB2)]
        dst = [sb(f"dst{i}", [TILE, 1], U32) for i in range(NB2)]
        CB = 8
        yin = [sb(f"yin{i}", [LB, 2, CB, E]) for i in range(2)]
        ysum = [sb(f"ysum{i}", [LB, CB, E]) for i in range(2)]
        yfin = [sb(f"yfin{i}", [LB, CB, E]) for i in range(2)]

        w_qk, w_vo, w_rest, w_emb, w_misc = sem("w_qk"), sem("w_vo"), sem("w_rest"), sem("w_emb"), sem("w_misc")
        zeroed, consts, pool_c, emb_zero = sem("zeroed"), sem("consts"), sem("pool_c"), sem("emb_zero")
        g_mm, g_hi, g_lo, prep = sem("g_mm"), sem("g_hi"), sem("g_lo"), sem("prep")
        raw_free, bias_mm = sem("raw_free"), sem("bias_mm")
        x_in, emb_done, h_ready, hb_ready = sem("x_in"), sem("emb_done"), sem("h_ready"), sem("hb_ready")
        a_vs, a_rs, b_vs, b_rs = sem("a_vs"), sem("a_rs"), sem("b_vs"), sem("b_rs")
        a_rb, a_cs, b_rb, b_cs = sem("a_rb"), sem("a_cs"), sem("b_rb"), sem("b_cs")
        a_cen, a_sq, a_var, a_x, a_self = sem("a_cen"), sem("a_sq"), sem("a_var"), sem("a_x"), sem("a_self")
        v_mm, v_evac, u_mm, u_hi, u_lo = sem("v_mm"), sem("v_evac"), sem("u_mm"), sem("u_hi"), sem("u_lo")
        s_mm, max_done, e1_done, mask_done, r1_done = sem("s_mm"), sem("max_done"), sem("e1_done"), sem("mask_done"), sem("r1_done")
        e2_done, p2_done, t_mm, t_evac, pv_mm = sem("e2_done"), sem("p2_done"), sem("t_mm"), sem("t_evac"), sem("pv_mm")
        b_cen, b_sq, b_var, b_x, b_self = sem("b_cen"), sem("b_sq"), sem("b_var"), sem("b_x"), sem("b_self")
        g0_mm, g0_dif, g0_exp, comb_done, cT_mm, cT_sb, gate_mm, gate_sb = sem("g0_mm"), sem("g0_dif"), sem("g0_exp"), sem("comb_done"), sem("cT_mm"), sem("cT_sb"), sem("gate_mm"), sem("gate_sb")
        z_mm, hid_done, y_mm, h2_done = sem("z_mm"), sem("hid_done"), sem("y_mm"), sem("h2_done")
        q_mm, q_hi, q_lo, x3_mm, x3_sb, s3_mm, th_done = sem("q_mm"), sem("q_hi"), sem("q_lo"), sem("x3_mm"), sem("x3_sb"), sem("s3_mm"), sem("th_done")
        val_mm, h3_done, h3T_mm, h3T_sb, g1_mm, g1_dif, g1_exp = sem("val_mm"), sem("h3_done"), sem("h3T_mm"), sem("h3T_sb"), sem("g1_mm"), sem("g1_dif"), sem("g1_exp")
        chosen_done, rank_mm, ranked_done, rows_done, rows_out = sem("chosen_done"), sem("rank_mm"), sem("ranked_done"), sem("rows_done"), sem("rows_out")
        cnt_mm, cum_in, cum_mm, past_in, meta_mm, meta_done, fill_known, fill_out, d_self = sem("cnt_mm"), sem("cum_in"), sem("cum_mm"), sem("past_in"), sem("meta_mm"), sem("meta_done"), sem("fill_known"), sem("fill_out"), sem("d_self")
        x_tile = [sem(f"x_tile{i}") for i in range(NB2)]
        xT_mm, xT_sb, zt_mm, hT_sb, yt_mm, yo_done = sem("xT_mm"), sem("xT_sb"), sem("zt_mm"), sem("hT_sb"), sem("yt_mm"), sem("yo_done")
        y_out = [sem(f"y_out{i}") for i in range(NB2)]
        y_in = [sem(f"y_in{i}") for i in range(2)]
        ys_done, fin_done = sem("ys_done"), sem("fin_done")
        fin_out = [sem(f"fin_out{i}") for i in range(2)]

        passed = {e: sem(f"passed_{n}") for e, n in ((mybir.EngineType.SP, "sp"), (mybir.EngineType.Pool, "pool"),
                                                     (mybir.EngineType.PE, "pe"), (mybir.EngineType.DVE, "dve"), (mybir.EngineType.Activation, "act"))}
        A_LINKS, B_LINKS = 2 + SUB, 34
        PARTS = [(0, 1), (3, 4), (5, 6, 7), (8, 9, 10), (12, 13), (14, 15), (16, 17), (18, 19),
                 (20, 21, 22), (23, 24, 25), (26, 27), (28, 29), (30, 31, 32), (33, 34), (35, 36, 37), (38, 39), (41, 42, 43), (44, 45), (46,), (47,)]
        assert len(PARTS) == SUB + 4
        PREP = 11
        CONSTS = 19
        block = ctx.enter_context(nc.Block())

        def alone(eng):
            eng.sem_inc(passed[eng.engine], 1)

        def fill(eng, side):
            FG = 16
            with eng.Fori(side * X1 // (2 * FG), (side + 1) * X1 // (2 * FG)) as e:
                alone(eng)
                _, ends = nc.values_load_multi_w_load_instructions(filli[0:1, bass.ds(e * FG, FG)], engines=[eng.engine],
                                                                   min_val=0, max_val=X1 * CAP - TILE,
                                                                   skip_runtime_bounds_check_because="an expert has at most T rows, below CAP - TILE")
                for i in range(FG):
                    eng.dma_start(rows_d[bass.ds(ends[i], TILE)], tail[:]).then_inc(fill_out, 16)

        def x_rows(img):
            return x[img:img + 1] if isinstance(img, int) else x[bass.ds(img, 1)]

        @block.sync
        def _(sp):
            def load_images(n):
                for img in range(2):
                    for c in range(CH):
                        src = x_rows(2 * n + img)[:, c].rearrange("o (a p) w -> p (o a) w", p=PATCH)
                        r = 64 * img + c * PATCH
                        sp.dma_start(xin[r:r + PATCH], src).then_inc(x_in, 16)

            sp.wait_ge(zeroed, 1)
            load_images(0)
            sp.wait_ge(emb_zero, 1)
            for r in range(2):
                sp.dma_start(tokw[64 * r:64 * r + KR, :, 64 * r:64 * r + E], tokW).then_inc(w_emb, 16)
                sp.dma_start(tokbias[64 * r:64 * r + E], tokb.rearrange("(e o) -> e o", o=1)).then_inc(w_emb, 16)
            for r in range(2):
                sp.dma_start(raw[0:E, 0:1024].rearrange("d (h i) -> d h i", h=HEADS)[:, :, 64 * r:64 * r + E],
                             Wq.rearrange("(h d) i -> d h i", d=E)).then_inc(w_qk, 16)
                sp.dma_start(raw[0:E, 1024:2048].rearrange("d (h i) -> d h i", h=HEADS)[:, :, 64 * r:64 * r + E],
                             Wk.rearrange("(h d) i -> d h i", d=E)).then_inc(w_qk, 16)
            for r in range(2):
                lo, hi = 64 * r, 64 * r + E
                sp.dma_start(raw2[lo:hi, 0:X0], Wg).then_inc(w_misc, 16)
                sp.dma_start(raw2[lo:hi, X0:X0 + X1], Wr).then_inc(w_misc, 16)
                for c in range(2):
                    sp.dma_start(raw2[lo:hi, 128 + E * c:128 + E * (c + 1)], qw).then_inc(w_misc, 16)
            sp.dma_start(b1raw[:], b1T).then_inc(w_misc, 16)
            for r in range(2):
                sp.dma_start(b2raw[X0 * r:X0 * r + X0], b2).then_inc(w_misc, 16)
            sp.dma_start(w2s[:], W2.rearrange("x h e -> h x e")).then_inc(w_misc, 16)
            sp.dma_start(bgb[:, 0, :], bg.partition_broadcast(LB)).then_inc(w_misc, 16)
            sp.dma_start(bgb[:, 1, :], bias.partition_broadcast(LB)).then_inc(w_misc, 16)
            sp.dma_start(brb[:], br.partition_broadcast(LB)).then_inc(w_misc, 16)
            sp.wait_ge(g_mm, 2)
            for r in range(2):
                sp.dma_start(raw[0:E, 0:1024].rearrange("d (h i) -> d h i", h=HEADS)[:, :, 64 * r:64 * r + E],
                             Wv.rearrange("(h d) i -> d h i", d=E)).then_inc(w_vo, 16)
            sp.dma_start(raw[0:E, 1024:1024 + HEADS * E].rearrange("d (h e) -> d h e", h=HEADS),
                         WoT.rearrange("(h d) e -> d h e", d=E)).then_inc(w_vo, 16)
            sp.wait_ge(g_mm, 3)
            for r in range(2):
                sp.dma_start(raw[64 * r:64 * r + E, 0:X0 * HID].rearrange("d (x h) -> d x h", x=X0),
                             W1.rearrange("x d h -> d x h")).then_inc(w_rest, 16)

            def sp_stage_a(n):
                sp.wait_ge(emb_done, n + 2)
                load_images(n + 2)

            sp.wait_ge(emb_done, 1)
            load_images(1)
            sp_stage_a(0)
            sp_stage_a(1)
            with sp.Fori(1, NPAIR - 3) as t:
                sp_stage_a(t + 1)

            sp.wait_ge(fill_known, 1)
            sp.dma_start(rows_d[X1 * CAP:X1 * CAP + TILE], tail[:]).then_inc(fill_out, 16)
            fill(sp, 0)
            sp.wait_ge(rows_out, 16 * 8 * NPAIR)
            sp.wait_ge(fill_out, 16 * (X1 + 1))
            sp.wait_ge(meta_done, 1)

            def load_tiles(g, reuse):
                src = metai[0:1, g] if isinstance(g, int) else metai[0:1, bass.ds(g, 1)].rearrange("o g i k -> o (g i) k")
                alone(sp)
                _, at = nc.values_load_multi_w_load_instructions(src.rearrange("o i k -> o (i k)"), engines=[mybir.EngineType.SP],
                                                                 min_val=0, max_val=X1 * CAP,
                                                                 skip_runtime_bounds_check_because="metai is clamped")
                for i in range(NB2):
                    if reuse:
                        sp.wait_ge(yo_done, g * NB2 + i - (NB2 - 1))
                        alone(sp)
                    row, ex = at[2 * i], nc.s_assert_within(at[2 * i + 1], 0, X1 - 1, skip_runtime_bounds_check_because="metai's experts are clamped to X1 - 1")
                    sp.dma_start(xr[i][:], rows_d[bass.ds(row, TILE)]).then_inc(x_tile[i], 16)
                    sp.dma_start(wt[i][:], E1W[bass.ds(ex, 1)].rearrange("o d h -> (o d) h")).then_inc(x_tile[i], 16)

            load_tiles(0, False)
            with sp.Fori(1, NTILE // NB2) as g:
                load_tiles(g, True)

            for i in range(NB2):
                sp.wait_ge(y_out[i], 16 * (NTILE // NB2))

            def load_y(s, i, reuse):
                if reuse:
                    sp.wait_ge(ys_done, s - 1)
                for c in range(2):
                    src = y_d[bass.ds(T * c + s * (CB * LB), CB * LB)].rearrange("(b p q) e -> p b (q e)", p=LB, q=4)
                    sp.dma_start(yin[i][:, c].rearrange("p (b q) e -> p b (q e)", q=4), src).then_inc(y_in[i], 16)

            load_y(0, 0, False)
            load_y(1, 1, False)
            out_rows = out.rearrange("i t e -> (i t) e")

            def store(s, i):
                sp.wait_ge(fin_done, s + 1)
                sp.dma_start(out_rows[bass.ds(s * (CB * LB), CB * LB)].rearrange("(b p) e -> p b e", p=LB),
                             yfin[i][:]).then_inc(fin_out[i], 16)

            NS = NBLK // CB
            with sp.Fori(0, NS // 2 - 1) as g:
                s = g * 2
                for i in range(2):
                    load_y(s + 2 + i, i, True)
                    store(s + i, i)
            for i in range(2):
                store(NS - 2 + i, i)
            for i in range(2):
                sp.wait_ge(fin_out[i], 16 * (NS // 2))

        @block.gpsimd
        def _(pool):
            pool.memset(xin[:], 0.0).then_inc(zeroed, 1)
            pool.memset(tokw[:], 0.0).then_inc(emb_zero, 1)
            made = [0]

            def own(ins):
                ins.then_inc(pool_c, 1)
                made[0] += 1
                pool.wait_ge(pool_c, made[0])

            def diagonal(m, fill, base=0):
                n = m.shape[1]
                return pool.affine_select(out=m, in_=m, compare_op=ALU.not_equal, fill=fill, base=base,
                                          pattern=[[-1, n]], channel_multiplier=1)

            own(pool.memset(ident[:], 0.0))
            diagonal(ident[:], 1.0).then_inc(consts, 1)
            for img in range(2):
                own(pool.memset(center[img][:], 0.0))
                own(pool.memset(center[img][64 * img:64 * img + 64], -1.0 / E))
                for c in range(2):
                    part = center[img][64 * img:64 * img + 64, 64 * c:64 * c + 64]
                    diagonal(part, 1.0 - 1.0 / E).then_inc(consts, 1)
                    pool.wait_ge(consts, 2 + 2 * img + c)
            pool.memset(average[:], 0.5 / E).then_inc(consts, 1)
            own(pool.memset(before[:], 1.0))
            pool.affine_select(out=before[:], in_=before[:], compare_op=ALU.is_gt, fill=0.0, base=0,
                               pattern=[[1, 128]], channel_multiplier=-1).then_inc(consts, 1)
            pool.memset(ones16[:], 1.0).then_inc(consts, 1)
            own(pool.memset(upto[:], 1.0))
            pool.affine_select(out=upto[:], in_=upto[:], compare_op=ALU.is_ge, fill=0.0, base=0,
                               pattern=[[1, X1]], channel_multiplier=-1).then_inc(consts, 1)
            pool.memset(onesf[:], 1.0).then_inc(consts, 1)
            pool.memset(ones_row[:], 1.0).then_inc(consts, 1)
            pool.memset(power[:], -0.5).then_inc(consts, 1)
            pool.memset(eps[:], EPS).then_inc(consts, 1)
            own(pool.memset(ident16[:], 0.0))
            diagonal(ident16[:], 1.0).then_inc(consts, 1)
            own(pool.memset(pick[:], 0.0))
            own(pool.affine_select(out=pick[:], in_=pick[:], compare_op=ALU.not_equal, fill=1.0, base=0,
                                   pattern=[[-1, X0], [0, 128]], channel_multiplier=1))
            pool.affine_select(out=pick[:], in_=pick[:], compare_op=ALU.not_equal, fill=1.0, base=-X0,
                               pattern=[[-1, X0], [0, 128]], channel_multiplier=1).then_inc(consts, 1)
            pool.iota(iota_i[:], pattern=[[1, NTILE]], base=0, channel_multiplier=0).then_inc(consts, 1)
            pool.iota(iota_p_i[:], pattern=[[0, 1]], base=0, channel_multiplier=1).then_inc(consts, 1)
            own(pool.memset(tail[:], 0.0))
            pool.memset(tail[:, E + 1:E + 2], FAR).then_inc(consts, 1)
            pool.memset(seen[:], 0.0).then_inc(consts, 1)
            pool.memset(seen16[:], 0.0).then_inc(consts, 1)

            def pool_stage_a(n, k):
                pool.wait_ge(e1_done, SUB * n + k + 1)
                alone(pool)
                view = e1[k % NA][:].rearrange("p b m -> p (b m)")
                diag = bass.AP(view.tensor, view.offset, [list(view.ap[0]), [3 * LB, 2], [1, LB]])
                pool.affine_select(out=diag, in_=diag, compare_op=ALU.is_ge, fill=NEG, base=0,
                                   pattern=[[0, 2], [-1, LB]], channel_multiplier=1).then_inc(mask_done, 1)

            def scatter(n, c):
                if c == 0:
                    pool.wait_ge(rows_done, n + 1)
                    alone(pool)
                pool.indirect_dma_start(out=rows_d, out_offset=bass.IndirectOffsetOnAxis(ap=posi[:, c:c + 1], axis=0),
                                        in_=rows[:, c, :], in_offset=None).then_inc(rows_out, 16)

            pool.wait_ge(consts, CONSTS)

            def rstd(st, done):
                pool.tensor_tensor(st[:], st[:], power[0:LB], ALU.pow).then_inc(done, 1)

            def rstd_a(n):
                pool.wait_ge(a_vs, n + 1)
                rstd(st_a, a_rs)

            def rstd_b(n, r):
                pool.wait_ge(b_vs, 3 * n + r + 1)
                rstd(st_b, b_rs)

            def round_(n, a, nb, nr, nxt):
                for k in range(SUB + 4):
                    if a and k < SUB:
                        pool_stage_a(n, k)
                    if nb is not None and k in (0, 9, 15):
                        rstd_b(nb, (0, 9, 15).index(k))
                    if nr is not None and 2 <= k <= 9:
                        scatter(nr, k - 2)
                    if nxt and k == SUB + 1:
                        rstd_a(n + 1)

            rstd_a(0)
            round_(0, True, None, None, True)
            round_(1, True, 0, None, True)
            with pool.Fori(1, NPAIR - 2) as t:
                round_(t + 1, True, t, t - 1, True)
            round_(NPAIR - 1, True, NPAIR - 2, NPAIR - 3, False)
            round_(NPAIR, False, NPAIR - 1, NPAIR - 2, False)
            for c in range(8):
                scatter(NPAIR - 1, c)

            def send(t, i):
                pool.wait_ge(yo_done, t + 1)
                alone(pool)
                pool.indirect_dma_start(out=y_d, out_offset=bass.IndirectOffsetOnAxis(ap=dst[i][:, 0:1], axis=0),
                                        in_=yo[i][:], in_offset=None, bounds_check=2 * T - 1, oob_is_err=False).then_inc(y_out[i], 16)

            with pool.Fori(0, NTILE // NB2) as g:
                t = g * NB2
                for i in range(NB2):
                    send(t + i, i)

        @block.tensor
        def _(pe):
            mm = pe.matmul

            pe.wait_ge(w_qk, 64)
            wq = raw[0:E, 0:1024].rearrange("d (h i) -> d h i", h=HEADS)
            wk = raw[0:E, 1024:2048].rearrange("d (h i) -> d h i", h=HEADS)
            for h in range(HEADS):
                last = mm(ps_s[h // 4][:, 128 * (h % 4):128 * (h % 4) + 128], wq[:, h], wk[:, h], start=True, stop=True)
                if h % 4 == 3:
                    last.then_inc(g_mm, 1)
            pe.wait_ge(w_vo, 48)
            wo = raw[0:E, 1024:1024 + HEADS * E].rearrange("d (h e) -> d h e", h=HEADS)
            for h in range(HEADS):
                last = mm(ps_u[:, E * h:E * h + E], wq[:, h], wo[:, h], start=True, stop=True)
            last.then_inc(g_mm, 1)
            pe.wait_ge(prep, 3)
            for e in range(X0):
                last = mm(ps_t[0:2 * X0, 0:E], b1diag[:, e, :], w2s[:, e, :], start=e == 0, stop=e == X0 - 1)
            last.then_inc(bias_mm, 1)
            pe.wait_ge(consts, CONSTS)
            pe.wait_ge(w_emb, 64)
            pe.wait_ge(prep, PREP)
            pe.wait_ge(g_lo, 3)

            def embed(n, part):
                if part == 0:
                    pe.wait_ge(x_in, 16 * 2 * CH * (n + 1))
                    if not (isinstance(n, int) and n == 0):
                        pe.wait_ge(h_ready, n)
                    if not (isinstance(n, int) and n < 2):
                        pe.wait_ge(gate_sb, X0 * (n - 1))
                for px in range(2 * part, 2 * part + 2):
                    last = mm(ps_e[:, 0:L], tokw[0:64 + KR, px, :],
                              xin[0:64 + KR].rearrange("p a (b q) -> p a b q", q=PATCH)[:, :, :, px],
                              start=px == 0, stop=px == PATCH - 1)
                if part == 7:
                    last.then_inc(emb_done, 1)

            def centered(dest, h):
                mm(dest[:, 0:L], center[0][:], h, start=True, stop=True)
                return mm(dest[:, L:2 * L], center[1][:], h, start=True, stop=True)

            def variances(dest, sq):
                for c in range(4):
                    last = mm(dest[0:LB, c:c + 1], sq[:, LB * c:LB * c + LB], average[:, 0:1], start=True, stop=True)
                return last

            def spread(dest, st):
                for c in range(4):
                    last = mm(dest[:, LB * c:LB * c + LB], st[:, c:c + 1].to_broadcast([LB, 128]), ident[0:LB, 0:LB],
                              start=True, stop=True)
                return last

            def start_a(n, step):
                if step == 0:
                    pe.wait_ge(h_ready, n + 1)
                    if not (isinstance(n, int) and n == 0):
                        pe.wait_ge(e1_done, SUB * n)
                    else:
                        pe.wait_ge(g_lo, 3)
                    centered(ps_s[0], h_a[:]).then_inc(a_cen, 1)
                if step == 1:
                    pe.wait_ge(a_sq, n + 1)
                    variances(ps_s[1], sq_a).then_inc(a_var, 1)
                if step == 2:
                    pe.wait_ge(a_rs, n + 1)
                    spread(ps_s[1], st_a).then_inc(a_rb, 1)
                if step == 3:
                    u_step(n, 0)
                    v_step(n, 0)
                    s_step(n, 0)

            def v_step(n, c):
                if c == 0:
                    pe.wait_ge(t_evac, SUB * n) if not (isinstance(n, int) and n == 0) else None
                else:
                    pe.wait_ge(v_evac, 4 * n + c)
                mm(ps_t[0:LB, :], xh_a[:, LB * c:LB * c + LB], v16[:], start=True, stop=False)
                mm(ps_t[0:LB, :], xl_a[:, LB * c:LB * c + LB], v16[:], start=False, stop=True).then_inc(v_mm, 1)

            def u_step(n, h):
                if h == 0:
                    pe.wait_ge(a_x, n + 1)
                if not (isinstance(n, int) and n == 0 and h == 0):
                    pe.wait_ge(u_lo, HEADS * n + h)
                mm(ps_u[:, 0:2 * L], g16[:, h, :], xh_a[:], start=True, stop=False)
                mm(ps_u[:, 0:2 * L], g16[:, h, :], xl_a[:], start=False, stop=True).then_inc(u_mm, 1)

            def s_step(n, k):
                h, img = k // 2, k % 2
                pe.wait_ge(u_lo, HEADS * n + h + 1)
                if k >= 2:
                    pe.wait_ge(e1_done, SUB * n + k - 1)
                u, sl = us[h % 2], slice(img * L, img * L + L)
                for b in range(2):
                    uu = u[:, img * L + LB * b:img * L + LB * b + LB]
                    mm(ps_s[k % 2][0:LB, L * b:L * b + L], uu, xh_a[:, sl], start=True, stop=False)
                    last = mm(ps_s[k % 2][0:LB, L * b:L * b + L], uu, xl_a[:, sl], start=False, stop=True)
                last.then_inc(s_mm, 1)

            def t_step(n, k):
                pe.wait_ge(p2_done, SUB * n + k + 1)
                if k == 0:
                    pe.wait_ge(v_evac, 4 * n + 4)
                else:
                    pe.wait_ge(t_evac, SUB * n + k)
                for c in range(3):
                    last = pe.transpose(ps_t[0:LB, LB * c:LB * c + LB], p2[k % NA][:, LB * c:LB * c + LB], ident[0:LB, 0:LB])
                last.then_inc(t_mm, 1)

            def pv_step(n, k):
                h, img = k // 2, k % 2
                pe.wait_ge(t_evac, SUB * n + k + 1)
                if k == 0:
                    if not (isinstance(n, int) and n == 0):
                        pe.wait_ge(hb_ready, n)
                    mm(ps_o[:, 0:L], ident[:], h_a[:], start=True, stop=False, skip_group_check=True)
                o = ps_o[64 * img:64 * img + E]
                mm(o[:, 0:L], vt[:, 2 * img, E * h:E * h + E], pt[k % NA][:, 0:L], start=False, stop=False,
                   skip_group_check=True)
                mm(o[:, LB:L], vt[:, 2 * img + 1, E * h:E * h + E], pt[k % NA][:, L:L + LB], start=False,
                   stop=h == HEADS - 1, skip_group_check=True).then_inc(pv_mm, 1)

            def stage_b(n, j):
                X, Y = ps_b
                if j in (0, 22, 36):
                    r = {0: 0, 22: 1, 36: 2}[j]
                    if r == 0:
                        pe.wait_ge(hb_ready, n + 1)
                        if not (isinstance(n, int) and n == 0):
                            pe.wait_ge(h3T_sb, n)
                    elif r == 1:
                        pe.wait_ge(h2_done, n + 1)
                    else:
                        pe.wait_ge(h3_done, n + 1)
                    centered(X, h_b[:]).then_inc(b_cen, 1)
                if j in (1, 24, 38):
                    r = {1: 0, 24: 1, 38: 2}[j]
                    pe.wait_ge(b_sq, 3 * n + r + 1)
                    if r == 0 and not (isinstance(n, int) and n == 0):
                        pe.wait_ge(ranked_done, n)
                    variances(Y, sq_b).then_inc(b_var, 1)
                if j in (3, 26, 41):
                    pe.wait_ge(b_rs, 3 * n + {3: 0, 26: 1, 41: 2}[j] + 1)
                    spread(Y, st_b).then_inc(b_rb, 1)
                if j == 5:
                    pe.wait_ge(b_x, 3 * n + 1)
                    for c in range(4):
                        mm(X[0:LB, X0 * c:X0 * c + X0], xh_b[:, LB * c:LB * c + LB], wg16[:], start=True, stop=False)
                        last = mm(X[0:LB, X0 * c:X0 * c + X0], xl_b[:, LB * c:LB * c + LB], wg16[:], start=False, stop=True)
                    last.then_inc(g0_mm, 1)
                if j == 9:
                    pe.wait_ge(comb_done, n + 1)
                    for c in range(4):
                        last = mm(Y[0:2 * X0, LB * c:LB * c + LB], comb16[:, c, :], ident16[:], start=True, stop=True)
                    last.then_inc(cT_mm, 1)
                if j == 12:
                    pe.wait_ge(cT_sb, n + 1)
                    for img in range(2):
                        mm(Y[64 * img:64 * img + E, 0:L], b2p[:], combT[:, img * L:img * L + L], start=True, stop=False,
                           skip_group_check=True)
                if 12 <= j < 12 + X0:
                    e = j - 12
                    pe.wait_ge(cT_sb, n + 1)
                    if e >= 1:
                        pe.wait_ge(gate_sb, X0 * n + e)
                    mm(ps_e[:, 0:2 * L], pick[:, e, :], combT16[:], start=True, stop=True).then_inc(gate_mm, 1)
                if 13 <= j <= 13 + X0:
                    e = j - 13
                    if e >= 1:
                        pe.wait_ge(hid_done, X0 * n + e)
                        for img in range(2):
                            last = mm(Y[64 * img:64 * img + E, 0:L], w2s[:, e - 1, :], hid[(e - 1) % 2][:, img * L:img * L + L],
                                      start=False, stop=e == X0, skip_group_check=True)
                        last.then_inc(y_mm, 1)
                    if e < X0:
                        mm(X[:, 0:2 * L], w116[:, HID * e:HID * e + HID], xh_b[:], start=True, stop=False)
                        mm(X[:, 0:2 * L], w116[:, HID * e:HID * e + HID], xl_b[:], start=False, stop=True).then_inc(z_mm, 1)
                if j == 29:
                    pe.wait_ge(b_x, 3 * n + 2)
                    mm(X[:, 0:2 * L], qw16[:], xh_b[:], start=True, stop=False)
                    mm(X[:, 0:2 * L], qw16[:], xl_b[:], start=False, stop=True).then_inc(q_mm, 1)
                    for c in range(4):
                        last = pe.transpose(Y[0:LB, E * c:E * c + E], xf_b[0:E, LB * c:LB * c + LB], ident[0:E, 0:E])
                    last.then_inc(x3_mm, 1)
                if j in (31, 32):
                    img = j - 31
                    pe.wait_ge(q_lo, n + 1)
                    pe.wait_ge(x3_sb, n + 1)
                    for c in range(2):
                        s = slice(img * L + LB * c, img * L + LB * c + LB)
                        mm(ps_b[img][0:LB, L * c:L * c + L], xh_b[:, s], q16[:, img * L:img * L + L], start=True, stop=False)
                        last = mm(ps_b[img][0:LB, L * c:L * c + L], xl_b[:, s], q16[:, img * L:img * L + L], start=False, stop=True)
                    last.then_inc(s3_mm, 1)
                if j == 34:
                    pe.wait_ge(th_done, 2 * n + 2)
                    for img in range(2):
                        for c in range(2):
                            last = mm(X[64 * img:64 * img + E, 0:L], x3t[:, 2 * img + c, :], th[img][:, L * c:L * c + L],
                                      start=c == 0, stop=c == 1)
                    last.then_inc(val_mm, 1)
                if j == 44:
                    pe.wait_ge(b_x, 3 * n + 3)
                    alone(pe)
                    for c in range(4):
                        pe.transpose(X[0:LB, 256 + E * c:256 + E * c + E], xf_b[0:E, LB * c:LB * c + LB], ident[0:E, 0:E])
                    for b in range(2):
                        last = pe.transpose(X[0:LB, 128 * b:128 * b + 128], h_b[:, LB * b:LB * b + LB], ident[:])
                    last.then_inc(h3T_mm, 1)
                    for c in range(4):
                        mm(Y[0:LB, X1 * c:X1 * c + X1], xh_b[:, LB * c:LB * c + LB], wr16[:], start=True, stop=False)
                        last = mm(Y[0:LB, X1 * c:X1 * c + X1], xl_b[:, LB * c:LB * c + LB], wr16[:], start=False, stop=True)
                    last.then_inc(g1_mm, 1)
                if j == 46:
                    pe.wait_ge(chosen_done, n + 1)
                    if not (isinstance(n, int) and n == 0):
                        pe.wait_ge(rows_done, n)
                    for c in range(4):
                        o = Y[0:LB, X1 * c:X1 * c + X1]
                        mm(o, ones16[0:LB, 0:LB], seen16[:], start=True, stop=False)
                        for d in range(c):
                            mm(o, ones16[0:LB, 0:LB], chosen[:, d, :], start=False, stop=False)
                        last = mm(o, before[0:LB, 0:LB], chosen[:, c, :], start=False, stop=True)
                    last.then_inc(rank_mm, 1)

            def round_(n, a, nb, e):
                for k, js in enumerate(PARTS):
                    for op in ORD_PE:
                        if op == "S" and a and k + 1 < SUB:
                            s_step(n, k + 1)
                        if op == "U" and a and k == 0:
                            u_step(n, 1)
                        if op == "U" and a and k % 2 and (k + 3) // 2 < HEADS:
                            u_step(n, (k + 3) // 2)
                        if op == "V" and a and k < 3:
                            v_step(n, k + 1)
                        if op == "b" and nb is not None:
                            stage_b(nb, js[0])
                        if op == "T" and a and 0 <= k - 3 < SUB:
                            t_step(n, k - 3)
                        if op == "E" and e is not None and 9 <= k < SUB:
                            for part in ((k - 9,) if k < SUB - 1 else (6, 7)):
                                embed(e, part)
                        if op == "c" and nb is not None and len(js) > 1:
                            stage_b(nb, js[1])
                        if op == "B" and nb is not None and len(js) > 2:
                            stage_b(nb, js[2])
                        if op == "P" and a and 0 <= k - 4 < SUB:
                            pv_step(n, k - 4)
                        if op == "N" and e is not None and k >= SUB:
                            start_a(n + 1, k - SUB)

            for part in range(8):
                embed(0, part)
            for step in range(4):
                start_a(0, step)
            round_(0, True, None, 1)
            round_(1, True, 0, 2)
            with pe.Fori(1, NPAIR - 2) as t:
                round_(t + 1, True, t, t + 2)
            round_(NPAIR - 1, True, NPAIR - 2, None)
            round_(NPAIR, False, NPAIR - 1, None)

            pe.wait_ge(rows_done, NPAIR)
            mm(ps_b[0][0:X1, 0:LB], seen16[:], ones16[0:LB, 0:LB], start=True, stop=True)
            mm(ps_b[1][0:1, 0:X1], ones16[0:LB, 0:1], seen16[:], start=True, stop=True).then_inc(cnt_mm, 1)
            pe.wait_ge(cum_in, 1)
            mm(ps_u[0:X1, 0:1], upto[:], ntl[:], start=True, stop=True).then_inc(cum_mm, 1)
            pe.wait_ge(past_in, 1)
            mm(ps_s[0][0:1, 0:NTILE], skip[:], past[:], start=True, stop=True)
            mm(ps_s[1][0:1, 0:NTILE], onesf[0:X1, 0:1], past[:], start=True, stop=True).then_inc(meta_mm, 1)
            pe.wait_ge(meta_done, 1)

            def x_step(t, i):
                pe.wait_ge(x_tile[i % NB2], 32 * ((t - i) // NB2 + 1) if isinstance(t, int) else (t - i) * (32 // NB2) + 32)
                if not (isinstance(t, int) and t < 2):
                    pe.wait_ge(xT_sb, t - 1)
                alone(pe)
                pe.transpose(ps_s[i % 2][0:E, 0:TILE], xr[i][:, 0:E], ident[:]).then_inc(xT_mm, 1)

            def z_step(t, i):
                pe.wait_ge(xT_sb, t + 1)
                if not (isinstance(t, int) and t < 2):
                    pe.wait_ge(hT_sb, t - 1)
                mm(ps_b[i % 2][:, 0:TILE], wt[i][:, 0:HID], xT[i % 2][:], start=True, stop=True).then_inc(zt_mm, 1)

            def y_step(t, i):
                pe.wait_ge(hT_sb, t + 1)
                if not (isinstance(t, int) and t < 2):
                    pe.wait_ge(yo_done, t - 1)
                o = [ps_u, ps_t][i % 2][:, 0:E]
                mm(o, hT[i % 2][:], wt[i][:, HID:HID + E], start=True, stop=False)
                mm(o, ones_row[B2ROW:B2ROW + 1, :], wt[i][B2ROW:B2ROW + 1, 0:E], start=False, stop=True).then_inc(yt_mm, 1)

            for t in range(2 * NB2):
                x_step(t, t % NB2)
                if t >= 1:
                    z_step(t - 1, (t - 1) % NB2)
                if t >= 2:
                    y_step(t - 2, (t - 2) % NB2)
            with pe.Fori(2, NTILE // NB2) as g:
                t = g * NB2
                for i in range(NB2):
                    x_step(t + i, i)
                    z_step(t + i - 1, (i - 1) % NB2)
                    y_step(t + i - 2, (i - 2) % NB2)
            z_step(NTILE - 1, NB2 - 1)
            y_step(NTILE - 2, NB2 - 2)
            y_step(NTILE - 1, NB2 - 1)

        @block.scalar
        def _(act):
            def copy(dest, src, scale=1.0):
                return act.activation(dest, src, ACT.Copy, scale=scale)

            for g in range(2):
                act.wait_ge(g_mm, g + 1)
                copy(g16[:, 4 * g:4 * g + 4, :].rearrange("p h i -> p (h i)"), ps_s[g][:], E ** -0.5).then_inc(g_hi, 1)
            act.wait_ge(g_mm, 3)
            copy(v16[:], ps_u[:], SC_V).then_inc(g_hi, 1)
            act.wait_ge(consts, CONSTS)
            act.wait_ge(w_emb, 64)

            def start_a(n, step):
                if step == 0:
                    act.wait_ge(emb_done, n + 1)
                    if not (isinstance(n, int) and n == 0):
                        act.wait_ge(pv_mm, SUB * n - (SUB - 1))
                    act.activation(h_a[:], ps_e[:, 0:L], ACT.Identity, bias=tokbias[:, 0:1]).then_inc(h_ready, 1)
                    act.wait_ge(a_cen, n + 1)
                    act.activation(sq_a[:], ps_s[0][:, 0:2 * L], ACT.Square).then_inc(a_sq, 1)
                    if not (isinstance(n, int) and n == 0):
                        act.wait_ge(a_x, n)
                    copy(xf_a[:], ps_s[0][:, 0:2 * L]).then_inc(a_cs, 1)
                if step == 1:
                    act.wait_ge(a_var, n + 1)
                    act.activation(st_a[:], ps_s[1][0:LB, 0:4], ACT.Identity, bias=eps[0:LB, 0:1]).then_inc(a_vs, 1)
                if step == 3:
                    u_hi_step(n, 0)
                    v_out(n, 0)

            def v_out(n, c):
                act.wait_ge(v_mm, 4 * n + c + 1)
                if c == 0 and not (isinstance(n, int) and n == 0):
                    act.wait_ge(pv_mm, SUB * n)
                copy(vt[:, c, :], ps_t[0:LB, :], 1.0 / SC_V).then_inc(v_evac, 1)

            def u_hi_step(n, h):
                act.wait_ge(u_mm, HEADS * n + h + 1)
                copy(us[h % 2][:], ps_u[:, 0:2 * L]).then_inc(u_hi, 1)

            def exp1(n, k):
                act.wait_ge(max_done, SUB * n + k + 1)
                if not (isinstance(n, int) and n == 0 and k < NA):
                    act.wait_ge(e2_done, SUB * n + k - NA + 1)
                for b in range(2):
                    last = act.activation(e1[k % NA][:, b, :], ps_s[k % 2][0:LB, L * b:L * b + L], ACT.Exp,
                                          bias=nmax[k % NA][:, b:b + 1], accum_out=sum1[k % NA][:, b:b + 1])
                last.then_inc(e1_done, 1)

            def exp2(n, k):
                act.wait_ge(mask_done, SUB * n + k + 1)
                act.wait_ge(r1_done, SUB * n + k + 1)
                if not (isinstance(n, int) and n == 0 and k < NA):
                    act.wait_ge(t_mm, SUB * n + k - NA + 1)
                for b in range(2):
                    last = act.activation(p2[k % NA][:, LB * b:LB * b + LB * (b + 1)], e1[k % NA][:, b, 0:LB * (b + 1)],
                                          ACT.Exp, scale=rin1[k % NA][:, b:b + 1], accum_out=sum2[k % NA][:, b:b + 1])
                last.then_inc(e2_done, 1)

            def t_out(n, k):
                act.wait_ge(t_mm, SUB * n + k + 1)
                if not (isinstance(n, int) and n == 0 and k < NA):
                    act.wait_ge(pv_mm, SUB * n + k - NA + 1)
                copy(pt[k % NA][:], ps_t[0:LB, 0:3 * LB]).then_inc(t_evac, 1)

            def stage_b(n, j):
                X, Y = ps_b
                if j in (0, 23, 37):
                    r = {0: 0, 23: 1, 37: 2}[j]
                    act.wait_ge(b_cen, 3 * n + r + 1)
                    act.activation(sq_b[:], X[:, 0:2 * L], ACT.Square).then_inc(b_sq, 1)
                    if not (isinstance(n, int) and n == 0 and r == 0):
                        act.wait_ge(b_x, 3 * n + r)
                    copy(xf_b[:], X[:, 0:2 * L]).then_inc(b_cs, 1)
                if j in (1, 25, 39):
                    r = {1: 0, 25: 1, 39: 2}[j]
                    act.wait_ge(b_var, 3 * n + r + 1)
                    act.activation(st_b[:], Y[0:LB, 0:4], ACT.Identity, bias=eps[0:LB, 0:1]).then_inc(b_vs, 1)
                if j in (7, 46):
                    act.wait_ge(*((g0_dif, n + 1) if j == 7 else (g1_dif, n + 1)))
                    act.activation(edif[:], dif[:], ACT.Exp).then_inc(g0_exp if j == 7 else g1_exp, 1)
                if j == 10:
                    act.wait_ge(cT_mm, n + 1)
                    copy(combT16[:], Y[0:2 * X0, 0:2 * L])
                    copy(combT[:], Y[0:2 * X0, 0:2 * L]).then_inc(cT_sb, 1)
                if 12 <= j < 12 + X0:
                    e = j - 12
                    act.wait_ge(gate_mm, X0 * n + e + 1)
                    if e >= 2:
                        act.wait_ge(hid_done, X0 * n + e - 1)
                    copy(gate[e % 2][:], ps_e[:, 0:2 * L]).then_inc(gate_sb, 1)
                if j == 30:
                    act.wait_ge(q_mm, n + 1)
                    copy(q16[:], X[:, 0:2 * L]).then_inc(q_hi, 1)
                    act.wait_ge(x3_mm, n + 1)
                    copy(x3t[:].rearrange("p c e -> p (c e)"), Y[0:LB, 0:4 * E]).then_inc(x3_sb, 1)
                if j in (32, 33):
                    img = j - 32
                    act.wait_ge(s3_mm, 2 * n + img + 1)
                    act.activation(th[img][:], ps_b[img][0:LB, 0:2 * L], ACT.Tanh, scale=0.5).then_inc(th_done, 1)
                if j == 45:
                    act.wait_ge(h3T_mm, n + 1)
                    if not (isinstance(n, int) and n == 0):
                        act.wait_ge(rows_out, 16 * 8 * n)
                    src = X[0:LB, 256:512].rearrange("p (c e) -> p c e", e=E)
                    for choice in range(2):
                        copy(rows[:].rearrange("p (c o) r -> p c o r", o=2)[:, :, choice, 0:E], src)
                    dest = hres[:, 4 * n:4 * n + 4, :] if isinstance(n, int) else hres[:, bass.ds(4 * n, 4), :]
                    for img in range(2):
                        d2 = hres[:, 4 * n + 2 * img:4 * n + 2 * img + 2, :] if isinstance(n, int) else hres[:, bass.ds(4 * n + 2 * img, 2), :]
                        last = copy(d2, X[0:LB, 0:256].rearrange("p (b i e) -> p i b e", b=2, i=2)[:, img])
                    last.then_inc(h3T_sb, 1)

            def round_(n, a, nb, nxt):
                for k, js in enumerate(PARTS):
                    for op in ORD_ACT:
                        if op == "t" and a and 0 <= k - 4 < SUB:
                            t_out(n, k - 4)
                        if op == "x" and a and 0 <= k - 1 < SUB:
                            exp2(n, k - 1)
                        if op == "u" and a and k % 2 == 0 and k // 2 + 1 < HEADS:
                            u_hi_step(n, k // 2 + 1)
                        if op == "v" and a and k < 3:
                            v_out(n, k + 1)
                        if op == "b" and nb is not None:
                            stage_b(nb, js[0])
                        if op == "e" and a and k < SUB:
                            exp1(n, k)
                        if op == "c" and nb is not None and len(js) > 1:
                            stage_b(nb, js[1])
                        if op == "B" and nb is not None and len(js) > 2:
                            stage_b(nb, js[2])
                        if op == "N" and nxt and k >= SUB:
                            start_a(n + 1, k - SUB)
                if a:
                    act.wait_ge(pv_mm, SUB * (n + 1))
                    copy(h_b[:], ps_o[:, 0:L]).then_inc(hb_ready, 1)

            for step in range(4):
                start_a(0, step)
            round_(0, True, None, True)
            round_(1, True, 0, True)
            with act.Fori(1, NPAIR - 2) as t:
                round_(t + 1, True, t, True)
            round_(NPAIR - 1, True, NPAIR - 2, False)
            round_(NPAIR, False, NPAIR - 1, False)

            act.wait_ge(fill_known, 1)
            fill(act, 1)

            def h_out(t, i):
                act.wait_ge(zt_mm, t + 1)
                if not (isinstance(t, int) and t < 2):
                    act.wait_ge(yt_mm, t - 1)
                act.activation(hT[i % 2][:], ps_b[i % 2][:, 0:TILE], ACT.Relu).then_inc(hT_sb, 1)

            for i in range(NB2):
                h_out(i, i)
            with act.Fori(0, NTILE // NB2 - 1) as g:
                t = g * NB2
                for i in range(NB2):
                    h_out(t + NB2 + i, i)

        @block.vector
        def _(dve):
            dve.wait_ge(consts, CONSTS)
            dve.tensor_copy(iota[:], iota_i[:]).then_inc(prep, 1)
            dve.wait_ge(w_misc, 16 * 15)
            dve.tensor_copy(iota_p[:], iota_p_i[:]).then_inc(prep, 1)
            for e in range(X0):
                last = dve.tensor_scalar(b1diag[:, e, :], ident[:, 0:2 * X0], 0.0, None, ALU.mult)
            last.then_inc(d_self, 1)
            dve.wait_ge(d_self, 1)
            for c in range(2):
                last = dve.tensor_copy(b1diag[:].rearrange("p a b -> p (a b)")[:, X0 * c:X0 * c + (X0 - 1) * (2 * X0 + 1) + 1:2 * X0 + 1], b1raw[:])
            last.then_inc(prep, 1)
            dve.wait_ge(bias_mm, 1)
            dve.tensor_scalar(w2s[:].rearrange("p x e -> p (x e)"), w2s[:].rearrange("p x e -> p (x e)"), 1.0 / SC_0, None, ALU.mult).then_inc(prep, 1)
            dve.tensor_scalar(nb1[:], b1raw[:], -SC_0, None, ALU.mult).then_inc(prep, 1)
            dve.tensor_tensor(b2p[:], ps_t[0:2 * X0, 0:E], b2raw[:], ALU.add).then_inc(prep, 1)
            dve.tensor_tensor(bgb[:, 0, :], bgb[:, 0, :], bgb[:, 1, :], ALU.add).then_inc(prep, 1)
            chain = [1]

            def own(ins):
                ins.then_inc(d_self, 1)
                chain[0] += 1
                dve.wait_ge(d_self, chain[0])

            def split(dest, src, scale):
                own(dve.tensor_scalar(dest, src, scale, None, ALU.mult))
                return dve.scalar_tensor_tensor(dest[64:128], src[64:128], scale, dest[64:128], ALU.mult, ALU.subtract)

            split(wg16[:], raw2[:, 0:X0], SC_0).then_inc(prep, 1)
            split(wr16[:], raw2[:, X0:X0 + X1], SC_R).then_inc(prep, 1)
            split(qw16[:], raw2[:, 128:256], 1.0).then_inc(prep, 1)
            for g in range(2):
                dve.wait_ge(g_hi, g + 1)
                d = g16[64:128, 4 * g:4 * g + 4, :].rearrange("p h i -> p (h i)")
                dve.scalar_tensor_tensor(d, ps_s[g][64:128, :], E ** -0.5, d, ALU.mult, ALU.subtract).then_inc(g_lo, 1)
            dve.wait_ge(g_hi, 3)
            dve.scalar_tensor_tensor(v16[64:128], ps_u[64:128], SC_V, v16[64:128], ALU.mult, ALU.subtract).then_inc(g_lo, 1)
            dve.wait_ge(w_rest, 32)
            split(w116[:], raw[:, 0:X0 * HID], SC_0).then_inc(prep, 1)
            own(dve.tensor_scalar(region[:], iota[0:LB, 0:X1], float(CAP), None, ALU.mult))
            for c in range(4):
                for choice in range(2):
                    last = dve.tensor_scalar(place[:, 2 * c + choice:2 * c + choice + 1], iota_p[0:LB], 4.0, float(choice * T + c), ALU.mult, ALU.add)
            own(last)
            for i in range(2):
                own(dve.memset(xT[i][:], 0.0))
                own(dve.memset(xT[i][E:E + 1, :], 1.0))
            A, B = Chain(dve, a_self, A_LINKS), Chain(dve, b_self, B_LINKS)

            def start_a(n, step):
                if step == 3:
                    u_lo_step(n, 0)
                if step == 2:
                    A.start(n)
                    dve.wait_ge(a_cs, n + 1)
                    dve.wait_ge(a_rb, n + 1)
                    A.add(dve.tensor_tensor(xf_a[:], ps_s[1][:, 0:2 * L], xf_a[:], ALU.mult))
                    A.wait()
                    A.add(dve.tensor_copy(xh_a[:], xf_a[:]))
                    A.wait()
                    dve.tensor_tensor(xl_a[:], xf_a[:], xh_a[:], ALU.subtract).then_inc(a_x, 1)

            def u_lo_step(n, h):
                dve.wait_ge(u_hi, HEADS * n + h + 1)
                u = us[h % 2]
                dve.tensor_tensor(u[64:128], ps_u[64:128, 0:2 * L], u[64:128], ALU.subtract).then_inc(u_lo, 1)

            def max_step(n, k):
                dve.wait_ge(s_mm, SUB * n + k + 1)
                dve.tensor_reduce(nmax[k % NA][:], ps_s[k % 2][0:LB, 0:2 * L].rearrange("p (b m) -> p b m", b=2), AX, ALU.max,
                                  negate=True).then_inc(max_done, 1)

            def r1_step(n, k):
                dve.wait_ge(e1_done, SUB * n + k + 1)
                dve.reciprocal(rin1[k % NA][:], sum1[k % NA][:]).then_inc(r1_done, 1)

            def scale_step(n, k):
                dve.wait_ge(e2_done, SUB * n + k + 1)
                A.add(dve.reciprocal(rin2[k % NA][:], sum2[k % NA][:]))
                A.wait()
                for b in range(2):
                    part = p2[k % NA][:, LB * b:LB * b + LB * (b + 1)]
                    last = dve.tensor_scalar(part, part, rin2[k % NA][:, b:b + 1], None, ALU.mult)
                last.then_inc(p2_done, 1)

            def top2(X, dif_sem):
                alone(dve)
                for c in range(4):
                    last = dve.max(mx8[:, c, :], lg[:, c, 0:X])
                B.add(last)
                B.wait()
                dve.tensor_tensor(dif[:], mx8[:, :, 1], mx8[:, :, 0], ALU.subtract).then_inc(dif_sem, 1)
                for c in range(4):
                    last = dve.max_index(ix8[:, c, :], mx8[:, c, :], lg[:, c, 0:X])
                B.add(last)
                B.wait()
                B.add(dve.tensor_copy(ixf[:].rearrange("p (c o) -> p c o", o=2), ix8[:, :, 0:2]))
                B.wait()
                B.add(dve.tensor_tensor(onehot[:, :, 0:X], iota[0:LB, 0:X].unsqueeze(1).to_broadcast([LB, 8, X]),
                                        ixf[:].unsqueeze(2).to_broadcast([LB, 8, X]), ALU.is_equal))
                B.wait()

            def gate_weights():
                B.add(dve.tensor_scalar(eone[:], edif[:], 1.0, None, ALU.add))
                B.wait()
                B.add(dve.reciprocal(gates[:, :, 0], eone[:]))
                B.wait()
                B.add(dve.tensor_tensor(gates[:, :, 1], edif[:], gates[:, :, 0], ALU.mult))
                B.wait()

            def stage_b(n, j):
                X, Y = ps_b
                if j in (4, 28, 43):
                    r = {4: 0, 28: 1, 43: 2}[j]
                    if r == 0:
                        B.start(n)
                    dve.wait_ge(b_cs, 3 * n + r + 1)
                    dve.wait_ge(b_rb, 3 * n + r + 1)
                    B.add(dve.tensor_tensor(xf_b[:], Y[:, 0:2 * L], xf_b[:], ALU.mult))
                    B.wait()
                    B.add(dve.tensor_copy(xh_b[:], xf_b[:]))
                    B.wait()
                    dve.tensor_tensor(xl_b[:], xf_b[:], xh_b[:], ALU.subtract).then_inc(b_x, 1)
                if j == 6:
                    dve.wait_ge(g0_mm, n + 1)
                    B.add(dve.scalar_tensor_tensor(lg[:, :, 0:X0], X[0:LB, 0:4 * X0].rearrange("p (c x) -> p c x", x=X0),
                                                   1.0 / SC_0, bgb[:, 0:1, :].to_broadcast([LB, 4, X0]), ALU.mult, ALU.add))
                    B.wait()
                    top2(X0, g0_dif)
                if j == 8:
                    dve.wait_ge(g0_exp, n + 1)
                    gate_weights()
                    B.add(dve.tensor_tensor(weighed[:, :, 0:X0], onehot[:, :, 0:X0],
                                            gates[:].rearrange("p c o -> p (c o)").unsqueeze(2).to_broadcast([LB, 8, X0]), ALU.mult))
                    B.wait()
                    w = weighed[:].rearrange("p (c o) x -> p c o x", o=2)
                    B.add(dve.tensor_tensor(comb[:], w[:, :, 0, 0:X0], w[:, :, 1, 0:X0], ALU.add))
                    B.wait()
                    B.add(dve.tensor_copy(comb16[:, :, 0:X0], comb[:]))
                    B.wait()
                    dve.tensor_tensor(comb16[:, :, X0:2 * X0], comb[:], comb16[:, :, 0:X0], ALU.subtract).then_inc(comb_done, 1)
                if 13 <= j < 13 + X0:
                    e = j - 13
                    dve.wait_ge(z_mm, X0 * n + e + 1)
                    dve.wait_ge(gate_sb, X0 * n + e + 1)
                    if e >= 2:
                        dve.wait_ge(y_mm, X0 * n + e - 1)
                    dve.scalar_tensor_tensor(hid[e % 2][:], X[:, 0:2 * L], nb1[:, e:e + 1], gate[e % 2][:], ALU.max, ALU.mult).then_inc(hid_done, 1)
                if j == 21:
                    dve.wait_ge(y_mm, X0 * n + X0)
                    dve.tensor_tensor(h_b[:], Y[:, 0:L], h_b[:], ALU.add).then_inc(h2_done, 1)
                if j == 30:
                    dve.wait_ge(q_hi, n + 1)
                    dve.tensor_tensor(q16[64:128], X[64:128, 0:2 * L], q16[64:128], ALU.subtract).then_inc(q_lo, 1)
                    for img in range(2):
                        sl = slice(64 * img, 64 * img + 64)
                        last = dve.reduce_sum(colsum[sl, 0:1], xf_b[sl, img * L:img * L + L], AX)
                    B.add(last)
                if j == 35:
                    B.wait()
                    dve.wait_ge(val_mm, n + 1)
                    B.add(dve.tensor_scalar(half[:], X[:, 0:L], colsum[:, 0:1], 0.5, ALU.add, ALU.mult))
                    B.wait()
                    dve.tensor_tensor(h_b[:], half[:], h_b[:], ALU.add).then_inc(h3_done, 1)
                if j == 45:
                    dve.wait_ge(g1_mm, n + 1)
                    B.add(dve.scalar_tensor_tensor(lg[:], Y[0:LB, 0:4 * X1].rearrange("p (c x) -> p c x", x=X1),
                                                   1.0 / SC_R, brb[:].unsqueeze(1).to_broadcast([LB, 4, X1]), ALU.mult, ALU.add))
                    B.wait()
                    top2(X1, g1_dif)
                    oh = onehot[:].rearrange("p (c o) x -> p c o x", o=2)
                    dve.tensor_tensor(chosen[:], oh[:, :, 0, :], oh[:, :, 1, :], ALU.add).then_inc(chosen_done, 1)
                if j == 47:
                    dve.wait_ge(g1_exp, n + 1)
                    gate_weights()
                    dve.wait_ge(h3T_sb, n + 1)
                    dve.tensor_copy(rows[:, :, E:E + 1], gates[:].rearrange("p c o -> p (c o)").unsqueeze(2))
                    B.add(dve.tensor_copy(rows[:, :, E + 1:E + 2], place[:].unsqueeze(2)))
                    dve.wait_ge(rank_mm, n + 1)
                    dve.tensor_tensor(ranked[:], Y[0:LB, 0:4 * X1].rearrange("p (c x) -> p c x", x=X1),
                                      region[:].unsqueeze(1).to_broadcast([LB, 4, X1]), ALU.add).then_inc(ranked_done, 1)
                if j == 48:
                    dve.wait_ge(ranked_done, n + 1)
                    B.add(dve.tensor_tensor(weighed[:].rearrange("p (c o) x -> p c o x", o=2), onehot[:].rearrange("p (c o) x -> p c o x", o=2),
                                            ranked[:].unsqueeze(2).to_broadcast([LB, 4, 2, X1]), ALU.mult))
                    B.add(dve.reduce_sum(added[:], chosen[:].rearrange("p c x -> p x c"), AX))
                    B.wait()
                    B.add(dve.reduce_sum(posf[:], weighed[:], AX))
                if j == 49:
                    B.wait()
                    B.add(dve.tensor_tensor(seen[:], seen[:], added[:], ALU.add))
                    B.add(dve.tensor_copy(posi[:], posf[:]))
                    B.add(dve.tensor_scalar(place[:], place[:], 4.0 * LB, None, ALU.add))
                    B.wait()
                    dve.tensor_copy(seen16[:], seen[:]).then_inc(rows_done, 1)
                    B.end()

            def round_(n, a, nb, nr, nxt):
                A.start(n, 2)
                for k, js in enumerate(PARTS):
                    for op in ORD_DVE:
                        if op == "m" and a and k < SUB:
                            max_step(n, k)
                        if op == "r" and a and 0 <= k - 1 < SUB:
                            r1_step(n, k - 1)
                        if op == "s" and a and 0 <= k - 2 < SUB:
                            scale_step(n, k - 2)
                            if k - 2 == SUB - 1:
                                A.end()
                        if op == "w" and nr is not None and k < 2:
                            B.start(nr, B_LINKS - 6 + 3 * k)
                            stage_b(nr, 48 + k)
                        if op == "b" and nb is not None:
                            stage_b(nb, js[0])
                        if op == "u" and a and k % 2 == 0 and k // 2 + 1 < HEADS:
                            u_lo_step(n, k // 2 + 1)
                        if op == "N" and nxt and k >= SUB:
                            start_a(n + 1, k - SUB)
                        if op == "c" and nb is not None and len(js) > 1:
                            stage_b(nb, js[1])
                        if op == "B" and nb is not None and len(js) > 2:
                            stage_b(nb, js[2])

            for step in range(4):
                start_a(0, step)
            round_(0, True, None, None, True)
            round_(1, True, 0, None, True)
            with dve.Fori(1, NPAIR - 2) as t:
                round_(t + 1, True, t, t - 1, True)
            round_(NPAIR - 1, True, NPAIR - 2, NPAIR - 3, False)
            round_(NPAIR, False, NPAIR - 1, NPAIR - 2, False)
            for k in range(2):
                B.start(NPAIR - 1, B_LINKS - 6 + 3 * k)
                stage_b(NPAIR - 1, 48 + k)

            dve.wait_ge(cnt_mm, 1)
            own(dve.tensor_tensor(fillf[:], ps_b[1][0:1, 0:X1], region[0:1, :], ALU.add))
            dve.tensor_copy(filli[:], fillf[:]).then_inc(fill_known, 1)
            own(dve.tensor_copy(cnt[:], ps_b[0][0:X1, 0:1]))
            own(dve.tensor_scalar(steps[:], iota[0:X1, 0:T // TILE + 1], float(TILE), None, ALU.mult))
            own(dve.tensor_scalar(less[:], steps[:], cnt[:, 0:1], None, ALU.is_lt))
            dve.reduce_sum(ntl[:], less[:], AX).then_inc(cum_in, 1)
            dve.wait_ge(cum_in, 1)
            own(dve.tensor_scalar(skip[:], ntl[:], -float(TILE), float(CAP), ALU.mult, ALU.add))
            dve.wait_ge(cum_mm, 1)
            own(dve.tensor_copy(cum[:], ps_u[0:X1, 0:1]))
            dve.tensor_scalar(past[:], iota[0:X1, :], cum[:, 0:1], None, ALU.is_ge).then_inc(past_in, 1)
            dve.wait_ge(meta_mm, 1)
            own(dve.scalar_tensor_tensor(metaf[:, 0, :], iota[0:1, :], float(TILE), ps_s[0][0:1, 0:NTILE], ALU.mult, ALU.add))
            own(dve.tensor_scalar(metaf[:, 0, :], metaf[:, 0, :], float(X1 * CAP), None, ALU.min))
            own(dve.tensor_scalar(metaf[:, 1, :], ps_s[1][0:1, 0:NTILE], float(X1 - 1), None, ALU.min))
            dve.tensor_copy(metai[:].rearrange("o g i k -> o k (g i)"), metaf[:]).then_inc(meta_done, 1)

            def x_out(t, i):
                dve.wait_ge(xT_mm, t + 1)
                if not (isinstance(t, int) and t < 2):
                    dve.wait_ge(zt_mm, t - 1)
                dve.tensor_copy(xT[i % 2][0:E], ps_s[i % 2][0:E, 0:TILE]).then_inc(xT_sb, 1)

            def y_rows(t, i):
                dve.wait_ge(yt_mm, t + 1)
                if not (isinstance(t, int) and t < NB2):
                    dve.wait_ge(y_out[i], (t - i) * (16 // NB2))
                dve.tensor_copy(dst[i][:], xr[i][:, E + 1:E + 2])
                dve.tensor_scalar(yo[i][:], [ps_u, ps_t][i % 2][:, 0:E], xr[i][:, E:E + 1], None, ALU.mult).then_inc(yo_done, 1)

            for t in range(2 * NB2):
                x_out(t, t % NB2)
                if t >= 2:
                    y_rows(t - 2, (t - 2) % NB2)
            with dve.Fori(2, NTILE // NB2) as g:
                t = g * NB2
                for i in range(NB2):
                    x_out(t + i, i)
                    y_rows(t + i - 2, (i - 2) % NB2)
            y_rows(NTILE - 2, NB2 - 2)
            y_rows(NTILE - 1, NB2 - 1)

            NS = NBLK // CB

            def finish(s, i, first):
                dve.wait_ge(y_in[i], 16 * (s - i) + 32)
                dve.tensor_tensor(ysum[i][:], yin[i][:, 0], yin[i][:, 1], ALU.add).then_inc(ys_done, 1)
                dve.wait_ge(ys_done, s + 1)
                if not first:
                    dve.wait_ge(fin_out[i], (s - i) * 8)
                src = hres[:, CB * s:CB * s + CB, :] if isinstance(s, int) else hres[:, bass.ds(CB * s, CB), :]
                dve.tensor_tensor(yfin[i][:], ysum[i][:], src, ALU.add).then_inc(fin_done, 1)

            finish(0, 0, True)
            finish(1, 1, True)
            with dve.Fori(0, NS // 2 - 1) as g:
                s = g * 2
                for i in range(2):
                    finish(s + 2 + i, i, False)


_ORDER = ["x", "tokW", "tokb", "Wq", "Wk", "Wv", "WoT", "Wg", "bg", "bias", "W1", "b1", "b1T", "W2", "b2",
          "qw", "Wr", "br", "E1W"]


def kernel(**inputs):
    import numpy as _np
    import concourse.bacc as _bacc
    from concourse import mybir as _mybir
    from concourse.bass_utils import run_bass_kernel_spmd as _run

    i = {k: _np.asarray(v) for k, v in inputs.items()}
    E, K = i["L0_tok_W"].shape
    CH = i["x"].shape[1]
    X, _, HID = i["L1_ffn_W1"].shape
    packed = _np.zeros((X, 128, HID + E), i["L1_ffn_W1"].dtype)
    packed[:, 0:E, 0:HID] = i["L1_ffn_W1"]
    packed[:, E, 0:HID] = i["L1_ffn_b1"]
    packed[:, B2ROW, 0:E] = i["L1_ffn_b2"]
    packed[:, :, HID:] = i["L1_ffn_W2"]
    laid = {
        "x": i["x"],
        "tokW": i["L0_tok_W"].reshape(E, CH * PATCH, PATCH).transpose(1, 2, 0),
        "tokb": i["L0_tok_b"], "Wq": i["L0_attn_Wq"], "Wk": i["L0_attn_Wk"], "Wv": i["L0_attn_Wv"],
        "WoT": i["L0_attn_Wo"].T, "Wg": i["L0_ffn_Wg"], "bg": i["L0_ffn_bg"], "bias": i["L0_ffn_bias"],
        "W1": i["L0_ffn_W1"], "b1": i["L0_ffn_b1"], "b1T": i["L0_ffn_b1"].T, "W2": i["L0_ffn_W2"], "b2": i["L0_ffn_b2"],
        "qw": i["L1_attn_q_weight"], "Wr": i["L1_ffn_Wr"], "br": i["L1_ffn_br"],
        "E1W": packed,
    }
    nc = _bacc.Bacc("TRN2", target_bir_lowering=False, num_devices=1)
    arrays, args = {}, []
    for name in _ORDER:
        a = _np.ascontiguousarray(laid[name])
        arrays[f"in_{name}"] = a
        args.append(nc.dram_tensor(f"in_{name}", a.shape, _mybir.dt.from_np(a.dtype), kind="ExternalInput").ap())
    n_img = i["x"].shape[0]
    tokens = (i["x"].shape[2] // PATCH) * (i["x"].shape[3] // PATCH)
    out = nc.dram_tensor("out_0", (n_img, tokens, E), F32, kind="ExternalOutput").ap()
    vit_tower(nc, *args, out)
    r = _run(nc, [arrays], core_ids=[0])
    return r.results[0]["out_0"]
```

```python
from contextlib import ExitStack

import concourse.bass as bass
from concourse import mybir

F32 = mybir.dt.float32
F16 = mybir.dt.float16
BF16 = mybir.dt.bfloat16
I32 = mybir.dt.int32
U32 = mybir.dt.uint32
ALU = mybir.AluOpType
ACT = mybir.ActivationFunctionType
AX = mybir.AxisListType.X

PATCH = 16
EPS = 1e-5
NEG = -1e30
B2ROW = 96


ORD_PE = "ESVbNCTcPBdUD"
ORD_ACT = "etuxHbhNvcCdBD"
ORD_DVE = "ruNmbCscdBD"


class Chain:

    def __init__(self, eng, sem, per_round):
        self.eng, self.sem, self.per, self.n, self.done = eng, sem, per_round, 0, 0

    def start(self, n, done=0):
        self.n, self.done = n, done

    def add(self, instruction):
        instruction.then_inc(self.sem, 1)
        self.done += 1

    def wait(self):
        self.eng.wait_ge(self.sem, self.n * self.per + self.done)

    def end(self):
        assert self.done == self.per, (self.done, self.per)


def vit_tower(nc, x, tokW, tokb, Wq, Wk, Wv, WoT, Wg, bg, bias, W1, b1, b1T, W2, b2,
              qw, Wr, br, E1W, out):
    NIMG, CH, HH, WW = x.shape
    NH, NW = HH // PATCH, WW // PATCH
    L = NH * NW
    LB = L // 2
    NPAIR = NIMG // 2
    T = NIMG * L
    NBLK = T // LB
    E = tokb.shape[0]
    KR = CH * PATCH
    HEADS = Wq.shape[0] // E
    SUB = 2 * HEADS
    X0, HID = W1.shape[0], W1.shape[2]
    X1 = Wr.shape[1]
    TILE = 128
    CAP = (T // TILE + 2) * TILE
    NB2 = 8
    NTILE = -(-(2 * T // TILE + X1 - 1) // NB2) * NB2
    ROW = E + 2
    FAR = 2.0 ** 20
    SC_V, SC_0, SC_R = 64.0, 256.0, 16.0
    assert E == 64 and LB <= 128 and HID == 128 and L % 2 == 0 and 2 * T < FAR and X1 * CAP < 2 ** 24

    with ExitStack() as ctx:
        def sb(name, shape, dt=F32):
            return ctx.enter_context(nc.sbuf_tensor(name, shape, dt))

        def sem(name):
            return ctx.enter_context(nc.semaphore(name))

        def bank(name):
            return ctx.enter_context(nc.psum_tensor(name, [128, 512], F32))
        ps_s = [bank("ps_s0"), bank("ps_s1")]
        ps_u = bank("ps_u")
        ps_t = bank("ps_t")
        ps_o = bank("ps_o")
        ps_b = [bank("ps_b0"), bank("ps_b1")]
        ps_c = bank("ps_c")

        rows_d = nc.dram_tensor("rows_scratch", (X1 * CAP + TILE, ROW), F32).ap()
        y_d = nc.dram_tensor("y_scratch", (2 * T, E), F32).ap()

        ident = sb("ident", [128, 128])
        center = [sb("center_a", [128, 128]), sb("center_b", [128, 128])]
        average = sb("average", [128, 128])
        before = sb("before", [128, 128], BF16)
        ones16 = sb("ones16", [128, 128], BF16)
        upto = sb("upto", [X1, X1])
        onesf = sb("onesf", [128, 8])
        power = sb("power", [128, 4])
        ident16 = sb("ident16", [LB, LB], F16)
        eps = sb("eps", [128, 1])
        iota_i = sb("iota_i", [128, NTILE], I32)
        iota = sb("iota", [128, NTILE])
        iota_p_i = sb("iota_p_i", [128, 1], I32)
        iota_p = sb("iota_p", [128, 1])
        region = sb("region", [LB, X1])
        place = sb("place", [LB, 8])
        tokw = sb("tokw", [128, PATCH, 128])
        tokbias = sb("tokbias", [128, 1])
        raw = sb("raw", [128, 2048])
        raw2 = sb("raw2", [128, 1024])
        g16 = sb("g16", [128, HEADS, 128], F16)
        v16 = sb("v16", [128, HEADS * E], F16)
        wg16 = sb("wg16", [128, X0], F16)
        w116 = sb("w116", [128, X0 * HID], F16)
        qw16 = sb("qw16", [128, 128], F16)
        wr16 = sb("wr16", [128, X1], F16)
        w2s = sb("w2s", [HID, X0, E])
        b1raw = sb("b1raw", [HID, X0])
        nb1 = sb("nb1", [HID, X0])
        b1diag = sb("b1diag", [HID, X0, 2 * X0])
        b2raw = sb("b2raw", [2 * X0, E])
        b2p = sb("b2p", [2 * X0, E])
        bgb = sb("bgb", [LB, 2, X0])
        brb = sb("brb", [LB, X1])
        tail = sb("tail", [TILE, ROW])

        xin = sb("xin", [128, NH, WW])
        NA = 4
        h_a = sb("h_a", [128, L])
        sq_a = sb("sq_a", [128, 2 * L])
        st_a = sb("st_a", [LB, 4])
        sth_a = sb("sth_a", [LB, 2, 4], F16)
        xf_a = sb("xf_a", [128, 2 * L])
        xh_a = [sb(f"xh_a{i}", [128, 2 * L], F16) for i in range(2)]
        xl_a = [sb(f"xl_a{i}", [128, 2 * L], F16) for i in range(2)]
        vt = [sb(f"vt{i}", [LB, 4, HEADS * E]) for i in range(2)]
        us = [sb(f"us{i}", [128, 2 * L], F16) for i in range(2)]
        e1 = [sb(f"e1{i}", [LB, 2, L]) for i in range(NA)]
        nmax = [sb(f"nmax{i}", [LB, 2]) for i in range(NA)]
        sum1 = [sb(f"sum1{i}", [LB, 2]) for i in range(NA)]
        rin1 = [sb(f"rin1{i}", [LB, 2]) for i in range(NA)]
        sum2 = [sb(f"sum2{i}", [LB, 2]) for i in range(NA)]
        rin2 = [sb(f"rin2{i}", [LB, 2]) for i in range(NA)]
        p2 = [sb(f"p2{i}", [LB, 3 * LB]) for i in range(NA)]
        pt = [sb(f"pt{i}", [LB, 3 * LB]) for i in range(NA)]

        h_b = sb("h_b", [128, L])
        sq_b = sb("sq_b", [128, 2 * L])
        st_b = sb("st_b", [LB, 4])
        sth_b = sb("sth_b", [LB, 2, 4], F16)
        xf_b = sb("xf_b", [128, 2 * L])
        xh_b = sb("xh_b", [128, 2 * L], F16)
        xl_b = sb("xl_b", [128, 2 * L], F16)

        h_c = sb("h_c", [128, L])
        sq_c = sb("sq_c", [128, 2 * L])
        st_c = sb("st_c", [LB, 4])
        sth_c = sb("sth_c", [LB, 2, 4], F16)
        xf_c = sb("xf_c", [128, 2 * L])
        xh_c = sb("xh_c", [128, 2 * L], F16)
        xl_c = sb("xl_c", [128, 2 * L], F16)

        lg = sb("lg", [LB, 4, X1])
        mx8 = sb("mx8", [LB, 4, 8])
        ix8 = sb("ix8", [LB, 4, 8], U32)
        ixf = sb("ixf", [LB, 8])
        dif = sb("dif", [LB, 4])
        edif = sb("edif", [LB, 4])
        eone = sb("eone", [LB, 4])
        gates = sb("gates", [LB, 4, 2])
        onehot = sb("onehot", [LB, 8, X1])
        weighed = sb("weighed", [LB, 8, X1])
        comb = sb("comb", [LB, 4, X0])
        comb16 = sb("comb16", [LB, 4, 2 * X0], F16)
        combT = sb("combT", [2 * X0, 2 * L])
        combT16 = sb("combT16", [2 * X0, 2 * L], F16)
        pick = sb("pick", [2 * X0, X0, 128], F16)
        gate = [sb(f"gate{i}", [HID, 2 * L]) for i in range(2)]
        hid = [sb(f"hid{i}", [HID, 2 * L]) for i in range(2)]
        q16 = sb("q16", [128, 2 * L], F16)
        x3t = sb("x3t", [LB, 4, E])
        th = [sb(f"th{i}", [LB, 2 * L]) for i in range(2)]
        colsum = sb("colsum", [128, 1])
        half = sb("half", [128, L])
        hres = sb("hres", [LB, NBLK, E])
        rows = sb("rows", [LB, 8, ROW])
        chosen = sb("chosen", [LB, 4, X1], BF16)
        seen = sb("seen", [LB, X1])
        seen16 = sb("seen16", [LB, X1], BF16)
        added = sb("added", [LB, X1])
        ranked = sb("ranked", [LB, 4, X1])
        posf = sb("posf", [LB, 8])
        posi = sb("posi", [LB, 8], U32)

        cnt = sb("cnt", [X1, 1])
        steps = sb("steps", [X1, T // TILE + 1])
        less = sb("less", [X1, T // TILE + 1])
        ntl = sb("ntl", [X1, 1])
        cum = sb("cum", [X1, 1])
        past = sb("past", [X1, NTILE])
        skip = sb("skip", [X1, 1])
        fillf = sb("fillf", [1, X1])
        filli = sb("filli", [1, X1], I32)
        metaf = sb("metaf", [1, 2, NTILE])
        metai = sb("metai", [1, 2, NTILE], I32)

        xr = [sb(f"xr{i}", [TILE, ROW]) for i in range(NB2)]
        wt = [sb(f"wt{i}", [128, HID + E]) for i in range(NB2)]
        b2_row = sb("b2_row", [128, TILE])
        xT = [sb(f"xT{i}", [128, TILE]) for i in range(2)]
        hT = [sb(f"hT{i}", [HID, TILE]) for i in range(2)]
        yo = [sb(f"yo{i}", [TILE, E]) for i in range(NB2)]
        dst = [sb(f"dst{i}", [TILE, 1], U32) for i in range(NB2)]
        CB = 8
        yin = [sb(f"yin{i}", [LB, 2, CB, E]) for i in range(2)]
        ysum = [sb(f"ysum{i}", [LB, CB, E]) for i in range(2)]
        yfin = [sb(f"yfin{i}", [LB, CB, E]) for i in range(2)]

        w_qk, w_vo, w_rest, w_emb, w_misc = sem("w_qk"), sem("w_vo"), sem("w_rest"), sem("w_emb"), sem("w_misc")
        zeroed, consts, pool_c, emb_zero = sem("zeroed"), sem("consts"), sem("pool_c"), sem("emb_zero")
        g_mm, g_hi, g_lo, prep = sem("g_mm"), sem("g_hi"), sem("g_lo"), sem("prep")
        raw_free, bias_mm = sem("raw_free"), sem("bias_mm")
        x_in, emb_done, h_ready, hb_ready = sem("x_in"), sem("emb_done"), sem("h_ready"), sem("hb_ready")
        a_vs, a_rs, b_vs, b_rs = sem("a_vs"), sem("a_rs"), sem("b_vs"), sem("b_rs")
        a_rb, a_cs, b_rb, b_cs = sem("a_rb"), sem("a_cs"), sem("b_rb"), sem("b_cs")
        a_cen, a_sq, a_var, a_x, a_self = sem("a_cen"), sem("a_sq"), sem("a_var"), sem("a_x"), sem("a_self")
        v_mm, v_evac, u_mm, u_hi, u_lo = sem("v_mm"), sem("v_evac"), sem("u_mm"), sem("u_hi"), sem("u_lo")
        s_mm, max_done, e1_done, mask_done, r1_done = sem("s_mm"), sem("max_done"), sem("e1_done"), sem("mask_done"), sem("r1_done")
        e2_done, p2_done, t_mm, t_evac, pv_mm = sem("e2_done"), sem("p2_done"), sem("t_mm"), sem("t_evac"), sem("pv_mm")
        c_cen, c_var, c_x, c_self, c_vs, c_rs, c_rb, c_cs = sem("c_cen"), sem("c_var"), sem("c_x"), sem("c_self"), sem("c_vs"), sem("c_rs"), sem("c_rb"), sem("c_cs")
        x_self, hb_used = sem("x_self"), sem("hb_used")
        pa_self, pb_self, pc_self = sem("pa_self"), sem("pb_self"), sem("pc_self")
        b_cen, b_sq, b_var, b_x, b_self = sem("b_cen"), sem("b_sq"), sem("b_var"), sem("b_x"), sem("b_self")
        g0_mm, g0_dif, g0_exp, comb_done, cT_mm, cT_sb, gate_mm, gate_sb = sem("g0_mm"), sem("g0_dif"), sem("g0_exp"), sem("comb_done"), sem("cT_mm"), sem("cT_sb"), sem("gate_mm"), sem("gate_sb")
        z_mm, hid_done, y_mm, h2_done = sem("z_mm"), sem("hid_done"), sem("y_mm"), sem("h2_done")
        q_mm, q_hi, q_lo, x3_mm, x3_sb, s3_mm, th_done = sem("q_mm"), sem("q_hi"), sem("q_lo"), sem("x3_mm"), sem("x3_sb"), sem("s3_mm"), sem("th_done")
        val_mm, h3_done, h3T_mm, h3T_sb, g1_mm, g1_dif, g1_exp = sem("val_mm"), sem("h3_done"), sem("h3T_mm"), sem("h3T_sb"), sem("g1_mm"), sem("g1_dif"), sem("g1_exp")
        chosen_done, rank_mm, ranked_done, rows_done, rows_out = sem("chosen_done"), sem("rank_mm"), sem("ranked_done"), sem("rows_done"), sem("rows_out")
        cnt_mm, cum_in, cum_mm, past_in, meta_mm, meta_done, fill_known, fill_out, d_self = sem("cnt_mm"), sem("cum_in"), sem("cum_mm"), sem("past_in"), sem("meta_mm"), sem("meta_done"), sem("fill_known"), sem("fill_out"), sem("d_self")
        x_tile = [sem(f"x_tile{i}") for i in range(NB2)]
        w_tile = [sem(f"w_tile{i}") for i in range(NB2)]
        xT_mm, xT_sb, zt_mm, hT_sb, yt_mm, yo_done = sem("xT_mm"), sem("xT_sb"), sem("zt_mm"), sem("hT_sb"), sem("yt_mm"), sem("yo_done")
        y_out = [sem(f"y_out{i}") for i in range(NB2)]
        y_in = [sem(f"y_in{i}") for i in range(2)]
        ys_done, fin_done = sem("ys_done"), sem("fin_done")
        fin_out = [sem(f"fin_out{i}") for i in range(2)]

        passed = {e: sem(f"passed_{n}") for e, n in ((mybir.EngineType.SP, "sp"), (mybir.EngineType.Pool, "pool"),
                                                     (mybir.EngineType.PE, "pe"), (mybir.EngineType.DVE, "dve"), (mybir.EngineType.Activation, "act"))}
        X_LINKS, A_LINKS, B_LINKS, C_LINKS = 2, SUB, 13, 21
        B_FROM, C_FROM = 29, 41
        PARTS_B = [(0,), (1,), (3, 4), (5, 6), (7, 8), (9, 10), (12,), (13, 14), (15, 16),
                   (17, 18), (19, 20), (21,)]
        PARTS_C = [(22, 23, 24), (25,), (26, 28), (29, 30), (31, 32), (33, 34), (35, 36), (37, 38), (39, 41, 43),
                   (44, 45), (51, 52), (53, 54), (55,), (48,), (49,)]
        assert len(PARTS_B) <= SUB and len(PARTS_C) <= SUB

        PREP = 11
        CONSTS = 18
        block = ctx.enter_context(nc.Block())

        def rounds(eng, round_):
            for r in range(-1, 4):
                round_(r, r % 2)
            with eng.Fori(2, NPAIR // 2 - 1) as t:
                for i in range(2):
                    round_(t * 2 + i, i)
            for r in range(NPAIR - 2, NPAIR + 3):
                round_(r, r % 2)

        def due(r, parity, k, first, last):
            for d in range(-1, 4):
                n, at = r - d, k + SUB * d
                if first <= at <= last and not (isinstance(n, int) and not 0 <= n < NPAIR):
                    return n, at, (parity - d) % 2
            return None

        def most(n, top):
            return min(n, top) if isinstance(n, int) else n

        def first_pairs(n, m):
            return isinstance(n, int) and n < m

        def alone(eng):
            eng.sem_inc(passed[eng.engine], 1)

        def fill(eng, side):
            FG = 16
            with eng.Fori(side * X1 // (2 * FG), (side + 1) * X1 // (2 * FG)) as e:
                alone(eng)
                _, ends = nc.values_load_multi_w_load_instructions(filli[0:1, bass.ds(e * FG, FG)], engines=[eng.engine],
                                                                   min_val=0, max_val=X1 * CAP - TILE,
                                                                   skip_runtime_bounds_check_because="an expert has at most T rows, below CAP - TILE")
                for i in range(FG):
                    eng.dma_start(rows_d[bass.ds(ends[i], TILE)], tail[:]).then_inc(fill_out, 16)

        def x_rows(img):
            return x[img:img + 1] if isinstance(img, int) else x[bass.ds(img, 1)]

        @block.sync
        def _(sp):
            def load_images(n):
                for img in range(2):
                    for c in range(CH):
                        src = x_rows(2 * n + img)[:, c].rearrange("o (a p) w -> p (o a) w", p=PATCH)
                        r = 64 * img + c * PATCH
                        sp.dma_start(xin[r:r + PATCH], src).then_inc(x_in, 16)

            sp.wait_ge(zeroed, 1)
            load_images(0)
            sp.wait_ge(emb_zero, 1)
            for r in range(2):
                sp.dma_start(tokw[64 * r:64 * r + KR, :, 64 * r:64 * r + E], tokW).then_inc(w_emb, 16)
                sp.dma_start(tokbias[64 * r:64 * r + E], tokb.rearrange("(e o) -> e o", o=1)).then_inc(w_emb, 16)
            for r in range(2):
                sp.dma_start(raw[0:E, 0:1024].rearrange("d (h i) -> d h i", h=HEADS)[:, :, 64 * r:64 * r + E],
                             Wq.rearrange("(h d) i -> d h i", d=E)).then_inc(w_qk, 16)
                sp.dma_start(raw[0:E, 1024:2048].rearrange("d (h i) -> d h i", h=HEADS)[:, :, 64 * r:64 * r + E],
                             Wk.rearrange("(h d) i -> d h i", d=E)).then_inc(w_qk, 16)
            for r in range(2):
                lo, hi = 64 * r, 64 * r + E
                sp.dma_start(raw2[lo:hi, 0:X0], Wg).then_inc(w_misc, 16)
                sp.dma_start(raw2[lo:hi, X0:X0 + X1], Wr).then_inc(w_misc, 16)
                for c in range(2):
                    sp.dma_start(raw2[lo:hi, 128 + E * c:128 + E * (c + 1)], qw).then_inc(w_misc, 16)
            sp.dma_start(b1raw[:], b1T).then_inc(w_misc, 16)
            for r in range(2):
                sp.dma_start(b2raw[X0 * r:X0 * r + X0], b2).then_inc(w_misc, 16)
            sp.dma_start(w2s[:], W2.rearrange("x h e -> h x e")).then_inc(w_misc, 16)
            sp.dma_start(bgb[:, 0, :], bg.partition_broadcast(LB)).then_inc(w_misc, 16)
            sp.dma_start(bgb[:, 1, :], bias.partition_broadcast(LB)).then_inc(w_misc, 16)
            sp.dma_start(brb[:], br.partition_broadcast(LB)).then_inc(w_misc, 16)
            sp.wait_ge(g_mm, 2)
            for r in range(2):
                sp.dma_start(raw[0:E, 0:1024].rearrange("d (h i) -> d h i", h=HEADS)[:, :, 64 * r:64 * r + E],
                             Wv.rearrange("(h d) i -> d h i", d=E)).then_inc(w_vo, 16)
            sp.dma_start(raw[0:E, 1024:1024 + HEADS * E].rearrange("d (h e) -> d h e", h=HEADS),
                         WoT.rearrange("(h d) e -> d h e", d=E)).then_inc(w_vo, 16)
            sp.wait_ge(g_mm, 3)
            for r in range(2):
                sp.dma_start(raw[64 * r:64 * r + E, 0:X0 * HID].rearrange("d (x h) -> d x h", x=X0),
                             W1.rearrange("x d h -> d x h")).then_inc(w_rest, 16)

            def sp_stage_a(n):
                sp.wait_ge(emb_done, n + 2)
                load_images(n + 2)

            sp.wait_ge(emb_done, 1)
            load_images(1)
            sp_stage_a(0)
            sp_stage_a(1)
            with sp.Fori(1, NPAIR - 3) as t:
                sp_stage_a(t + 1)

            sp.wait_ge(fill_known, 1)
            sp.dma_start(rows_d[X1 * CAP:X1 * CAP + TILE], tail[:]).then_inc(fill_out, 16)
            fill(sp, 0)
            sp.wait_ge(rows_out, 16 * 8 * NPAIR)
            sp.wait_ge(fill_out, 16 * (X1 + 1))
            sp.wait_ge(meta_done, 1)

            def load_tiles(g, reuse):
                alone(sp)
                _, at = nc.values_load_multi_w_load_instructions(metai[0:1, 0, bass.ds(g * NB2, NB2)], engines=[mybir.EngineType.SP],
                                                                 min_val=0, max_val=X1 * CAP,
                                                                 skip_runtime_bounds_check_because="metai is clamped")
                for i in range(NB2):
                    if reuse:
                        sp.wait_ge(yo_done, g * NB2 + i - (NB2 - 1))
                        alone(sp)
                    sp.dma_start(xr[i][:], rows_d[bass.ds(at[i], TILE)]).then_inc(x_tile[i], 16)

            load_tiles(0, False)
            with sp.Fori(1, NTILE // NB2) as g:
                load_tiles(g, True)

            for i in range(NB2):
                sp.wait_ge(y_out[i], 16 * (NTILE // NB2))

            def load_y(s, i, reuse):
                if reuse:
                    sp.wait_ge(ys_done, s - 1)
                for c in range(2):
                    src = y_d[bass.ds(T * c + s * (CB * LB), CB * LB)].rearrange("(b p q) e -> p b (q e)", p=LB, q=4)
                    sp.dma_start(yin[i][:, c].rearrange("p (b q) e -> p b (q e)", q=4), src).then_inc(y_in[i], 16)

            load_y(0, 0, False)
            load_y(1, 1, False)
            out_rows = out.rearrange("i t e -> (i t) e")

            def store(s, i):
                sp.wait_ge(fin_done, s + 1)
                sp.dma_start(out_rows[bass.ds(s * (CB * LB), CB * LB)].rearrange("(b p) e -> p b e", p=LB),
                             yfin[i][:]).then_inc(fin_out[i], 16)

            NS = NBLK // CB
            with sp.Fori(0, NS // 2 - 1) as g:
                s = g * 2
                for i in range(2):
                    load_y(s + 2 + i, i, True)
                    store(s + i, i)
            for i in range(2):
                store(NS - 2 + i, i)
            for i in range(2):
                sp.wait_ge(fin_out[i], 16 * (NS // 2))

        @block.gpsimd
        def _(pool):
            pool.memset(xin[:], 0.0).then_inc(zeroed, 1)
            pool.memset(tokw[:], 0.0).then_inc(emb_zero, 1)
            made = [0]

            def own(ins):
                ins.then_inc(pool_c, 1)
                made[0] += 1
                pool.wait_ge(pool_c, made[0])

            def diagonal(m, fill, base=0):
                n = m.shape[1]
                return pool.affine_select(out=m, in_=m, compare_op=ALU.not_equal, fill=fill, base=base,
                                          pattern=[[-1, n]], channel_multiplier=1)

            own(pool.memset(ident[:], 0.0))
            diagonal(ident[:], 1.0).then_inc(consts, 1)
            for img in range(2):
                own(pool.memset(center[img][:], 0.0))
                own(pool.memset(center[img][64 * img:64 * img + 64], -1.0 / E))
                for c in range(2):
                    part = center[img][64 * img:64 * img + 64, 64 * c:64 * c + 64]
                    diagonal(part, 1.0 - 1.0 / E).then_inc(consts, 1)
                    pool.wait_ge(consts, 2 + 2 * img + c)
            pool.memset(average[:], 0.5 / E).then_inc(consts, 1)
            own(pool.memset(before[:], 1.0))
            pool.affine_select(out=before[:], in_=before[:], compare_op=ALU.is_gt, fill=0.0, base=0,
                               pattern=[[1, 128]], channel_multiplier=-1).then_inc(consts, 1)
            pool.memset(ones16[:], 1.0).then_inc(consts, 1)
            own(pool.memset(upto[:], 1.0))
            pool.affine_select(out=upto[:], in_=upto[:], compare_op=ALU.is_ge, fill=0.0, base=0,
                               pattern=[[1, X1]], channel_multiplier=-1).then_inc(consts, 1)
            pool.memset(onesf[:], 1.0).then_inc(consts, 1)
            own(pool.memset(b2_row[:], 0.0))
            own(pool.memset(b2_row[B2ROW:B2ROW + 1, :], 1.0))
            pool.memset(power[:], -0.5).then_inc(consts, 1)
            pool.memset(eps[:], EPS).then_inc(consts, 1)
            own(pool.memset(ident16[:], 0.0))
            diagonal(ident16[:], 1.0).then_inc(consts, 1)
            own(pool.memset(pick[:], 0.0))
            own(pool.affine_select(out=pick[:], in_=pick[:], compare_op=ALU.not_equal, fill=1.0, base=0,
                                   pattern=[[-1, X0], [0, 128]], channel_multiplier=1))
            pool.affine_select(out=pick[:], in_=pick[:], compare_op=ALU.not_equal, fill=1.0, base=-X0,
                               pattern=[[-1, X0], [0, 128]], channel_multiplier=1).then_inc(consts, 1)
            pool.iota(iota_i[:], pattern=[[1, NTILE]], base=0, channel_multiplier=0).then_inc(consts, 1)
            pool.iota(iota_p_i[:], pattern=[[0, 1]], base=0, channel_multiplier=1).then_inc(consts, 1)
            own(pool.memset(tail[:], 0.0))
            pool.memset(tail[:, E + 1:E + 2], FAR).then_inc(consts, 1)
            pool.memset(seen[:], 0.0).then_inc(consts, 1)
            pool.memset(seen16[:], 0.0).then_inc(consts, 1)

            def pool_stage_a(n, k):
                pool.wait_ge(e1_done, SUB * n + k + 1)
                alone(pool)
                view = e1[k % NA][:].rearrange("p b m -> p (b m)")
                diag = bass.AP(view.tensor, view.offset, [list(view.ap[0]), [3 * LB, 2], [1, LB]])
                pool.affine_select(out=diag, in_=diag, compare_op=ALU.is_ge, fill=NEG, base=0,
                                   pattern=[[0, 2], [-1, LB]], channel_multiplier=1).then_inc(mask_done, 1)

            def scatter(n, c):
                if c == 0:
                    pool.wait_ge(rows_done, n + 1)
                    alone(pool)
                pool.indirect_dma_start(out=rows_d, out_offset=bass.IndirectOffsetOnAxis(ap=posi[:, c:c + 1], axis=0),
                                        in_=rows[:, c, :], in_offset=None).then_inc(rows_out, 16)

            pool.wait_ge(consts, CONSTS)

            PA, PB, PC = Chain(pool, pa_self, 2), Chain(pool, pb_self, 2), Chain(pool, pc_self, 4)

            def rstd(P, st, sth, done):
                P.add(pool.tensor_tensor(st[:], st[:], power[0:LB], ALU.pow))
                P.wait()
                alone(pool)
                P.add(pool.tensor_copy(sth[:, 0, :], st[:]))
                P.wait()
                pool.tensor_tensor(sth[:, 1, :], st[:], sth[:, 0, :], ALU.subtract).then_inc(done, 1)

            def rstd_a(n):
                pool.wait_ge(a_vs, n + 1)
                PA.start(n)
                rstd(PA, st_a, sth_a, a_rs)

            def rstd_b(n):
                pool.wait_ge(b_vs, n + 1)
                PB.start(n)
                rstd(PB, st_b, sth_b, b_rs)

            def rstd_c(n, r):
                pool.wait_ge(c_vs, 2 * n + r + 1)
                PC.start(n, 2 * r)
                rstd(PC, st_c, sth_c, c_rs)

            def round_(r, parity):
                for k in range(SUB):
                    if x := due(r, parity, k, 0, SUB - 1):
                        pool_stage_a(x[0], x[1])
                    if x := due(r, parity, k, -6, -6):
                        rstd_a(x[0])
                    x = due(r, parity, k, B_FROM, B_FROM + len(PARTS_B) - 1)
                    if x and 1 in PARTS_B[x[1] - B_FROM]:
                        rstd_b(x[0])
                    x = due(r, parity, k, C_FROM, C_FROM + len(PARTS_C) - 1)
                    if x and 25 in PARTS_C[x[1] - C_FROM]:
                        rstd_c(x[0], 0)
                    if x and 39 in PARTS_C[x[1] - C_FROM]:
                        rstd_c(x[0], 1)
                    if x := due(r, parity, k, 56, 63):
                        scatter(x[0], x[1] - 56)

            rounds(pool, round_)

            def send(t, i):
                pool.wait_ge(yo_done, t + 1)
                alone(pool)
                pool.indirect_dma_start(out=y_d, out_offset=bass.IndirectOffsetOnAxis(ap=dst[i][:, 0:1], axis=0),
                                        in_=yo[i][:], in_offset=None, bounds_check=2 * T - 1, oob_is_err=False).then_inc(y_out[i], 16)

            with pool.Fori(0, NTILE // NB2) as g:
                t = g * NB2
                for i in range(NB2):
                    send(t + i, i)

        @block.tensor
        def _(pe):
            mm = pe.matmul

            pe.wait_ge(w_qk, 64)
            wq = raw[0:E, 0:1024].rearrange("d (h i) -> d h i", h=HEADS)
            wk = raw[0:E, 1024:2048].rearrange("d (h i) -> d h i", h=HEADS)
            for h in range(HEADS):
                last = mm(ps_s[h // 4][:, 128 * (h % 4):128 * (h % 4) + 128], wq[:, h], wk[:, h], start=True, stop=True)
                if h % 4 == 3:
                    last.then_inc(g_mm, 1)
            pe.wait_ge(w_vo, 48)
            wo = raw[0:E, 1024:1024 + HEADS * E].rearrange("d (h e) -> d h e", h=HEADS)
            for h in range(HEADS):
                last = mm(ps_u[:, E * h:E * h + E], wq[:, h], wo[:, h], start=True, stop=True)
            last.then_inc(g_mm, 1)
            pe.wait_ge(prep, 3)
            for e in range(X0):
                last = mm(ps_t[0:2 * X0, 0:E], b1diag[:, e, :], w2s[:, e, :], start=e == 0, stop=e == X0 - 1)
            last.then_inc(bias_mm, 1)
            pe.wait_ge(consts, CONSTS)
            pe.wait_ge(w_emb, 64)
            pe.wait_ge(prep, PREP)
            pe.wait_ge(g_lo, 3)

            def embed(n, part):
                if part == 0:
                    pe.wait_ge(x_in, 16 * 2 * CH * (n + 1))
                    if not first_pairs(n, 4):
                        pe.wait_ge(ranked_done, n - 3)
                    elif n >= 1:
                        pe.wait_ge(h_ready, n)
                for px in range(2 * part, 2 * part + 2):
                    last = mm(ps_c[:, 0:L], tokw[0:64 + KR, px, :],
                              xin[0:64 + KR].rearrange("p a (b q) -> p a b q", q=PATCH)[:, :, :, px],
                              start=px == 0, stop=px == PATCH - 1)
                if part == 7:
                    last.then_inc(emb_done, 1)

            def centered(dest, h):
                mm(dest[:, 0:L], center[0][:], h, start=True, stop=True)
                return mm(dest[:, L:2 * L], center[1][:], h, start=True, stop=True)

            def variances(dest, sq, at=0):
                for c in range(4):
                    last = mm(dest[0:LB, at + c:at + c + 1], sq[:, LB * c:LB * c + LB], average[:, 0:1], start=True, stop=True)
                return last

            def spread(dest, sth):
                for c in range(4):
                    for part in range(2):
                        end = mm(dest[:, LB * c:LB * c + LB], sth[:, part, c:c + 1].to_broadcast([LB, 128]), ident16[:],
                                 start=part == 0, stop=part == 1)
                return end

            def start_a(n, step):
                X, Y = ps_b
                if step == 0:
                    pe.wait_ge(h_ready, n + 1)
                    centered(X, h_a[:]).then_inc(a_cen, 1)
                if step == 1:
                    pe.wait_ge(a_sq, n + 1)
                    if not first_pairs(n, 3):
                        pe.wait_ge(h2_done, n - 2)
                    variances(Y, sq_a).then_inc(a_var, 1)
                if step == 2:
                    pe.wait_ge(a_rs, n + 1)
                    spread(Y, sth_a).then_inc(a_rb, 1)

            last = {"u": None, "gate": None, "t": None, "v": None}

            def shared(sem_, kind):
                if last[kind] is not None:
                    pe.wait_ge(sem_, last[kind])

            def v_step(n, c, q):
                shared(t_evac, "t")
                shared(v_evac, "v")
                if c == 0:
                    pe.wait_ge(a_x, n + 1)
                mm(ps_t[0:LB, :], xh_a[q][:, LB * c:LB * c + LB], v16[:], start=True, stop=False)
                mm(ps_t[0:LB, :], xl_a[q][:, LB * c:LB * c + LB], v16[:], start=False, stop=True).then_inc(v_mm, 1)
                last["v"] = 4 * n + c + 1

            def u_step(n, h, q):
                if h == 0:
                    pe.wait_ge(a_x, n + 1)
                shared(u_lo, "u")
                shared(gate_sb, "gate")
                mm(ps_u[:, 0:2 * L], g16[:, h, :], xh_a[q][:], start=True, stop=False)
                mm(ps_u[:, 0:2 * L], g16[:, h, :], xl_a[q][:], start=False, stop=True).then_inc(u_mm, 1)
                last["u"] = HEADS * n + h + 1

            def s_step(n, k, q):
                h, img = k // 2, k % 2
                pe.wait_ge(u_lo, HEADS * n + h + 1)
                if k >= 2 or not first_pairs(n, 1):
                    pe.wait_ge(e1_done, SUB * n + k - 1)
                u, sl = us[h % 2], slice(img * L, img * L + L)
                for b in range(2):
                    uu = u[:, img * L + LB * b:img * L + LB * b + LB]
                    mm(ps_s[k % 2][0:LB, L * b:L * b + L], uu, xh_a[q][:, sl], start=True, stop=False)
                    end = mm(ps_s[k % 2][0:LB, L * b:L * b + L], uu, xl_a[q][:, sl], start=False, stop=True)
                end.then_inc(s_mm, 1)

            def t_step(n, k):
                pe.wait_ge(p2_done, SUB * n + k + 1)
                shared(v_evac, "v")
                shared(t_evac, "t")
                for c in range(3):
                    end = pe.transpose(ps_t[0:LB, LB * c:LB * c + LB], p2[k % NA][:, LB * c:LB * c + LB], ident[0:LB, 0:LB])
                end.then_inc(t_mm, 1)
                last["t"] = SUB * n + k + 1

            def pv_step(n, k, q):
                h, img = k // 2, k % 2
                pe.wait_ge(t_evac, SUB * n + k + 1)
                if k == 0:
                    if not (isinstance(n, int) and n == 0):
                        pe.wait_ge(hb_ready, n)
                    mm(ps_o[:, 0:L], ident[:], h_a[:], start=True, stop=False, skip_group_check=True)
                o = ps_o[64 * img:64 * img + E]
                mm(o[:, 0:L], vt[q][:, 2 * img, E * h:E * h + E], pt[k % NA][:, 0:L], start=False, stop=False,
                   skip_group_check=True)
                mm(o[:, LB:L], vt[q][:, 2 * img + 1, E * h:E * h + E], pt[k % NA][:, L:L + LB], start=False,
                   stop=h == HEADS - 1, skip_group_check=True).then_inc(pv_mm, 1)

            def stage_b(n, j):
                X, Y = ps_b
                if j == 0:
                    pe.wait_ge(hb_ready, n + 1)
                    pe.wait_ge(a_cs, most(n + 3, NPAIR))
                    centered(X, h_b[:]).then_inc(b_cen, 1)
                if j == 1:
                    pe.wait_ge(b_sq, n + 1)
                    pe.wait_ge(a_x, most(n + 3, NPAIR))
                    variances(Y, sq_b).then_inc(b_var, 1)
                if j == 3:
                    pe.wait_ge(b_rs, n + 1)
                    spread(Y, sth_b).then_inc(b_rb, 1)
                if j == 5:
                    pe.wait_ge(b_x, n + 1)
                    for c in range(4):
                        mm(X[0:LB, X0 * c:X0 * c + X0], xh_b[:, LB * c:LB * c + LB], wg16[:], start=True, stop=False)
                        end = mm(X[0:LB, X0 * c:X0 * c + X0], xl_b[:, LB * c:LB * c + LB], wg16[:], start=False, stop=True)
                    end.then_inc(g0_mm, 1)
                if j == 9:
                    pe.wait_ge(comb_done, n + 1)
                    for c in range(4):
                        end = mm(Y[0:2 * X0, LB * c:LB * c + LB], comb16[:, c, :], ident16[:], start=True, stop=True)
                    end.then_inc(cT_mm, 1)
                if j == 12:
                    pe.wait_ge(cT_sb, n + 1)
                    mm(Y[:, 0:L], ident[:], h_b[:], start=True, stop=False, skip_group_check=True).then_inc(hb_used, 1)
                    for img in range(2):
                        mm(Y[64 * img:64 * img + E, 0:L], b2p[:], combT[:, img * L:img * L + L], start=False, stop=False,
                           skip_group_check=True)
                if 12 <= j < 12 + X0:
                    e = j - 12
                    shared(u_lo, "u")
                    if e >= 1:
                        pe.wait_ge(gate_sb, X0 * n + e)
                    mm(ps_u[:, 0:2 * L], pick[:, e, :], combT16[:], start=True, stop=True).then_inc(gate_mm, 1)
                    last["gate"] = X0 * n + e + 1
                if 13 <= j <= 13 + X0:
                    e = j - 13
                    if e >= 1:
                        pe.wait_ge(hid_done, X0 * n + e)
                        for img in range(2):
                            end = mm(Y[64 * img:64 * img + E, 0:L], w2s[:, e - 1, :], hid[(e - 1) % 2][:, img * L:img * L + L],
                                      start=False, stop=e == X0, skip_group_check=True)
                        end.then_inc(y_mm, 1)
                    if e < X0:
                        mm(X[:, 0:2 * L], w116[:, HID * e:HID * e + HID], xh_b[:], start=True, stop=False)
                        mm(X[:, 0:2 * L], w116[:, HID * e:HID * e + HID], xl_b[:], start=False, stop=True).then_inc(z_mm, 1)

            def stage_c(n, j):
                Z, VAR = ps_c, 2 * L
                if j in (22, 36):
                    if j == 22:
                        pe.wait_ge(h2_done, n + 1)
                        pe.wait_ge(h_ready, most(n + 4, NPAIR))
                    else:
                        pe.wait_ge(h3_done, n + 1)
                    centered(Z, h_c[:]).then_inc(c_cen, 1)
                if j in (24, 38):
                    pe.wait_ge(c_cs, 2 * n + (j == 38) + 1)
                    variances(Z, sq_c, VAR).then_inc(c_var, 1)
                if j in (26, 41):
                    pe.wait_ge(c_rs, 2 * n + (j == 41) + 1)
                    spread(Z, sth_c).then_inc(c_rb, 1)
                if j == 29:
                    pe.wait_ge(c_x, 2 * n + 1)
                    mm(Z[:, 0:2 * L], qw16[:], xh_c[:], start=True, stop=False)
                    mm(Z[:, 0:2 * L], qw16[:], xl_c[:], start=False, stop=True).then_inc(q_mm, 1)
                if j in (31, 32):
                    img = j - 31
                    pe.wait_ge(q_lo, n + 1)
                    if img == 1:
                        pe.wait_ge(th_done, 2 * n + 1)
                    for c in range(2):
                        s = slice(img * L + LB * c, img * L + LB * c + LB)
                        mm(Z[0:LB, L * c:L * c + L], xh_c[:, s], q16[:, img * L:img * L + L], start=True, stop=False)
                        end = mm(Z[0:LB, L * c:L * c + L], xl_c[:, s], q16[:, img * L:img * L + L], start=False, stop=True)
                    end.then_inc(s3_mm, 1)
                if j == 33:
                    pe.wait_ge(th_done, 2 * n + 2)
                    alone(pe)
                    for c in range(4):
                        end = pe.transpose(Z[0:LB, E * c:E * c + E], xf_c[0:E, LB * c:LB * c + LB], ident[0:E, 0:E])
                    end.then_inc(x3_mm, 1)
                if j == 34:
                    pe.wait_ge(x3_sb, n + 1)
                    for img in range(2):
                        for c in range(2):
                            end = mm(Z[64 * img:64 * img + E, 0:L], x3t[:, 2 * img + c, :], th[img][:, L * c:L * c + L],
                                      start=c == 0, stop=c == 1)
                    end.then_inc(val_mm, 1)
                if j == 44:
                    pe.wait_ge(c_x, 2 * n + 2)
                    alone(pe)
                    for c in range(4):
                        pe.transpose(Z[0:LB, 256 + E * c:256 + E * c + E], xf_c[0:E, LB * c:LB * c + LB], ident[0:E, 0:E])
                    for b in range(2):
                        end = pe.transpose(Z[0:LB, 128 * b:128 * b + 128], h_c[:, LB * b:LB * b + LB], ident[:])
                    end.then_inc(h3T_mm, 1)
                if j == 51:
                    pe.wait_ge(h3T_sb, n + 1)
                    for c in range(4):
                        mm(Z[0:LB, X1 * c:X1 * c + X1], xh_c[:, LB * c:LB * c + LB], wr16[:], start=True, stop=False)
                        end = mm(Z[0:LB, X1 * c:X1 * c + X1], xl_c[:, LB * c:LB * c + LB], wr16[:], start=False, stop=True)
                    end.then_inc(g1_mm, 1)
                if j == 54:
                    pe.wait_ge(chosen_done, n + 1)
                    if not (isinstance(n, int) and n == 0):
                        pe.wait_ge(rows_done, n)
                    for c in range(4):
                        o = Z[0:LB, X1 * c:X1 * c + X1]
                        mm(o, ones16[0:LB, 0:LB], seen16[:], start=True, stop=False)
                        for d in range(c):
                            mm(o, ones16[0:LB, 0:LB], chosen[:, d, :], start=False, stop=False)
                        end = mm(o, before[0:LB, 0:LB], chosen[:, c, :], start=False, stop=True)
                    end.then_inc(rank_mm, 1)

            def round_(r, parity):
                def stands(n, top):
                    return None if isinstance(n, int) and n <= 0 else most(n, top)
                begun = not (isinstance(r, int) and r < 0)
                last["u"] = stands(HEADS * r + 2, HEADS * NPAIR) if begun else None
                last["v"] = stands(4 * r + 1, 4 * NPAIR) if begun else None
                last["t"] = stands(SUB * r - 3, SUB * NPAIR) if begun else None
                last["gate"] = stands(X0 * (r - 2), X0 * NPAIR) if begun else None
                for k in range(SUB):
                    for op in ORD_PE:
                        first, to = {"S": (-1, 14), "U": (-3, 11), "V": (-1, 2), "T": (3, 18), "P": (4, 19), "E": (-10, -8), "N": (-7, -5)}.get(
                            op, (B_FROM, B_FROM + len(PARTS_B) - 1) if op in "bcd" else (C_FROM, C_FROM + len(PARTS_C) - 1))
                        x = due(r, parity, k, first, to)
                        if x is None:
                            continue
                        n, at, q = x
                        if op == "S":
                            s_step(n, at + 1, q)
                        elif op == "U" and at % 2:
                            u_step(n, (at + 3) // 2, q)
                        elif op == "V":
                            v_step(n, at + 1, q)
                        elif op == "T":
                            t_step(n, at - 3)
                        elif op == "P":
                            pv_step(n, at - 4, q)
                        elif op == "E":
                            for part in ((0, 1, 2), (3, 4, 5), (6, 7))[at + 10]:
                                embed(n, part)
                        elif op == "N":
                            start_a(n, at + 7)
                        elif op in "bcd" and "bcd".index(op) < len(PARTS_B[at - B_FROM]):
                            stage_b(n, PARTS_B[at - B_FROM]["bcd".index(op)])
                        elif op in "CBD" and "CBD".index(op) < len(PARTS_C[at - C_FROM]):
                            stage_c(n, PARTS_C[at - C_FROM]["CBD".index(op)])

            rounds(pe, round_)

            pe.wait_ge(rows_done, NPAIR)
            mm(ps_b[0][0:X1, 0:LB], seen16[:], ones16[0:LB, 0:LB], start=True, stop=True)
            mm(ps_b[1][0:1, 0:X1], ones16[0:LB, 0:1], seen16[:], start=True, stop=True).then_inc(cnt_mm, 1)
            pe.wait_ge(cum_in, 1)
            mm(ps_u[0:X1, 0:1], upto[:], ntl[:], start=True, stop=True).then_inc(cum_mm, 1)
            pe.wait_ge(past_in, 1)
            mm(ps_s[0][0:1, 0:NTILE], skip[:], past[:], start=True, stop=True)
            mm(ps_s[1][0:1, 0:NTILE], onesf[0:X1, 0:1], past[:], start=True, stop=True).then_inc(meta_mm, 1)
            pe.wait_ge(meta_done, 1)

            def x_step(t, i):
                pe.wait_ge(x_tile[i % NB2], (t - i) * (16 // NB2) + 16)
                if not (isinstance(t, int) and t < 2):
                    pe.wait_ge(xT_sb, t - 1)
                alone(pe)
                pe.transpose(ps_s[i % 2][0:E, 0:TILE], xr[i][:, 0:E], ident[:]).then_inc(xT_mm, 1)

            def z_step(t, i):
                pe.wait_ge(w_tile[i], (t - i) * (16 // NB2) + 16)
                pe.wait_ge(xT_sb, t + 1)
                if not (isinstance(t, int) and t < 2):
                    pe.wait_ge(hT_sb, t - 1)
                mm(ps_b[i % 2][:, 0:TILE], wt[i][:, 0:HID], xT[i % 2][:], start=True, stop=True).then_inc(zt_mm, 1)

            def y_step(t, i):
                pe.wait_ge(hT_sb, t + 1)
                if not (isinstance(t, int) and t < 2):
                    pe.wait_ge(yo_done, t - 1)
                o = [ps_u, ps_t][i % 2][:, 0:E]
                mm(o, hT[i % 2][:], wt[i][:, HID:HID + E], start=True, stop=False)
                mm(o, b2_row[:], wt[i][:, 0:E], start=False, stop=True).then_inc(yt_mm, 1)

            for t in range(2 * NB2):
                x_step(t, t % NB2)
                if t >= 1:
                    z_step(t - 1, (t - 1) % NB2)
                if t >= 2:
                    y_step(t - 2, (t - 2) % NB2)
            with pe.Fori(2, NTILE // NB2) as g:
                t = g * NB2
                for i in range(NB2):
                    x_step(t + i, i)
                    z_step(t + i - 1, (i - 1) % NB2)
                    y_step(t + i - 2, (i - 2) % NB2)
            z_step(NTILE - 1, NB2 - 1)
            y_step(NTILE - 2, NB2 - 2)
            y_step(NTILE - 1, NB2 - 1)

        @block.scalar
        def _(act):
            def copy(dest, src, scale=1.0):
                return act.activation(dest, src, ACT.Copy, scale=scale)

            for g in range(2):
                act.wait_ge(g_mm, g + 1)
                copy(g16[:, 4 * g:4 * g + 4, :].rearrange("p h i -> p (h i)"), ps_s[g][:], E ** -0.5).then_inc(g_hi, 1)
            act.wait_ge(g_mm, 3)
            copy(v16[:], ps_u[:], SC_V).then_inc(g_hi, 1)
            act.wait_ge(consts, CONSTS)
            act.wait_ge(w_emb, 64)

            def start_a(n, step):
                X, Y = ps_b
                if step == 0:
                    act.wait_ge(a_cen, n + 1)
                    act.activation(sq_a[:], X[:, 0:2 * L], ACT.Square).then_inc(a_sq, 1)
                    if not first_pairs(n, 1):
                        act.wait_ge(a_x, n)
                    copy(xf_a[:], X[:, 0:2 * L]).then_inc(a_cs, 1)
                if step == 1:
                    act.wait_ge(a_var, n + 1)
                    act.activation(st_a[:], Y[0:LB, 0:4], ACT.Identity, bias=eps[0:LB, 0:1]).then_inc(a_vs, 1)

            def embedded(n):
                act.wait_ge(emb_done, n + 1)
                if not first_pairs(n, 1):
                    act.wait_ge(pv_mm, SUB * n - (SUB - 1))
                act.activation(h_a[:], ps_c[:, 0:L], ACT.Identity, bias=tokbias[:, 0:1]).then_inc(h_ready, 1)

            def v_out(n, c, q):
                act.wait_ge(v_mm, 4 * n + c + 1)
                copy(vt[q][:, c, :], ps_t[0:LB, :], 1.0 / SC_V).then_inc(v_evac, 1)

            def sum_out(n):
                act.wait_ge(pv_mm, SUB * (n + 1))
                if not first_pairs(n, 1):
                    act.wait_ge(hb_used, n)
                copy(h_b[:], ps_o[:, 0:L]).then_inc(hb_ready, 1)

            def u_hi_step(n, h):
                act.wait_ge(u_mm, HEADS * n + h + 1)
                copy(us[h % 2][:], ps_u[:, 0:2 * L]).then_inc(u_hi, 1)

            def exp1(n, k):
                act.wait_ge(max_done, SUB * n + k + 1)
                if not (isinstance(n, int) and n == 0 and k < NA):
                    act.wait_ge(e2_done, SUB * n + k - NA + 1)
                for b in range(2):
                    last = act.activation(e1[k % NA][:, b, :], ps_s[k % 2][0:LB, L * b:L * b + L], ACT.Exp,
                                          bias=nmax[k % NA][:, b:b + 1], accum_out=sum1[k % NA][:, b:b + 1])
                last.then_inc(e1_done, 1)

            def exp2(n, k):
                act.wait_ge(mask_done, SUB * n + k + 1)
                act.wait_ge(r1_done, SUB * n + k + 1)
                if not (isinstance(n, int) and n == 0 and k < NA):
                    act.wait_ge(t_mm, SUB * n + k - NA + 1)
                for b in range(2):
                    last = act.activation(p2[k % NA][:, LB * b:LB * b + LB * (b + 1)], e1[k % NA][:, b, 0:LB * (b + 1)],
                                          ACT.Exp, scale=rin1[k % NA][:, b:b + 1], accum_out=sum2[k % NA][:, b:b + 1])
                last.then_inc(e2_done, 1)

            def t_out(n, k):
                act.wait_ge(t_mm, SUB * n + k + 1)
                if not (isinstance(n, int) and n == 0 and k < NA):
                    act.wait_ge(pv_mm, SUB * n + k - NA + 1)
                copy(pt[k % NA][:], ps_t[0:LB, 0:3 * LB]).then_inc(t_evac, 1)

            def stage_b(n, j):
                X, Y = ps_b
                if j == 0:
                    act.wait_ge(b_cen, n + 1)
                    act.activation(sq_b[:], X[:, 0:2 * L], ACT.Square).then_inc(b_sq, 1)
                    if not (isinstance(n, int) and n == 0):
                        act.wait_ge(b_x, n)
                    copy(xf_b[:], X[:, 0:2 * L]).then_inc(b_cs, 1)
                if j == 1:
                    act.wait_ge(b_var, n + 1)
                    act.activation(st_b[:], Y[0:LB, 0:4], ACT.Identity, bias=eps[0:LB, 0:1]).then_inc(b_vs, 1)
                if j == 7:
                    act.wait_ge(g0_dif, n + 1)
                    act.activation(edif[:], dif[:], ACT.Exp).then_inc(g0_exp, 1)
                if j == 10:
                    act.wait_ge(cT_mm, n + 1)
                    copy(combT16[:], Y[0:2 * X0, 0:2 * L])
                    copy(combT[:], Y[0:2 * X0, 0:2 * L]).then_inc(cT_sb, 1)
                if 12 <= j < 12 + X0:
                    e = j - 12
                    act.wait_ge(gate_mm, X0 * n + e + 1)
                    if e >= 2:
                        act.wait_ge(hid_done, X0 * n + e - 1)
                    copy(gate[e % 2][:], ps_u[:, 0:2 * L]).then_inc(gate_sb, 1)

            def stage_c(n, j):
                Z, VAR = ps_c, 2 * L
                if j in (23, 37):
                    act.wait_ge(c_cen, 2 * n + (j == 37) + 1)
                    act.activation(sq_c[:], Z[:, 0:2 * L], ACT.Square)
                    if not (isinstance(n, int) and n == 0 and j == 23):
                        act.wait_ge(c_x, 2 * n + (j == 37))
                    copy(xf_c[:], Z[:, 0:2 * L]).then_inc(c_cs, 1)
                if j in (25, 39):
                    act.wait_ge(c_var, 2 * n + (j == 39) + 1)
                    act.activation(st_c[:], Z[0:LB, VAR:VAR + 4], ACT.Identity, bias=eps[0:LB, 0:1]).then_inc(c_vs, 1)
                if j == 30:
                    act.wait_ge(q_mm, n + 1)
                    copy(q16[:], Z[:, 0:2 * L]).then_inc(q_hi, 1)
                if j in (31, 32):
                    img = j - 31
                    act.wait_ge(s3_mm, 2 * n + img + 1)
                    act.activation(th[img][:], Z[0:LB, 0:2 * L], ACT.Tanh, scale=0.5).then_inc(th_done, 1)
                if j == 33:
                    act.wait_ge(x3_mm, n + 1)
                    copy(x3t[:].rearrange("p c e -> p (c e)"), Z[0:LB, 0:4 * E]).then_inc(x3_sb, 1)
                if j == 45:
                    act.wait_ge(h3T_mm, n + 1)
                    if not (isinstance(n, int) and n == 0):
                        act.wait_ge(rows_out, 16 * 8 * n)
                    src = Z[0:LB, 256:512].rearrange("p (c e) -> p c e", e=E)
                    for choice in range(2):
                        copy(rows[:].rearrange("p (c o) r -> p c o r", o=2)[:, :, choice, 0:E], src)
                    for img in range(2):
                        at = 4 * n + 2 * img
                        dest = hres[:, at:at + 2, :] if isinstance(n, int) else hres[:, bass.ds(at, 2), :]
                        last = copy(dest, Z[0:LB, 0:256].rearrange("p (b i e) -> p i b e", b=2, i=2)[:, img])
                    last.then_inc(h3T_sb, 1)
                if j == 53:
                    act.wait_ge(g1_dif, n + 1)
                    act.activation(edif[:], dif[:], ACT.Exp).then_inc(g1_exp, 1)

            def round_(r, parity):
                for k in range(SUB):
                    for op in ORD_ACT:
                        first, to = {"e": (0, 15), "x": (1, 16), "u": (-2, 12), "v": (-1, 2), "t": (4, 19), "h": (-8, -8), "H": (19, 19), "N": (-7, -6)}.get(
                            op, (B_FROM, B_FROM + len(PARTS_B) - 1) if op in "bcd" else (C_FROM, C_FROM + len(PARTS_C) - 1))
                        x = due(r, parity, k, first, to)
                        if x is None:
                            continue
                        n, at, q = x
                        if op == "e":
                            exp1(n, at)
                        elif op == "x":
                            exp2(n, at - 1)
                        elif op == "u" and at % 2 == 0:
                            u_hi_step(n, (at + 2) // 2)
                        elif op == "v":
                            v_out(n, at + 1, q)
                        elif op == "t":
                            t_out(n, at - 4)
                        elif op == "h":
                            embedded(n)
                        elif op == "H":
                            sum_out(n)
                        elif op == "N":
                            start_a(n, at + 7)
                        elif op in "bcd" and "bcd".index(op) < len(PARTS_B[at - B_FROM]):
                            stage_b(n, PARTS_B[at - B_FROM]["bcd".index(op)])
                        elif op in "CBD" and "CBD".index(op) < len(PARTS_C[at - C_FROM]):
                            stage_c(n, PARTS_C[at - C_FROM]["CBD".index(op)])

            rounds(act, round_)

            act.wait_ge(fill_known, 1)
            fill(act, 1)

            def h_out(t, i):
                act.wait_ge(zt_mm, t + 1)
                if not (isinstance(t, int) and t < 2):
                    act.wait_ge(yt_mm, t - 1)
                act.activation(hT[i % 2][:], ps_b[i % 2][:, 0:TILE], ACT.Relu).then_inc(hT_sb, 1)

            G = NTILE // NB2

            def experts(first, count):
                alone(act)
                _, ex = nc.values_load_multi_w_load_instructions(metai[0:1, 1, bass.ds(first, count)], engines=[mybir.EngineType.Activation],
                                                                 min_val=0, max_val=X1 - 1,
                                                                 skip_runtime_bounds_check_because="metai's experts are clamped to X1 - 1")
                return ex

            def weights(i, ex):
                alone(act)
                act.dma_start(wt[i % NB2][:], E1W[bass.ds(ex, 1)].rearrange("o d h -> (o d) h")).then_inc(w_tile[i % NB2], 16)

            act.wait_ge(meta_done, 1)
            ex = experts(0, NB2 - 2)
            for i in range(NB2 - 2):
                weights(i, ex[i])
            ex = experts(NB2 - 2, NB2)
            for i in range(NB2):
                h_out(i, i)
                weights(i + NB2 - 2, ex[i])

            def tiles(t, count):
                ex = experts(t + NB2 - 2, count)
                for i in range(count):
                    h_out(t + i, i)
                    weights(i + NB2 - 2, ex[i])

            odd = (G - 2) % 2
            if odd:
                tiles(NB2, NB2)
            with act.Fori(0, (G - 2) // 2) as g:
                tiles(g * (2 * NB2) + (1 + odd) * NB2, 2 * NB2)
            ex = experts(NTILE - 2, 2)
            for i in range(NB2):
                h_out(NTILE - NB2 + i, i)
                if i < 2:
                    weights(i + NB2 - 2, ex[i])

        @block.vector
        def _(dve):
            dve.wait_ge(consts, CONSTS)
            dve.tensor_copy(iota[:], iota_i[:]).then_inc(prep, 1)
            dve.wait_ge(w_misc, 16 * 15)
            dve.tensor_copy(iota_p[:], iota_p_i[:]).then_inc(prep, 1)
            for e in range(X0):
                last = dve.tensor_scalar(b1diag[:, e, :], ident[:, 0:2 * X0], 0.0, None, ALU.mult)
            last.then_inc(d_self, 1)
            dve.wait_ge(d_self, 1)
            for c in range(2):
                last = dve.tensor_copy(b1diag[:].rearrange("p a b -> p (a b)")[:, X0 * c:X0 * c + (X0 - 1) * (2 * X0 + 1) + 1:2 * X0 + 1], b1raw[:])
            last.then_inc(prep, 1)
            dve.wait_ge(bias_mm, 1)
            dve.tensor_scalar(w2s[:].rearrange("p x e -> p (x e)"), w2s[:].rearrange("p x e -> p (x e)"), 1.0 / SC_0, None, ALU.mult).then_inc(prep, 1)
            dve.tensor_scalar(nb1[:], b1raw[:], -SC_0, None, ALU.mult).then_inc(prep, 1)
            dve.tensor_tensor(b2p[:], ps_t[0:2 * X0, 0:E], b2raw[:], ALU.add).then_inc(prep, 1)
            dve.tensor_tensor(bgb[:, 0, :], bgb[:, 0, :], bgb[:, 1, :], ALU.add).then_inc(prep, 1)
            chain = [1]

            def own(ins):
                ins.then_inc(d_self, 1)
                chain[0] += 1
                dve.wait_ge(d_self, chain[0])

            def split(dest, src, scale):
                own(dve.tensor_scalar(dest, src, scale, None, ALU.mult))
                return dve.scalar_tensor_tensor(dest[64:128], src[64:128], scale, dest[64:128], ALU.mult, ALU.subtract)

            split(wg16[:], raw2[:, 0:X0], SC_0).then_inc(prep, 1)
            split(wr16[:], raw2[:, X0:X0 + X1], SC_R).then_inc(prep, 1)
            split(qw16[:], raw2[:, 128:256], 1.0).then_inc(prep, 1)
            for g in range(2):
                dve.wait_ge(g_hi, g + 1)
                d = g16[64:128, 4 * g:4 * g + 4, :].rearrange("p h i -> p (h i)")
                dve.scalar_tensor_tensor(d, ps_s[g][64:128, :], E ** -0.5, d, ALU.mult, ALU.subtract).then_inc(g_lo, 1)
            dve.wait_ge(g_hi, 3)
            dve.scalar_tensor_tensor(v16[64:128], ps_u[64:128], SC_V, v16[64:128], ALU.mult, ALU.subtract).then_inc(g_lo, 1)
            dve.wait_ge(w_rest, 32)
            split(w116[:], raw[:, 0:X0 * HID], SC_0).then_inc(prep, 1)
            own(dve.tensor_scalar(region[:], iota[0:LB, 0:X1], float(CAP), None, ALU.mult))
            for c in range(4):
                for choice in range(2):
                    last = dve.tensor_scalar(place[:, 2 * c + choice:2 * c + choice + 1], iota_p[0:LB], 4.0, float(choice * T + c), ALU.mult, ALU.add)
            own(last)
            for i in range(2):
                own(dve.memset(xT[i][:], 0.0))
                own(dve.memset(xT[i][E:E + 1, :], 1.0))
            XS, A, B, C = Chain(dve, x_self, X_LINKS), Chain(dve, a_self, A_LINKS), Chain(dve, b_self, B_LINKS), Chain(dve, c_self, C_LINKS)

            def u_lo_step(n, h):
                dve.wait_ge(u_hi, HEADS * n + h + 1)
                u = us[h % 2]
                dve.tensor_tensor(u[64:128], ps_u[64:128, 0:2 * L], u[64:128], ALU.subtract).then_inc(u_lo, 1)

            def max_step(n, k):
                dve.wait_ge(s_mm, SUB * n + k + 1)
                dve.tensor_reduce(nmax[k % NA][:], ps_s[k % 2][0:LB, 0:2 * L].rearrange("p (b m) -> p b m", b=2), AX, ALU.max,
                                  negate=True).then_inc(max_done, 1)

            def r1_step(n, k):
                dve.wait_ge(e1_done, SUB * n + k + 1)
                dve.reciprocal(rin1[k % NA][:], sum1[k % NA][:]).then_inc(r1_done, 1)

            def scale_step(n, k):
                dve.wait_ge(e2_done, SUB * n + k + 1)
                A.start(n, k)
                A.add(dve.reciprocal(rin2[k % NA][:], sum2[k % NA][:]))
                A.wait()
                for b in range(2):
                    part = p2[k % NA][:, LB * b:LB * b + LB * (b + 1)]
                    last = dve.tensor_scalar(part, part, rin2[k % NA][:, b:b + 1], None, ALU.mult)
                last.then_inc(p2_done, 1)

            def top2(K, X, dif_sem):
                alone(dve)
                for c in range(4):
                    last = dve.max(mx8[:, c, :], lg[:, c, 0:X])
                K.add(last)
                K.wait()
                dve.tensor_tensor(dif[:], mx8[:, :, 1], mx8[:, :, 0], ALU.subtract).then_inc(dif_sem, 1)
                for c in range(4):
                    last = dve.max_index(ix8[:, c, :], mx8[:, c, :], lg[:, c, 0:X])
                K.add(last)
                K.wait()
                K.add(dve.tensor_copy(ixf[:].rearrange("p (c o) -> p c o", o=2), ix8[:, :, 0:2]))
                K.wait()
                K.add(dve.tensor_tensor(onehot[:, :, 0:X], iota[0:LB, 0:X].unsqueeze(1).to_broadcast([LB, 8, X]),
                                        ixf[:].unsqueeze(2).to_broadcast([LB, 8, X]), ALU.is_equal))
                K.wait()

            def gate_weights(K):
                K.add(dve.tensor_scalar(eone[:], edif[:], 1.0, None, ALU.add))
                K.wait()
                K.add(dve.reciprocal(gates[:, :, 0], eone[:]))
                K.wait()
                K.add(dve.tensor_tensor(gates[:, :, 1], edif[:], gates[:, :, 0], ALU.mult))
                K.wait()

            def normal(K, st, cs, rb, xf, xh, xl, count, done):
                dve.wait_ge(cs, count)
                dve.wait_ge(rb, count)
                K.add(dve.tensor_tensor(xf[:], st[:, 0:2 * L], xf[:], ALU.mult))
                K.wait()
                K.add(dve.tensor_copy(xh[:], xf[:]))
                K.wait()
                dve.tensor_tensor(xl[:], xf[:], xh[:], ALU.subtract).then_inc(done, 1)

            def start_a(n, q):
                XS.start(n)
                normal(XS, ps_b[1], a_cs, a_rb, xf_a, xh_a[q], xl_a[q], n + 1, a_x)

            def stage_b(n, j):
                X, Y = ps_b
                B.start(n, {4: 0, 6: 2, 8: 7}.get(j, 0))
                if j == 4:
                    normal(B, Y, b_cs, b_rb, xf_b, xh_b, xl_b, n + 1, b_x)
                if j == 6:
                    dve.wait_ge(g0_mm, n + 1)
                    B.add(dve.scalar_tensor_tensor(lg[:, :, 0:X0], X[0:LB, 0:4 * X0].rearrange("p (c x) -> p c x", x=X0),
                                                   1.0 / SC_0, bgb[:, 0:1, :].to_broadcast([LB, 4, X0]), ALU.mult, ALU.add))
                    B.wait()
                    top2(B, X0, g0_dif)
                if j == 8:
                    dve.wait_ge(g0_exp, n + 1)
                    gate_weights(B)
                    B.add(dve.tensor_tensor(weighed[:, :, 0:X0], onehot[:, :, 0:X0],
                                            gates[:].rearrange("p c o -> p (c o)").unsqueeze(2).to_broadcast([LB, 8, X0]), ALU.mult))
                    B.wait()
                    w = weighed[:].rearrange("p (c o) x -> p c o x", o=2)
                    B.add(dve.tensor_tensor(comb[:], w[:, :, 0, 0:X0], w[:, :, 1, 0:X0], ALU.add))
                    B.wait()
                    B.add(dve.tensor_copy(comb16[:, :, 0:X0], comb[:]))
                    B.wait()
                    dve.tensor_tensor(comb16[:, :, X0:2 * X0], comb[:], comb16[:, :, 0:X0], ALU.subtract).then_inc(comb_done, 1)
                    B.end()
                if 13 <= j < 13 + X0:
                    e = j - 13
                    dve.wait_ge(z_mm, X0 * n + e + 1)
                    dve.wait_ge(gate_sb, X0 * n + e + 1)
                    if e >= 2:
                        dve.wait_ge(y_mm, X0 * n + e - 1)
                    dve.scalar_tensor_tensor(hid[e % 2][:], X[:, 0:2 * L], nb1[:, e:e + 1], gate[e % 2][:], ALU.max, ALU.mult).then_inc(hid_done, 1)
                if j == 21:
                    dve.wait_ge(y_mm, X0 * n + X0)
                    if not (isinstance(n, int) and n == 0):
                        dve.wait_ge(h3T_mm, n)
                    dve.tensor_copy(h_c[:], Y[:, 0:L]).then_inc(h2_done, 1)

            def stage_c(n, j):
                Z = ps_c
                C.start(n, {28: 0, 30: 2, 35: 3, 43: 4, 52: 6, 55: 11, 48: 15, 49: 18}.get(j, 0))
                if j in (28, 43):
                    normal(C, Z, c_cs, c_rb, xf_c, xh_c, xl_c, 2 * n + (j == 43) + 1, c_x)
                if j == 30:
                    dve.wait_ge(q_hi, n + 1)
                    dve.tensor_tensor(q16[64:128], Z[64:128, 0:2 * L], q16[64:128], ALU.subtract).then_inc(q_lo, 1)
                    for img in range(2):
                        sl = slice(64 * img, 64 * img + 64)
                        last = dve.reduce_sum(colsum[sl, 0:1], xf_c[sl, img * L:img * L + L], AX)
                    C.add(last)
                if j == 35:
                    C.wait()
                    dve.wait_ge(val_mm, n + 1)
                    C.add(dve.tensor_scalar(half[:], Z[:, 0:L], colsum[:, 0:1], 0.5, ALU.add, ALU.mult))
                    C.wait()
                    dve.tensor_tensor(h_c[:], half[:], h_c[:], ALU.add).then_inc(h3_done, 1)
                if j == 52:
                    dve.wait_ge(g1_mm, n + 1)
                    C.add(dve.scalar_tensor_tensor(lg[:], Z[0:LB, 0:4 * X1].rearrange("p (c x) -> p c x", x=X1),
                                                   1.0 / SC_R, brb[:].unsqueeze(1).to_broadcast([LB, 4, X1]), ALU.mult, ALU.add))
                    C.wait()
                    top2(C, X1, g1_dif)
                    oh = onehot[:].rearrange("p (c o) x -> p c o x", o=2)
                    dve.tensor_tensor(chosen[:], oh[:, :, 0, :], oh[:, :, 1, :], ALU.add).then_inc(chosen_done, 1)
                if j == 55:
                    dve.wait_ge(g1_exp, n + 1)
                    gate_weights(C)
                    dve.wait_ge(h3T_sb, n + 1)
                    dve.tensor_copy(rows[:, :, E:E + 1], gates[:].rearrange("p c o -> p (c o)").unsqueeze(2))
                    C.add(dve.tensor_copy(rows[:, :, E + 1:E + 2], place[:].unsqueeze(2)))
                    dve.wait_ge(rank_mm, n + 1)
                    dve.tensor_tensor(ranked[:], Z[0:LB, 0:4 * X1].rearrange("p (c x) -> p c x", x=X1),
                                      region[:].unsqueeze(1).to_broadcast([LB, 4, X1]), ALU.add).then_inc(ranked_done, 1)
                if j == 48:
                    dve.wait_ge(ranked_done, n + 1)
                    C.add(dve.tensor_tensor(weighed[:].rearrange("p (c o) x -> p c o x", o=2), onehot[:].rearrange("p (c o) x -> p c o x", o=2),
                                            ranked[:].unsqueeze(2).to_broadcast([LB, 4, 2, X1]), ALU.mult))
                    C.add(dve.reduce_sum(added[:], chosen[:].rearrange("p c x -> p x c"), AX))
                    C.wait()
                    C.add(dve.reduce_sum(posf[:], weighed[:], AX))
                if j == 49:
                    C.wait()
                    C.add(dve.tensor_tensor(seen[:], seen[:], added[:], ALU.add))
                    C.add(dve.tensor_copy(posi[:], posf[:]))
                    C.add(dve.tensor_scalar(place[:], place[:], 4.0 * LB, None, ALU.add))
                    C.wait()
                    dve.tensor_copy(seen16[:], seen[:]).then_inc(rows_done, 1)
                    C.end()

            def round_(r, parity):
                for k in range(SUB):
                    for op in ORD_DVE:
                        first, to = {"m": (-1, 14), "r": (0, 15), "s": (2, 17), "u": (-2, 12), "N": (-4, -4)}.get(
                            op, (B_FROM, B_FROM + len(PARTS_B) - 1) if op in "bcd" else (C_FROM, C_FROM + len(PARTS_C) - 1))
                        x = due(r, parity, k, first, to)
                        if x is None:
                            continue
                        n, at, q = x
                        if op == "m":
                            max_step(n, at + 1)
                        elif op == "r":
                            r1_step(n, at)
                        elif op == "s":
                            scale_step(n, at - 2)
                        elif op == "u" and at % 2 == 0:
                            u_lo_step(n, (at + 2) // 2)
                        elif op == "N":
                            start_a(n, q)
                        elif op in "bcd" and "bcd".index(op) < len(PARTS_B[at - B_FROM]):
                            stage_b(n, PARTS_B[at - B_FROM]["bcd".index(op)])
                        elif op in "CBD" and "CBD".index(op) < len(PARTS_C[at - C_FROM]):
                            stage_c(n, PARTS_C[at - C_FROM]["CBD".index(op)])

            rounds(dve, round_)

            dve.wait_ge(cnt_mm, 1)
            own(dve.tensor_tensor(fillf[:], ps_b[1][0:1, 0:X1], region[0:1, :], ALU.add))
            dve.tensor_copy(filli[:], fillf[:]).then_inc(fill_known, 1)
            own(dve.tensor_copy(cnt[:], ps_b[0][0:X1, 0:1]))
            own(dve.tensor_scalar(steps[:], iota[0:X1, 0:T // TILE + 1], float(TILE), None, ALU.mult))
            own(dve.tensor_scalar(less[:], steps[:], cnt[:, 0:1], None, ALU.is_lt))
            dve.reduce_sum(ntl[:], less[:], AX).then_inc(cum_in, 1)
            dve.wait_ge(cum_in, 1)
            own(dve.tensor_scalar(skip[:], ntl[:], -float(TILE), float(CAP), ALU.mult, ALU.add))
            dve.wait_ge(cum_mm, 1)
            own(dve.tensor_copy(cum[:], ps_u[0:X1, 0:1]))
            dve.tensor_scalar(past[:], iota[0:X1, :], cum[:, 0:1], None, ALU.is_ge).then_inc(past_in, 1)
            dve.wait_ge(meta_mm, 1)
            own(dve.scalar_tensor_tensor(metaf[:, 0, :], iota[0:1, :], float(TILE), ps_s[0][0:1, 0:NTILE], ALU.mult, ALU.add))
            own(dve.tensor_scalar(metaf[:, 0, :], metaf[:, 0, :], float(X1 * CAP), None, ALU.min))
            own(dve.tensor_scalar(metaf[:, 1, :], ps_s[1][0:1, 0:NTILE], float(X1 - 1), None, ALU.min))
            dve.tensor_copy(metai[:], metaf[:]).then_inc(meta_done, 1)

            def x_out(t, i):
                dve.wait_ge(xT_mm, t + 1)
                if not (isinstance(t, int) and t < 2):
                    dve.wait_ge(zt_mm, t - 1)
                dve.tensor_copy(xT[i % 2][0:E], ps_s[i % 2][0:E, 0:TILE]).then_inc(xT_sb, 1)

            def y_rows(t, i):
                dve.wait_ge(yt_mm, t + 1)
                if not (isinstance(t, int) and t < NB2):
                    dve.wait_ge(y_out[i], (t - i) * (16 // NB2))
                dve.tensor_copy(dst[i][:], xr[i][:, E + 1:E + 2])
                dve.tensor_scalar(yo[i][:], [ps_u, ps_t][i % 2][:, 0:E], xr[i][:, E:E + 1], None, ALU.mult).then_inc(yo_done, 1)

            for t in range(2 * NB2):
                x_out(t, t % NB2)
                if t >= 2:
                    y_rows(t - 2, (t - 2) % NB2)
            with dve.Fori(2, NTILE // NB2) as g:
                t = g * NB2
                for i in range(NB2):
                    x_out(t + i, i)
                    y_rows(t + i - 2, (i - 2) % NB2)
            y_rows(NTILE - 2, NB2 - 2)
            y_rows(NTILE - 1, NB2 - 1)

            NS = NBLK // CB

            def finish(s, i, first):
                dve.wait_ge(y_in[i], 16 * (s - i) + 32)
                dve.tensor_tensor(ysum[i][:], yin[i][:, 0], yin[i][:, 1], ALU.add).then_inc(ys_done, 1)
                dve.wait_ge(ys_done, s + 1)
                if not first:
                    dve.wait_ge(fin_out[i], (s - i) * 8)
                src = hres[:, CB * s:CB * s + CB, :] if isinstance(s, int) else hres[:, bass.ds(CB * s, CB), :]
                dve.tensor_tensor(yfin[i][:], ysum[i][:], src, ALU.add).then_inc(fin_done, 1)

            finish(0, 0, True)
            finish(1, 1, True)
            with dve.Fori(0, NS // 2 - 1) as g:
                s = g * 2
                for i in range(2):
                    finish(s + 2 + i, i, False)


_ORDER = ["x", "tokW", "tokb", "Wq", "Wk", "Wv", "WoT", "Wg", "bg", "bias", "W1", "b1", "b1T", "W2", "b2",
          "qw", "Wr", "br", "E1W"]


def kernel(**inputs):
    import numpy as _np
    import concourse.bacc as _bacc
    from concourse import mybir as _mybir
    from concourse.bass_utils import run_bass_kernel_spmd as _run

    i = {k: _np.asarray(v) for k, v in inputs.items()}
    E, K = i["L0_tok_W"].shape
    CH = i["x"].shape[1]
    X, _, HID = i["L1_ffn_W1"].shape
    packed = _np.zeros((X, 128, HID + E), i["L1_ffn_W1"].dtype)
    packed[:, 0:E, 0:HID] = i["L1_ffn_W1"]
    packed[:, E, 0:HID] = i["L1_ffn_b1"]
    packed[:, B2ROW, 0:E] = i["L1_ffn_b2"]
    packed[:, :, HID:] = i["L1_ffn_W2"]
    laid = {
        "x": i["x"],
        "tokW": i["L0_tok_W"].reshape(E, CH * PATCH, PATCH).transpose(1, 2, 0),
        "tokb": i["L0_tok_b"], "Wq": i["L0_attn_Wq"], "Wk": i["L0_attn_Wk"], "Wv": i["L0_attn_Wv"],
        "WoT": i["L0_attn_Wo"].T, "Wg": i["L0_ffn_Wg"], "bg": i["L0_ffn_bg"], "bias": i["L0_ffn_bias"],
        "W1": i["L0_ffn_W1"], "b1": i["L0_ffn_b1"], "b1T": i["L0_ffn_b1"].T, "W2": i["L0_ffn_W2"], "b2": i["L0_ffn_b2"],
        "qw": i["L1_attn_q_weight"], "Wr": i["L1_ffn_Wr"], "br": i["L1_ffn_br"],
        "E1W": packed,
    }
    nc = _bacc.Bacc("TRN2", target_bir_lowering=False, num_devices=1)
    arrays, args = {}, []
    for name in _ORDER:
        a = _np.ascontiguousarray(laid[name])
        arrays[f"in_{name}"] = a
        args.append(nc.dram_tensor(f"in_{name}", a.shape, _mybir.dt.from_np(a.dtype), kind="ExternalInput").ap())
    n_img = i["x"].shape[0]
    tokens = (i["x"].shape[2] // PATCH) * (i["x"].shape[3] // PATCH)
    out = nc.dram_tensor("out_0", (n_img, tokens, E), F32, kind="ExternalOutput").ap()
    vit_tower(nc, *args, out)
    r = _run(nc, [arrays], core_ids=[0])
    return r.results[0]["out_0"]
```
